# Optimizing a Trainium2 kernel written in Bass

```python
import numpy as np
import jax
import jax.numpy as jnp

def _softmax(x, axis=-1):
    return jax.nn.softmax(x, axis=axis)
def _gelu(x):
    return jax.nn.gelu(x, approximate=True)
def _silu(x):
    return jax.nn.silu(x)
def _sigmoid(x):
    return jax.nn.sigmoid(x)
def _layernorm(x, axis=-1, eps=1e-5):
    m = jnp.mean(x, axis=axis, keepdims=True)
    v = jnp.var(x, axis=axis, keepdims=True)
    return (x - m) / jnp.sqrt(v + eps)
def _scatter_add(tgt, idx, src, axis=0):
    return tgt.at[idx].add(src)
def _segment_sum(src, seg, n):
    return jax.ops.segment_sum(src, seg, n)

kernel_name = 'mk_vit_tower_cls_d1_tok_img256_84b0ac'

def setup_inputs(seed: int = 0):
    np.random.seed(seed)
    _w = jnp.asarray
    def _rec_inputs():
        import jax
        import jax.numpy as jnp
        _rk = jax.random.key(seed)
        x = (-0.000392918 + 0.999932 * jax.random.normal(jax.random.fold_in(_rk, 1), (16, 512, 512, 1), jnp.float32))
        cls_tok = 0.02 * jax.random.normal(jax.random.fold_in(_rk, 5), (1, 1, 256), jnp.float32)
        return x, cls_tok
    x, cls_tok = _rec_inputs()
    def _L0_tok_setup():
        import jax, jax.numpy as jnp
        import numpy as np
        IMG = 512
        P1 = 8
        P0 = 16
        NP1 = (IMG // P1) ** 2
        NP0 = (IMG // P0) ** 2
        D1 = P1 * P1
        D0 = P0 * P0

        def _extract_patches(x, p):
            B, H, W, C = x.shape
            gh, gw = (H // p, W // p)
            x = x.reshape(B, gh, p, gw, p, C).transpose(0, 1, 3, 2, 4, 5)
            return x.reshape(B, gh * gw, p * p * C)

        def _unpatch(flat, p, img):
            B = flat.shape[0]
            e = img // p
            x = flat.reshape(B, e, e, p, p, 1).transpose(0, 1, 3, 2, 4, 5)
            return x.reshape(B, img, img, 1)
        key = jax.random.key(seed)
        k1, k2, k3 = jax.random.split(key, 3)
        return {'x': jax.random.normal(k1, (64, IMG, IMG, 1), dtype=jnp.float32), 'pos_emb': jax.random.normal(k2, (NP1, D1), dtype=jnp.float32) * 0.02, 'dense_w': jax.random.normal(k3, (D0, D0), dtype=jnp.float32) * (1.0 / np.sqrt(D0)), 'dense_b': jnp.zeros((D0,), dtype=jnp.float32)}
    _L0_tok_all = _L0_tok_setup()
    _L0_tok_in = {k: v for k, v in _L0_tok_all.items() if k in ('pos_emb', 'dense_w', 'dense_b', )}
    del _L0_tok_all

    def _L0_attn_setup():
        import jax, jax.numpy as jnp
        import numpy as np
        GAMMA = 0.96875
        ROPE_THETA = 10000.0

        def _rope(x):
            B, S, d = x.shape
            inv_freq = 1.0 / ROPE_THETA ** (jnp.arange(0, d, 2, dtype=jnp.float32) / d)
            angles = jnp.arange(S, dtype=jnp.float32)[:, None] * inv_freq[None, :]
            cos = jnp.cos(angles).astype(x.dtype)
            sin = jnp.sin(angles).astype(x.dtype)
            xs = x.reshape(B, S, d // 2, 2)
            x0, x1 = (xs[..., 0], xs[..., 1])
            out = jnp.stack([x0 * cos - x1 * sin, x1 * cos + x0 * sin], axis=-1)
            return out.reshape(B, S, d)

        def _decay_mask(S, dtype):
            n = jnp.arange(S)[:, None]
            m = jnp.arange(S)[None, :]
            diff = n - m
            D = jnp.exp(jnp.maximum(diff, 0).astype(jnp.float32) * np.log(GAMMA))
            return jnp.where(diff >= 0, D, 0.0).astype(dtype)
        key = jax.random.key(seed)
        k1, k2, k3, k4 = jax.random.split(key, 4)
        H = 256
        X = jax.random.normal(k1, (4, 8192, H), dtype=jnp.float32)
        W_Q = jax.random.normal(k2, (H, H), dtype=jnp.float32) / H
        W_K = jax.random.normal(k3, (H, H), dtype=jnp.float32) / H
        W_V = jax.random.normal(k4, (H, H), dtype=jnp.float32) / H
        return {'X': X, 'W_Q': W_Q, 'W_K': W_K, 'W_V': W_V}
    _L0_attn_all = _L0_attn_setup()
    _L0_attn_in = {k: v for k, v in _L0_attn_all.items() if k in ('W_Q', 'W_K', 'W_V', )}
    del _L0_attn_all

    def _L0_ffn_setup():
        import jax, jax.numpy as jnp
        import numpy as np
        NUM_EXPERTS = 8
        TOP_K = 2
        B, S, D = (8, 8192, 256)

        def _moe(tokens, router_w, w1, b1, w2, b2):
            N = tokens.shape[0]
            E = router_w.shape[0]
            logits = tokens.astype(jnp.float32) @ router_w.astype(jnp.float32).T
            probs = jax.nn.softmax(logits, axis=-1)
            rw, re = jax.lax.top_k(probs, TOP_K)
            if TOP_K > 1:
                rw = rw / jnp.maximum(rw.sum(-1, keepdims=True), 1e-12)
            rw = rw.astype(tokens.dtype)
            combine = jnp.zeros((N, E), tokens.dtype).at[jnp.arange(N)[:, None], re].set(rw)
            out = tokens
            for e in range(E):
                h = jax.nn.gelu(tokens @ w1[e] + b1[e], approximate=False)
                y = h @ w2[e] + b2[e]
                out = out + combine[:, e:e + 1] * y
            return out
        key = jax.random.key(seed)
        ks = jax.random.split(key, 4)
        scale = 1.0 / np.sqrt(D).astype(np.float32)
        return {'input_embeddings': jax.random.normal(ks[0], (B, S, D), jnp.float32), 'router_w': jax.random.normal(ks[1], (NUM_EXPERTS, D), jnp.float32) * scale, 'w1': jax.random.normal(ks[2], (NUM_EXPERTS, D, D), jnp.float32) * scale, 'b1': jnp.zeros((NUM_EXPERTS, D), jnp.float32), 'w2': jax.random.normal(ks[3], (NUM_EXPERTS, D, D), jnp.float32) * scale, 'b2': jnp.zeros((NUM_EXPERTS, D), jnp.float32)}
    _L0_ffn_all = _L0_ffn_setup()
    _L0_ffn_in = {k: v for k, v in _L0_ffn_all.items() if k in ('router_w', 'w1', 'b1', 'w2', 'b2', )}
    del _L0_ffn_all

    return {
        "x": x,
        "cls_tok": cls_tok,
        "L0_tok_pos_emb": _L0_tok_in["pos_emb"],
        "L0_tok_dense_w": _L0_tok_in["dense_w"],
        "L0_tok_dense_b": _L0_tok_in["dense_b"],
        "L0_attn_W_Q": _L0_attn_in["W_Q"],
        "L0_attn_W_K": _L0_attn_in["W_K"],
        "L0_attn_W_V": _L0_attn_in["W_V"],
        "L0_ffn_router_w": _L0_ffn_in["router_w"],
        "L0_ffn_w1": _L0_ffn_in["w1"],
        "L0_ffn_b1": _L0_ffn_in["b1"],
        "L0_ffn_w2": _L0_ffn_in["w2"],
        "L0_ffn_b2": _L0_ffn_in["b2"],
    }

def reference(x, cls_tok, L0_tok_pos_emb, L0_tok_dense_w, L0_tok_dense_b, L0_attn_W_Q, L0_attn_W_K, L0_attn_W_V, L0_ffn_router_w, L0_ffn_w1, L0_ffn_b1, L0_ffn_w2, L0_ffn_b2):
    import jax
    import jax.numpy as jnp
    def _L0_tok_ref(x, pos_emb, dense_w, dense_b):
        import jax, jax.numpy as jnp
        import numpy as np
        IMG = 512
        P1 = 8
        P0 = 16
        NP1 = (IMG // P1) ** 2
        NP0 = (IMG // P0) ** 2
        D1 = P1 * P1
        D0 = P0 * P0

        def _extract_patches(x, p):
            B, H, W, C = x.shape
            gh, gw = (H // p, W // p)
            x = x.reshape(B, gh, p, gw, p, C).transpose(0, 1, 3, 2, 4, 5)
            return x.reshape(B, gh * gw, p * p * C)

        def _unpatch(flat, p, img):
            B = flat.shape[0]
            e = img // p
            x = flat.reshape(B, e, e, p, p, 1).transpose(0, 1, 3, 2, 4, 5)
            return x.reshape(B, img, img, 1)
        flat = _extract_patches(x, P1)
        encoded = flat + pos_emb
        restored_img = _unpatch(encoded, P1, IMG)
        restored = _extract_patches(restored_img, P0)
        return restored @ dense_w + dense_b

    def _L0_attn_ref(X, W_Q, W_K, W_V):
        import jax, jax.numpy as jnp
        import numpy as np
        GAMMA = 0.96875
        ROPE_THETA = 10000.0

        def _rope(x):
            B, S, d = x.shape
            inv_freq = 1.0 / ROPE_THETA ** (jnp.arange(0, d, 2, dtype=jnp.float32) / d)
            angles = jnp.arange(S, dtype=jnp.float32)[:, None] * inv_freq[None, :]
            cos = jnp.cos(angles).astype(x.dtype)
            sin = jnp.sin(angles).astype(x.dtype)
            xs = x.reshape(B, S, d // 2, 2)
            x0, x1 = (xs[..., 0], xs[..., 1])
            out = jnp.stack([x0 * cos - x1 * sin, x1 * cos + x0 * sin], axis=-1)
            return out.reshape(B, S, d)

        def _decay_mask(S, dtype):
            n = jnp.arange(S)[:, None]
            m = jnp.arange(S)[None, :]
            diff = n - m
            D = jnp.exp(jnp.maximum(diff, 0).astype(jnp.float32) * np.log(GAMMA))
            return jnp.where(diff >= 0, D, 0.0).astype(dtype)
        B, S, _ = X.shape
        D = _decay_mask(S, X.dtype)
        Q = _rope(X @ W_Q)
        K = _rope(X @ W_K)
        V = X @ W_V
        ret = jnp.einsum('bqd,bkd->bqk', Q, K) * D[None]
        return ret @ V

    def _L0_ffn_ref(input_embeddings, router_w, w1, b1, w2, b2):
        import jax, jax.numpy as jnp
        import numpy as np
        NUM_EXPERTS = 8
        TOP_K = 2
        B, S, D = (8, 8192, 256)

        def _moe(tokens, router_w, w1, b1, w2, b2):
            N = tokens.shape[0]
            E = router_w.shape[0]
            logits = tokens.astype(jnp.float32) @ router_w.astype(jnp.float32).T
            probs = jax.nn.softmax(logits, axis=-1)
            rw, re = jax.lax.top_k(probs, TOP_K)
            if TOP_K > 1:
                rw = rw / jnp.maximum(rw.sum(-1, keepdims=True), 1e-12)
            rw = rw.astype(tokens.dtype)
            combine = jnp.zeros((N, E), tokens.dtype).at[jnp.arange(N)[:, None], re].set(rw)
            out = tokens
            for e in range(E):
                h = jax.nn.gelu(tokens @ w1[e] + b1[e], approximate=False)
                y = h @ w2[e] + b2[e]
                out = out + combine[:, e:e + 1] * y
            return out
        b, s, d = input_embeddings.shape
        tokens = input_embeddings.reshape(b * s, d)
        return _moe(tokens, router_w, w1, b1, w2, b2).reshape(b, s, d)

    h = _L0_tok_ref(x, L0_tok_pos_emb, L0_tok_dense_w, L0_tok_dense_b)
    h = jnp.concatenate([jnp.broadcast_to(cls_tok, (h.shape[0], 1, h.shape[2])), h], axis=1)
    h = h + _L0_attn_ref(_layernorm(h, axis=-1), L0_attn_W_Q, L0_attn_W_K, L0_attn_W_V)
    h = h + _L0_ffn_ref(_layernorm(h, axis=-1), L0_ffn_router_w, L0_ffn_w1, L0_ffn_b1, L0_ffn_w2, L0_ffn_b2)
    return h


_drawn_inputs = setup_inputs


def setup_inputs(seed=0):
    import zlib

    import numpy as np

    out = dict(_drawn_inputs(seed))
    spreads = {'L0_tok_dense_b': (0.0, 0.1), 'L0_ffn_b1': (0.0, 0.326), 'L0_ffn_b2': (0.0, 0.1)}
    factors = {'cls_tok': 32.355}
    for name, (base, spread) in spreads.items():
        noise = np.random.default_rng([zlib.crc32(name.encode()), seed]).standard_normal(out[name].shape)
        drawn = base * np.exp(spread * noise) if base else spread * noise
        out[name] = jnp.asarray(drawn.astype(out[name].dtype))
    for name, factor in factors.items():
        out[name] = (out[name] * factor).astype(out[name].dtype)
    return out
```

```python
from contextlib import ExitStack

import numpy as np

import concourse.bass as bass
from concourse import mybir

F32 = mybir.dt.float32
F32R = mybir.dt.float32r
U32 = mybir.dt.uint32
ALU = mybir.AluOpType
ACT = mybir.ActivationFunctionType
AX = mybir.AxisListType

P = 128
IMG, PATCH = 512, 16
B = 16
D = 256
KC = D // P
S = (IMG // PATCH) ** 2
TILES = 4
W = TILES * P
NJ = S // W
NB = B * NJ
E = 8
GAMMA = 0.96875
DECAY = GAMMA ** P
EPS = 1e-5
CLS = NB


def vit_kernel(nc, x_fm, pos_fm, dense_w, dense_b, cls_rows, wq, wk, wv, router_fm, w1, b1_fm, w2, b2,
               rope, mask, ident, iota, lo_rows, out):
    n_dram = nc.dram_tensor("n_fm", [NB + 1, P, KC, W], F32, kind="Internal").ap()
    r_dram = nc.dram_tensor("residual", [NB + 1, P, TILES, D], F32, kind="Internal").ap()
    c_dram = nc.dram_tensor("combine_fm", [NB + 1, 3 * E, W], F32, kind="Internal").ap()

    top = ExitStack()
    with top:
        def sem(name):
            return top.enter_context(nc.semaphore(name))

        def wait(eng, s, value):
            if not isinstance(value, int) or value > 0:
                eng.wait_ge(s, value)

        pair = [top.enter_context(nc.psum_tensor(f"pair{n}", [P, 2, 512], F32)) for n in range(4)]
        combine = top.enter_context(nc.sbuf_tensor("combine", [P, NB + 1, TILES, E], F32))

        n_stored = [sem(f"n_stored{j}") for j in range(NJ)]
        r_stored = [sem(f"r_stored{j}") for j in range(NJ)]
        c_stored = [sem(f"c_stored{j}") for j in range(NJ)]
        cls_stored = sem("cls_stored")

        phase1(nc, top, sem, wait, pair, combine, n_stored, r_stored, c_stored, cls_stored, n_dram, r_dram,
               c_dram, x_fm, pos_fm, dense_w, dense_b, cls_rows, wq, wk, wv, router_fm, rope, mask, ident, iota)
        phase2(nc, top, sem, wait, pair, combine, n_dram, r_dram, c_dram, w1, b1_fm, w2, b2, lo_rows, out)


def phase1(nc, top, sem, wait, pair, combine, n_stored, r_stored, c_stored, cls_stored, n_dram, r_dram, c_dram,
           x_fm, pos_fm, dense_w, dense_b, cls_rows, wq, wk, wv, router_fm, rope, mask, ident, iota):
    ctx = ExitStack()
    with ctx:
        def sb(name, shape, dt=F32):
            return ctx.enter_context(nc.sbuf_tensor(name, shape, dt))

        ident_sb = sb("ident_sb", [P, P])
        mask_sb = sb("mask_sb", [P, P])
        iota_sb = sb("iota_sb", [P, E])
        rope_sb = sb("rope_sb", [P, 4, NJ, W])
        dense_sb = sb("dense_sb", [P, KC, D])
        bias_sb = sb("bias_sb", [P, D])
        router_sb = sb("router_sb", [P, KC, E])
        qkv_sb = sb("qkv_sb", [P, 3, KC, D])
        qkv_hi = sb("qkv_hi", [P, 3, KC, D], F32R)
        qkv_lo = sb("qkv_lo", [P, 3, KC, D], F32R)
        pos_sb = sb("pos_sb", [P, KC, S])
        posw = sb("posw", [P, S // P, D])
        half = sb("half", [P, TILES])
        x_sb = sb("x_sb", [P, NJ, KC, W])
        h0 = sb("h0", [P, NJ, TILES, D])
        h1 = sb("h1", [P, TILES, D])
        a_sb = sb("a_sb", [P, TILES, D])
        n_sb = sb("n_sb", [P, TILES, D])
        stats = [sb(f"stats{n}", [P, TILES, 6]) for n in range(2)]
        moments = [sb(f"moments{n}", [P, TILES, 2]) for n in range(2)]
        var_eps = [sb(f"var_eps{n}", [P, TILES]) for n in range(2)]
        rstd = [sb(f"rstd{n}", [P, TILES]) for n in range(2)]
        a_hi = sb("a_hi", [P, KC, W], F32R)
        a_lo = sb("a_lo", [P, KC, W], F32R)
        by_cos = sb("by_cos", [P, 2, W])
        by_sin = sb("by_sin", [P, 2, W])
        q_sb = sb("q_sb", [P, NJ, KC, W])
        k_sb = sb("k_sb", [P, KC, W])
        v_sb = sb("v_sb", [P, NJ, TILES, D])
        kt_sb = sb("kt_sb", [P, TILES, D])
        p_sb = sb("p_sb", [P, TILES, P])
        z_sb = sb("z_sb", [P, NJ * TILES, KC, D])
        nt_sb = sb("nt_sb", [P, NJ, KC, W])
        r_sb = sb("r_sb", [P, NJ, TILES, D])
        ct_sb = sb("ct_sb", [3 * E, NJ, W])
        lg = sb("lg", [P, TILES, E])
        top8 = sb("top8", [P, TILES, 8])
        idx8 = sb("idx8", [P, TILES, 8], U32)
        idxf = sb("idxf", [P, TILES, 2])
        below = sb("below", [P, TILES, E])
        expo = sb("expo", [P, TILES, E])
        zsum = sb("zsum", [P, TILES])
        zrec = sb("zrec", [P, TILES])
        hit0 = sb("hit0", [P, TILES, E])
        hit1 = sb("hit1", [P, TILES, E])
        prob = sb("prob", [P, TILES, E])
        picked = sb("picked", [P, TILES, E])
        psum2 = sb("psum2", [P, TILES])
        prec2 = sb("prec2", [P, TILES])
        chosen = sb("chosen", [P, TILES, E])
        c3 = sb("c3", [P, TILES, 3, E], F32R)
        q0 = sb("q0", [P, D])
        k0 = sb("k0", [P, D])
        v0 = sb("v0", [P, D])
        qk0 = sb("qk0", [P, D])
        s0 = sb("s0", [P, 1])

        loaded = sem("loaded")
        x_loaded = [sem(f"x_loaded{j}") for j in range(NJ)]
        half_set = sem("half_set")
        qkv_split = sem("qkv_split")
        posw_mm, posw_done = sem("posw_mm"), sem("posw_done")
        h0_mm, h0_done = sem("h0_mm"), sem("h0_done")
        stats_done = [sem(f"stats_done{n}") for n in range(2)]
        moments_done = [sem(f"moments_done{n}") for n in range(2)]
        var_done = [sem(f"var_done{n}") for n in range(2)]
        rstd_done = [sem(f"rstd_done{n}") for n in range(2)]
        normed = [sem(f"normed{n}") for n in range(2)]
        at_mm, a_hi_done, a_lo_done = sem("at_mm"), sem("a_hi_done"), sem("a_lo_done")
        q_mm, k_mm, v_mm = sem("q_mm"), sem("k_mm"), sem("v_mm")
        rope_mult, rope_done = sem("rope_mult"), sem("rope_done")
        v_done = sem("v_done")
        s_mm, p_done = sem("s_mm"), sem("p_done")
        kt_mm, kt_done = sem("kt_mm"), sem("kt_done")
        dz_mm, z_done = sem("dz_mm"), sem("z_done")
        o_mm, h1_done = sem("o_mm"), sem("h1_done")
        r_done = sem("r_done")
        nt_mm, nt_done = sem("nt_mm"), sem("nt_done")
        lg_mm, lg_done = sem("lg_mm"), sem("lg_done")
        top_done, idx_done = sem("top_done"), sem("idx_done")
        below_done, expo_done = sem("below_done"), sem("expo_done")
        route = sem("route")
        ct_mm, ct_done = sem("ct_mm"), sem("ct_done")
        cls_mm, cls_qkv, cls_state = sem("cls_mm"), sem("cls_qkv"), sem("cls_state")
        cls_score, shares_done, split_hi = sem("cls_score"), sem("shares_done"), sem("split_hi")

        apart = sem("apart")
        LOADS = 13 * 16
        ROUTE = 13
        CLS_STORES = 16 * 3 * TILES
        def parity(j, d):
            return (j + d) % NJ

        def image(i, j, d):
            return i + (j + d) // NJ

        def lives(i, j, d):
            return not isinstance(i, int) or 0 <= NJ * i + j + d < NB

        def own(i, j, d=0):
            return NJ * i + j + d + 1

        def both(i, j, d=0):
            return own(i, j, d) + 1

        def states_through(i, j, d=0):
            last = NJ * TILES - 1
            return last * image(i, j, d) + (last if parity(j, d) == NJ - 1 else TILES * (parity(j, d) + 1))

        def state_tiles(j):
            return range(TILES - 1 if j == NJ - 1 else TILES)

        def wait_apart(eng, s, count):
            eng.wait_ge(s, count)
            eng.sem_inc(apart, 1)

        def schedule(eng, turn):
            for j in range(NJ):
                turn(0, j)
            with eng.Fori(1, B - 1) as i:
                for j in range(NJ):
                    turn(i, j)
            for i in (B - 1, B):
                for j in range(NJ):
                    turn(i, j)

        block = ctx.enter_context(nc.Block())

        @block.sync
        def _(sp):
            for dst, src in ((ident_sb[:, :], ident), (mask_sb[:, :], mask), (iota_sb[:, :], iota),
                             (h0[:, 0, 0, :], cls_rows), (router_sb[:, :, :], router_fm),
                             (dense_sb[:, :, :], dense_w.rearrange("(k p) n -> p k n", p=P)),
                             (bias_sb[:, :], dense_b), (pos_sb[:, :, :], pos_fm),
                             (qkv_sb[:, 0, :, :], wq.rearrange("(k p) n -> p k n", p=P)),
                             (qkv_sb[:, 1, :, :], wk.rearrange("(k p) n -> p k n", p=P)),
                             (qkv_sb[:, 2, :, :], wv.rearrange("(k p) n -> p k n", p=P)),
                             (rope_sb[:, 0:2, :, :], rope[:, 0:2]), (rope_sb[:, 2:4, :, :], rope[:, 2:4])):
                sp.dma_start(dst, src).then_inc(loaded, 16)

            def load_x(i, j):
                wait(sp, h0_mm, 2 * own(i, j, -2))
                sp.dma_start(x_sb[:, j, :, :], x_fm[bass.ds(NJ * i + j, 1)].rearrange("a p k t -> (a p) k t"))\
                    .then_inc(x_loaded[j], 16)

            def store_n(i, j):
                wait(sp, nt_done, 2 * both(i, j))
                sp.dma_start(n_dram[bass.ds(NJ * i + j, 1)].rearrange("a p k t -> (a p) k t"), nt_sb[:, j, :, :])\
                    .then_inc(n_stored[j], 16)

            def store_r(i, j):
                wait(sp, r_done, both(i, j))
                sp.dma_start(r_dram[bass.ds(NJ * i + j, 1)].rearrange("a p c n -> (a p) c n"), r_sb[:, j, :, :])\
                    .then_inc(r_stored[j], 16)

            def store_c(i, j):
                wait(sp, ct_done, both(i, j))
                sp.dma_start(c_dram[bass.ds(NJ * i + j, 1)].rearrange("a p t -> (a p) t"), ct_sb[:, j, :])\
                    .then_inc(c_stored[j], 16)

            load_x(0, 0)
            load_x(0, 1)
            sp.wait_ge(nt_done, 2)
            sp.wait_ge(r_done, 1)
            sp.wait_ge(ct_done, 1)
            for c in range(TILES):
                tile = slice(c * P, (c + 1) * P)
                sp.dma_start(n_dram[CLS, :, :, tile], nt_sb[:, 1, :, 0:P]).then_inc(cls_stored, 16)
                sp.dma_start(r_dram[CLS, :, c, :], r_sb[:, 1, 0, :]).then_inc(cls_stored, 16)
                sp.dma_start(c_dram[CLS, :, tile], ct_sb[:, 1, 0:P]).then_inc(cls_stored, 16)

            def turn(i, j):
                if lives(i, j, 2):
                    load_x(image(i, j, 2), j)
                if lives(i, j, -1):
                    store_r(image(i, j, -1), parity(j, -1))
                    store_n(image(i, j, -1), parity(j, -1))
                if lives(i, j, -2):
                    store_c(image(i, j, -2), j)

            schedule(sp, turn)
            sp.wait_ge(cls_stored, CLS_STORES)
            for j in range(NJ):
                for stored in (n_stored, r_stored, c_stored):
                    sp.wait_ge(stored[j], 16 * B)

        @block.tensor
        def _(pe):
            def split_product(dst, x, w, x_stationary):
                passes = [(k, a, b) for k in range(KC) for a, b in ((0, 1), (1, 0), (0, 0))]
                for n, (k, a, b) in enumerate(passes):
                    lhs, rhs = (x[a](k), w[b](k)) if x_stationary else (w[b](k), x[a](k))
                    mm = pe.matmul(dst, lhs, rhs, start=(n == 0), stop=(n == len(passes) - 1))
                return mm

            def half_bank(buf, c, width=D):
                return buf[:, c // 2, (c % 2) * D:(c % 2) * D + width]

            def transpose_tiles(src, dst, ready, base, tiles, done):
                for k in range(KC):
                    for c in range(tiles):
                        if k == 0:
                            pe.wait_ge(ready, base + c + 1)
                        mm = pe.transpose(dst[:, k, c * P:(c + 1) * P], src[:, c, k * P:(k + 1) * P], ident_sb[:, :])
                    mm.then_inc(done, 1)

            def project(i, j):
                pe.wait_ge(x_loaded[j], 16 * (i + 1))
                wait(pe, rope_mult, 2 * own(i, j, -1) - 1)
                for c in range(TILES):
                    for k in range(KC):
                        mm = pe.matmul(half_bank(pair[0], c), x_sb[:, j, k, c * P:(c + 1) * P], dense_sb[:, k, :],
                                       start=(k == 0), stop=(k == KC - 1))
                    if c % 2:
                        mm.then_inc(h0_mm, 1)

            def transpose_a(i, j):
                wait(pe, h1_done, 2 * both(i, j, -2))
                transpose_tiles(a_sb, pair[3], normed[0], TILES * own(i, j, -1) + 1, TILES, at_mm)

            def qkv(i, j):
                pe.wait_ge(a_hi_done, 2 * both(i, j))
                pe.wait_ge(a_lo_done, 2 * both(i, j))
                wait(pe, nt_done, 2 * both(i, j, -2))
                pe.wait_ge(h0_done, 2 * own(i, j))
                x = (lambda k: a_hi[:, k, :]), (lambda k: a_lo[:, k, :])
                for m, (dst, done) in enumerate(((pair[0], q_mm), (pair[1], k_mm))):
                    if m == 1:
                        wait(pe, z_done, states_through(i, j, -2) + 2 if lives(i, j, -1) else 0)
                    for f in range(KC):
                        w = [lambda k, half=half: half[:, m, k, f * P:(f + 1) * P] for half in (qkv_hi, qkv_lo)]
                        split_product(dst[:, f, :], x, w, False).then_inc(done, 1)
                wait(pe, z_done, states_through(i, j, -1))
                for c in range(TILES):
                    x = [lambda k, half=half: half[:, k, c * P:(c + 1) * P] for half in (a_hi, a_lo)]
                    w = [lambda k, half=half: half[:, 2, k, :] for half in (qkv_hi, qkv_lo)]
                    mm = split_product(half_bank(pair[2], c), x, w, True)
                    if c % 2:
                        mm.then_inc(v_mm, 1)

            def scores(i, j):
                pe.wait_ge(rope_done, 2 * own(i, j))
                for c in range(TILES):
                    for k in range(KC):
                        mm = pe.matmul(pair[1][:, 0, c * P:(c + 1) * P], k_sb[:, k, c * P:(c + 1) * P],
                                       q_sb[:, j, k, c * P:(c + 1) * P], start=(k == 0), stop=(k == KC - 1))
                mm.then_inc(s_mm, 1)
                pe.wait_ge(v_done, 2 * own(i, j))
                for c in range(TILES):
                    for k in range(KC):
                        mm = pe.transpose(pair[2][:, c // 2, (c % 2) * D + k * P:(c % 2) * D + (k + 1) * P],
                                          k_sb[:, k, c * P:(c + 1) * P], ident_sb[:, :])
                    if c % 2:
                        mm.then_inc(kt_mm, 1)

            def state_steps(i, j):
                pe.wait_ge(p_done, own(i, j))
                for c in state_tiles(j):
                    if c % 2 == 0:
                        pe.wait_ge(kt_done, 2 * own(i, j, -1) + 1 + c // 2)
                    for k in range(KC):
                        mm = pe.matmul(pair[1 + c // 2][:, c % 2, k * D:(k + 1) * D],
                                       kt_sb[:, c, k * P:(k + 1) * P], v_sb[:, j, c, :], start=True, stop=True)
                    mm.then_inc(dz_mm, 1)

            def retention(i, j):
                pe.wait_ge(p_done, own(i, j))
                pe.wait_ge(lg_done, both(i, j, -1))
                wait(pe, ct_done, both(i, j, -2))
                for c in range(TILES):
                    if c > 0 or j > 0:
                        pe.wait_ge(z_done, states_through(i, j, -1) + c)
                    for k in range(KC):
                        pe.matmul(half_bank(pair[3], c), q_sb[:, j, k, c * P:(c + 1) * P],
                                  z_sb[:, j * TILES + c, k, :], start=(k == 0), stop=False)
                    mm = pe.matmul(half_bank(pair[3], c), p_sb[:, c, :], v_sb[:, j, c, :], start=False, stop=True)
                    if c % 2:
                        mm.then_inc(o_mm, 1)

            def transpose_n(i, j):
                if lives(i, j, 2):
                    pe.wait_ge(h0_done, 2 * own(i, j, 2))
                else:
                    pe.wait_ge(rope_mult, 2 * NB)
                    pe.wait_ge(nt_done, 2 * both(i, j, -1))
                transpose_tiles(n_sb, pair[0], normed[1], TILES * own(i, j, -1) + 1, TILES, nt_mm)

            def logits(src, tiles):
                for c in range(tiles):
                    for k in range(KC):
                        mm = pe.matmul(pair[3][:, 0, c * E:(c + 1) * E], src[:, k, c * P:(c + 1) * P],
                                       router_sb[:, k, :], start=(k == 0), stop=(k == KC - 1))
                mm.then_inc(lg_mm, 1)

            def transpose_shares(tiles):
                for c in range(tiles):
                    mm = pe.transpose(pair[3][0:3 * E, 1, c * P:(c + 1) * P],
                                      c3[:, c, :, :].rearrange("p a e -> p (a e)").bitcast(F32), ident_sb[:, :])
                mm.then_inc(ct_mm, 1)

            pe.wait_ge(loaded, LOADS)
            for c in range(S // P):
                for k in range(KC):
                    mm = pe.matmul(half_bank(pair[c // TILES], c % TILES), pos_sb[:, k, c * P:(c + 1) * P],
                                   dense_sb[:, k, :], start=(k == 0), stop=(k == KC - 1))
            mm.then_inc(posw_mm, 1)
            transpose_tiles(a_sb, pair[3], normed[0], 0, 1, at_mm)
            pe.wait_ge(qkv_split, 1)
            pe.wait_ge(a_hi_done, 2)
            pe.wait_ge(a_lo_done, 2)
            for m in range(3):
                x = [lambda k, half=half: half[:, k, 0:P] for half in (a_hi, a_lo)]
                w = [lambda k, half=half: half[:, m, k, :] for half in (qkv_hi, qkv_lo)]
                mm = split_product(half_bank(pair[2], m), x, w, True)
            mm.then_inc(cls_mm, 1)
            pe.wait_ge(cls_qkv, 3)
            for k in range(KC):
                mm = pe.matmul(pair[3][:, 0, k * D:(k + 1) * D], k0[0:1, k * P:(k + 1) * P], v0[0:1, :],
                               start=True, stop=True)
            mm.then_inc(cls_mm, 1)
            pe.wait_ge(posw_done, 1)
            transpose_tiles(n_sb, pair[0], normed[1], 0, 1, nt_mm)
            pe.wait_ge(nt_done, 2)
            pe.wait_ge(cls_state, 1)
            logits(nt_sb[:, 1, :, :], 1)
            project(0, 0)
            pe.wait_ge(route, ROUTE)
            transpose_shares(1)
            pe.wait_ge(lg_done, 1)
            pe.wait_ge(ct_done, 1)
            transpose_a(0, 0)

            def turn(i, j):
                if lives(i, j, 0):
                    qkv(i, j)
                if lives(i, j, -1):
                    retention(image(i, j, -1), parity(j, -1))
                if lives(i, j, 1):
                    project(image(i, j, 1), parity(j, 1))
                if lives(i, j, 0):
                    scores(i, j)
                if lives(i, j, 1):
                    transpose_a(image(i, j, 1), parity(j, 1))
                if lives(i, j, -1):
                    transpose_n(image(i, j, -1), parity(j, -1))
                if lives(i, j, 0):
                    state_steps(i, j)
                if lives(i, j, 1) and lives(i, j, -1):
                    pe.wait_ge(a_hi_done, 2 * both(i, j, 1))
                    pe.wait_ge(a_lo_done, 2 * both(i, j, 1))
                if lives(i, j, -1):
                    pe.wait_ge(nt_done, 2 * both(i, j, -1))
                    logits(nt_sb[:, parity(j, -1), :, :], TILES)
                if lives(i, j, -2):
                    pe.wait_ge(route, ROUTE * both(i, j, -2))
                    pe.wait_ge(ct_done, both(i, j, -3))
                    transpose_shares(TILES)

            schedule(pe, turn)

        @block.scalar
        def _(act):
            def copy_banks(dst, src, need, count, done):
                for m in range(2):
                    act.wait_ge(need, count + m + 1)
                    act.activation(dst(m), src[:, m, :], ACT.Copy).then_inc(done, 1)

            def split_a(i, j):
                wait(act, v_mm, 2 * own(i, j, -1))
                copy_banks(lambda m: a_hi[:, m, :], pair[3], at_mm, 2 * both(i, j, -1), a_hi_done)

            def copy_v(i, j):
                wait(act, o_mm, 2 * own(i, j, -2))
                copy_banks(lambda m: v_sb[:, j, 2 * m:2 * m + 2, :].rearrange("p c n -> p (c n)"), pair[2], v_mm,
                           2 * own(i, j, -1), v_done)

            def copy_kt(i, j):
                wait(act, dz_mm, states_through(i, j, -1))
                copy_banks(lambda m: kt_sb[:, 2 * m:2 * m + 2, :].rearrange("p c n -> p (c n)"), pair[2], kt_mm,
                           2 * own(i, j, -1), kt_done)

            def cls_is_stored(i, j):
                if j == 1 and isinstance(i, int):
                    act.wait_ge(cls_stored, CLS_STORES)

            def copy_n(i, j):
                wait(act, n_stored[j], 16 * i)
                cls_is_stored(i, j)
                wait(act, lg_mm, both(i, j, -2))
                copy_banks(lambda m: nt_sb[:, j, m, :], pair[0], nt_mm, 2 * both(i, j, -1), nt_done)

            def exps(tiles, turn_no):
                act.wait_ge(below_done, turn_no + 1)
                act.activation(expo[:, 0:tiles, :], below[:, 0:tiles, :], ACT.Exp).then_inc(expo_done, 1)

            def copy_shares(i, j):
                wait(act, c_stored[j], 16 * i)
                cls_is_stored(i, j)
                act.wait_ge(ct_mm, both(i, j))
                act.activation(ct_sb[:, j, :], pair[3][0:3 * E, 1, :], ACT.Copy).then_inc(ct_done, 1)

            for m in range(2):
                act.wait_ge(at_mm, m + 1)
                act.activation(a_hi[:, m, 0:P], pair[3][:, m, 0:P], ACT.Copy).then_inc(a_hi_done, 1)
            act.wait_ge(cls_mm, 1)
            act.activation(q0[:, :], pair[2][:, 0, 0:D], ACT.Copy).then_inc(cls_qkv, 1)
            act.activation(k0[:, :], pair[2][:, 0, D:2 * D], ACT.Copy).then_inc(cls_qkv, 1)
            act.activation(v0[:, :], pair[2][:, 1, 0:D], ACT.Copy).then_inc(cls_qkv, 1)
            act.wait_ge(cls_mm, 2)
            act.activation(z_sb[:, 0, :, :].rearrange("p k n -> p (k n)"), pair[3][:, 0, :], ACT.Copy)\
                .then_inc(cls_state, 1)
            for m in range(2):
                act.wait_ge(nt_mm, m + 1)
                act.activation(nt_sb[:, 1, m, 0:P], pair[0][:, m, 0:P], ACT.Copy).then_inc(nt_done, 1)
            exps(1, 0)
            act.wait_ge(ct_mm, 1)
            act.activation(ct_sb[:, 1, 0:P], pair[3][0:3 * E, 1, 0:P], ACT.Copy).then_inc(ct_done, 1)
            split_a(0, 0)

            def turn(i, j):
                if lives(i, j, 0):
                    copy_v(i, j)
                if lives(i, j, -2):
                    exps(TILES, both(i, j, -3))
                if lives(i, j, 0):
                    copy_kt(i, j)
                if lives(i, j, 1):
                    split_a(image(i, j, 1), parity(j, 1))
                if lives(i, j, -1):
                    copy_n(image(i, j, -1), parity(j, -1))
                if lives(i, j, -2):
                    copy_shares(image(i, j, -2), j)

            schedule(act, turn)

        @block.vector
        def _(dve):
            def norm(which, src, dst, tiles, turn_no, free):
                for c in range(tiles):
                    ins = dve.bn_stats(stats[which][:, c, :], src[:, c, :])
                ins.then_inc(stats_done[which], 1)
                wait_apart(dve, stats_done[which], turn_no + 1)
                for c in range(tiles):
                    ins = dve.bn_aggr(moments[which][:, c, :], stats[which][:, c, :])
                ins.then_inc(moments_done[which], 1)
                free()
                dve.wait_ge(moments_done[which], turn_no + 1)
                dve.wait_ge(rstd_done[which], turn_no + 1)
                for c in range(tiles):
                    dve.tensor_scalar(dst[:, c, :], src[:, c, :], moments[which][:, c, 0:1], rstd[which][:, c:c + 1],
                                      ALU.subtract, ALU.mult).then_inc(normed[which], 1)

            def two_tiles(buf, m):
                return buf[:, 2 * m:2 * m + 2, :].rearrange("p c n -> p (c n)")

            def add_position(i, j):
                wait(dve, h1_done, 2 * both(i, j, -2))
                for m in range(2):
                    dve.wait_ge(h0_mm, 2 * own(i, j, -1) + m + 1)
                    dve.tensor_tensor(two_tiles(h0[:, j, :, :], m), pair[0][:, m, :],
                                      two_tiles(posw, 2 * j + m), ALU.add).then_inc(h0_done, 1)
                dve.wait_ge(h0_done, 2 * own(i, j))
                norm(0, h0[:, j, :, :], a_sb, TILES, both(i, j, -1), lambda: dve.wait_ge(at_mm, 2 * both(i, j, -1)))

            def low_a(i, j):
                wait(dve, v_mm, 2 * own(i, j, -1))
                for m in range(2):
                    dve.wait_ge(a_hi_done, 2 * both(i, j, -1) + m + 1)
                    dve.tensor_tensor(a_lo[:, m, :], pair[3][:, m, :], a_hi[:, m, :].bitcast(F32), ALU.subtract)\
                        .then_inc(a_lo_done, 1)

            def rotate(i, j, m):
                src, mm = ((pair[0], q_mm), (pair[1], k_mm))[m]
                wait(dve, rope_done, 2 * own(i, j, -1) + m)
                dve.wait_ge(mm, 2 * own(i, j))
                for dst, table in ((by_cos, 2 * m), (by_sin, 2 * m + 1)):
                    ins = dve.tensor_tensor(dst[:, :, :], src[:, :, :],
                                            rope_sb[:, table, j:j + 1, :].to_broadcast([P, 2, W]), ALU.mult)
                ins.then_inc(rope_mult, 1)

            def masked(i, j):
                dve.wait_ge(s_mm, own(i, j))
                wait(dve, o_mm, 2 * own(i, j, -1))
                dve.tensor_tensor(p_sb[:, :, :], pair[1][:, 0, :].rearrange("p (c n) -> p c n", c=TILES),
                                  mask_sb[:, :].unsqueeze(1).to_broadcast([P, TILES, P]), ALU.mult)\
                    .then_inc(p_done, 1)

            def states(i, j):
                for c in state_tiles(j):
                    dve.wait_ge(dz_mm, states_through(i, j, -1) + c + 1)
                    n = j * TILES + c
                    if n > 0:
                        dve.wait_ge(z_done, states_through(i, j, -1) + c)
                    dve.scalar_tensor_tensor(z_sb[:, n + 1, :, :].rearrange("p k n -> p (k n)"),
                                             z_sb[:, n, :, :].rearrange("p k n -> p (k n)"), DECAY,
                                             pair[1 + c // 2][:, c % 2, :], ALU.mult, ALU.add).then_inc(z_done, 1)

            def after_retention(i, j):
                dve.wait_ge(r_done, both(i, j, -1))
                for m in range(2):
                    dve.wait_ge(o_mm, 2 * own(i, j, -1) + m + 1)
                    dve.tensor_tensor(two_tiles(h1, m), pair[3][:, m, :], two_tiles(h0[:, j, :, :], m), ALU.add)\
                        .then_inc(h1_done, 1)
                dve.wait_ge(h1_done, 2 * both(i, j))
                norm(1, h1, n_sb, TILES, both(i, j, -1), lambda: dve.wait_ge(nt_mm, 2 * both(i, j, -1)))

            def take_logits(tiles, turn_no):
                dve.wait_ge(lg_mm, turn_no + 1)
                dve.tensor_copy(lg[:, 0:tiles, :], pair[3][:, 0, 0:tiles * E].rearrange("p (c e) -> p c e", e=E))\
                    .then_inc(lg_done, 1)

            def router(tiles, turn_no, kept):
                T = slice(0, tiles)
                shape = [P, tiles, E]
                taken = [ROUTE * turn_no]

                def step(ins):
                    ins.then_inc(route, 1)
                    taken[0] = taken[0] + 1

                def steps_landed():
                    dve.wait_ge(route, taken[0])

                wait_apart(dve, lg_done, turn_no + 1)
                for c in range(tiles):
                    ins = dve.max(top8[:, c, :], lg[:, c, :])
                ins.then_inc(top_done, 1)
                dve.wait_ge(top_done, turn_no + 1)
                dve.tensor_tensor(below[:, T, :], lg[:, T, :], top8[:, T, 0:1].to_broadcast(shape), ALU.subtract)\
                    .then_inc(below_done, 1)
                for c in range(tiles):
                    ins = dve.max_index(idx8[:, c, :], top8[:, c, :], lg[:, c, :])
                ins.then_inc(idx_done, 1)
                dve.wait_ge(idx_done, turn_no + 1)
                step(dve.tensor_copy(idxf[:, T, :], idx8[:, T, 0:2]))
                steps_landed()
                experts = iota_sb[:, :].unsqueeze(1).to_broadcast(shape)
                step(dve.tensor_tensor(hit0[:, T, :], experts, idxf[:, T, 0:1].to_broadcast(shape), ALU.is_equal))
                step(dve.tensor_tensor(hit1[:, T, :], experts, idxf[:, T, 1:2].to_broadcast(shape), ALU.is_equal))
                dve.wait_ge(expo_done, turn_no + 1)
                step(dve.tensor_reduce(zsum[:, T], expo[:, T, :], AX.X, ALU.add))
                steps_landed()
                step(dve.reciprocal(zrec[:, T], zsum[:, T]))
                step(dve.tensor_tensor(hit0[:, T, :], hit0[:, T, :], hit1[:, T, :], ALU.add))
                steps_landed()
                step(dve.tensor_tensor(prob[:, T, :], expo[:, T, :], zrec[:, T].unsqueeze(2).to_broadcast(shape),
                                       ALU.mult))
                steps_landed()
                step(dve.tensor_tensor(picked[:, T, :], prob[:, T, :], hit0[:, T, :], ALU.mult))
                steps_landed()
                step(dve.tensor_reduce(psum2[:, T], picked[:, T, :], AX.X, ALU.add))
                steps_landed()
                step(dve.tensor_scalar(psum2[:, T], psum2[:, T], 1e-12, None, ALU.max))
                steps_landed()
                step(dve.reciprocal(prec2[:, T], psum2[:, T]))
                steps_landed()
                step(dve.tensor_tensor(chosen[:, T, :], picked[:, T, :],
                                       prec2[:, T].unsqueeze(2).to_broadcast(shape), ALU.mult))
                wait(dve, ct_mm, turn_no)
                steps_landed()
                dve.tensor_copy(c3[:, T, 0, :], chosen[:, T, :])
                dve.tensor_copy(c3[:, T, 1, :], chosen[:, T, :]).then_inc(shares_done, 1)
                dve.tensor_copy(kept, chosen[:, T, :])
                dve.wait_ge(shares_done, turn_no + 1)
                step(dve.tensor_tensor(c3[:, T, 2, :], chosen[:, T, :], c3[:, T, 0, :].bitcast(F32), ALU.subtract))

            dve.memset(half[:, :], -0.5).then_inc(half_set, 1)
            dve.wait_ge(loaded, LOADS)
            norm(0, h0[:, 0, :, :], a_sb, 1, 0, lambda: None)
            dve.wait_ge(posw_mm, 1)
            for c in range(S // P):
                ins = dve.tensor_tensor(posw[:, c, :], pair[c // 4][:, (c // 2) % 2, (c % 2) * D:(c % 2) * D + D],
                                        bias_sb[:, :], ALU.add)
            ins.then_inc(posw_done, 1)
            for m in range(2):
                dve.wait_ge(a_hi_done, m + 1)
                dve.tensor_tensor(a_lo[:, m, 0:P], pair[3][:, m, 0:P], a_hi[:, m, 0:P].bitcast(F32), ALU.subtract)\
                    .then_inc(a_lo_done, 1)
            dve.wait_ge(cls_qkv, 3)
            dve.tensor_tensor(qk0[:, :], q0[:, :], k0[:, :], ALU.mult).then_inc(cls_score, 1)
            dve.wait_ge(cls_score, 1)
            dve.tensor_reduce(s0[:, :], qk0[:, :], AX.X, ALU.add).then_inc(cls_score, 1)
            dve.wait_ge(cls_score, 2)
            dve.scalar_tensor_tensor(h1[:, 0, :], v0[:, :], s0[:, 0:1], h0[:, 0, 0, :], ALU.mult, ALU.add)\
                .then_inc(h1_done, 2)
            dve.wait_ge(h1_done, 2)
            norm(1, h1, n_sb, 1, 0, lambda: None)
            take_logits(1, 0)
            router(1, 0, combine[:, CLS, 0:1, :])
            dve.wait_ge(posw_done, 1)
            add_position(0, 0)
            low_a(0, 0)

            def turn(i, j):
                if lives(i, j, -2):
                    take_logits(TILES, both(i, j, -3))
                if lives(i, j, 0):
                    rotate(i, j, 0)
                    rotate(i, j, 1)
                if lives(i, j, -2):
                    router(TILES, both(i, j, -3),
                           combine[:, bass.ds(NJ * i + j - 2, 1), :, :].rearrange("p a c e -> p (a c) e"))
                if lives(i, j, -1):
                    after_retention(image(i, j, -1), parity(j, -1))
                if lives(i, j, 1):
                    add_position(image(i, j, 1), parity(j, 1))
                if lives(i, j, 0):
                    masked(i, j)
                if lives(i, j, 1):
                    low_a(image(i, j, 1), parity(j, 1))
                if lives(i, j, 0):
                    states(i, j)

            schedule(dve, turn)

        @block.gpsimd
        def _(pool):
            def inverse_deviation(which, tiles, turn_no):
                wait_apart(pool, moments_done[which], turn_no + 1)
                pool.tensor_scalar(var_eps[which][:, 0:tiles], moments[which][:, 0:tiles, 1], EPS, None, ALU.add)\
                    .then_inc(var_done[which], 1)
                pool.wait_ge(var_done[which], turn_no + 1)
                pool.tensor_tensor(rstd[which][:, 0:tiles], var_eps[which][:, 0:tiles], half[:, 0:tiles], ALU.pow)\
                    .then_inc(rstd_done[which], 1)

            def rotate(i, j, m):
                if m == 0:
                    wait(pool, o_mm, 2 * own(i, j, -2))
                    dst = q_sb[:, j, :, :]
                else:
                    wait(pool, kt_mm, 2 * own(i, j, -1))
                    dst = k_sb[:, :, :]
                pool.wait_ge(rope_mult, 2 * own(i, j, -1) + m + 1)
                pool.tensor_tensor(dst[:, 0, :], by_cos[:, 0, :], by_sin[:, 1, :], ALU.subtract)
                pool.tensor_tensor(dst[:, 1, :], by_cos[:, 1, :], by_sin[:, 0, :], ALU.add).then_inc(rope_done, 1)

            def residual(i, j):
                wait(pool, r_stored[j], 16 * i)
                if j == 1 and isinstance(i, int):
                    pool.wait_ge(cls_stored, CLS_STORES)
                pool.wait_ge(normed[1], TILES * own(i, j) + 1)
                pool.tensor_tensor(r_sb[:, j, :, :], h1[:, :, :], n_sb[:, :, :], ALU.add).then_inc(r_done, 1)

            pool.wait_ge(half_set, 1)
            inverse_deviation(0, 1, 0)
            pool.wait_ge(loaded, LOADS)
            whole = "p m k n -> p (m k n)"
            pool.tensor_scalar(qkv_hi[:, :, :, :].rearrange(whole), qkv_sb[:, :, :, :].rearrange(whole), 1.0, 0.0,
                               ALU.mult, ALU.add).then_inc(split_hi, 1)
            pool.wait_ge(split_hi, 1)
            pool.tensor_tensor(qkv_lo[:, :, :, :].rearrange(whole), qkv_sb[:, :, :, :].rearrange(whole),
                               qkv_hi[:, :, :, :].rearrange(whole).bitcast(F32), ALU.subtract).then_inc(qkv_split, 1)
            inverse_deviation(1, 1, 0)
            pool.wait_ge(normed[1], 1)
            pool.tensor_tensor(r_sb[:, 1, 0, :], h1[:, 0, :], n_sb[:, 0, :], ALU.add).then_inc(r_done, 1)
            inverse_deviation(0, TILES, 1)

            def turn(i, j):
                if lives(i, j, 0):
                    rotate(i, j, 0)
                    rotate(i, j, 1)
                if lives(i, j, -1):
                    inverse_deviation(1, TILES, both(i, j, -2))
                if lives(i, j, 1):
                    inverse_deviation(0, TILES, both(i, j, 0))
                if lives(i, j, -1):
                    residual(image(i, j, -1), parity(j, -1))

            schedule(pool, turn)


def phase2(nc, top, sem, wait, pair, combine, n_dram, r_dram, c_dram, w1, b1_fm, w2, b2_rows, lo_rows, out):
    ctx = ExitStack()
    with ctx:
        def sb(name, shape, dt=F32):
            return ctx.enter_context(nc.sbuf_tensor(name, shape, dt))

        raw = sb("raw", [P, E, 2, KC, D])
        w_hi = sb("w_hi", [P, E, 2, KC, D], F32R)
        w_lo = sb("w_lo", [P, E, 2, KC, D], F32R)
        b1_sb = sb("b1_sb", [P, E, KC])
        b2_sb = sb("b2_sb", [3 * E, D])
        b2_hi = sb("b2_hi", [3 * E, D], F32R)
        b2_low = sb("b2_low", [3 * E, D])
        b2_top = sb("b2_top", [3 * E, D])
        b2_3 = sb("b2_3", [3 * E, D], F32R)
        rows_sb = sb("rows_sb", [3 * E, 2])
        n_in = sb("n_in", [P, NJ, KC, W])
        n_hi = sb("n_hi", [P, NJ, KC, W], F32R)
        n_lo = sb("n_lo", [P, NJ, KC, W], F32R)
        r_in = sb("r_in", [P, NJ, TILES, D])
        c_in = sb("c_in", [3 * E, NJ, W], F32R)
        g = sb("g", [P, 2, KC, W])
        g_hi = sb("g_hi", [P, 2, KC, W], F32R)
        g_lo = sb("g_lo", [P, 2, KC, W], F32R)
        share = sb("share", [P, TILES, E])
        acc = sb("acc", [P, TILES, D])
        total = sb("total", [P, TILES, D])

        weights_in, small_in = sem("weights_in"), sem("small_in")
        w_hi_done, w_split = sem("w_hi_done"), sem("w_split")
        b2_steps = sem("b2_steps")
        block_in = [sem(f"block_in{j}") for j in range(NJ)]
        n_hi_done, n_lo_done = sem("n_hi_done"), sem("n_lo_done")
        h_mm, gelu_done, g_hi_done, g_lo_done = sem("h_mm"), sem("gelu_done"), sem("g_hi_done"), sem("g_lo_done")
        y_mm, share_done, y_added = sem("y_mm"), sem("share_done"), sem("y_added")
        out_stored = sem("out_stored")
        LOADS = 3 * 16
        USES = E + 1

        def schedule(eng, turn):
            for j in range(NJ):
                turn(0, j)
            with eng.Fori(1, B) as i:
                for j in range(NJ):
                    turn(i, j)
            turn(B, 0)

        def blocks(i, j):
            return NJ * i + j

        def is_cls(i):
            return isinstance(i, int) and i == B

        block = ctx.enter_context(nc.Block())

        @block.sync
        def _(sp):
            def load(i, j):
                at = bass.ds(NJ * i + j, 1)
                sp.dma_start(n_in[:, j, :, :], n_dram[at].rearrange("a p k t -> (a p) k t")).then_inc(block_in[j], 16)
                sp.dma_start(c_in[:, j, :].bitcast(F32), c_dram[at].rearrange("a p t -> (a p) t"))\
                    .then_inc(block_in[j], 16)
                sp.dma_start(r_in[:, j, :, :], r_dram[at].rearrange("a p c n -> (a p) c n")).then_inc(block_in[j], 16)

            load(0, 0)
            for m in range(3):
                sp.dma_start(b2_sb[m * E:(m + 1) * E, :], b2_rows).then_inc(small_in, 16)
            sp.dma_start(rows_sb[:, :], lo_rows).then_inc(small_in, 16)
            sp.dma_start(b1_sb[:, :, :], b1_fm).then_inc(small_in, 16)
            for e in range(E):
                for m, w in enumerate((w1, w2)):
                    sp.dma_start(raw[:, e, m, :, :], w[e].rearrange("(k p) n -> p k n", p=P)).then_inc(weights_in, 16)

            def turn(i, j):
                if is_cls(i):
                    return
                wait(sp, y_added, USES * blocks(i, j))
                load(i + (j + 1) // NJ, (j + 1) % NJ)
                sp.wait_ge(y_added, USES * (blocks(i, j) + 1))
                sp.dma_start(out[bass.ds(i, 1), 1 + j * W:1 + (j + 1) * W, :]
                             .rearrange("a (c p) n -> p (a c) n", p=P), total[:, :, :]).then_inc(out_stored, 16)

            schedule(sp, turn)
            sp.wait_ge(y_added, USES * (NB + 1))
            sp.dma_start(out[:, 0, :], total[0:B, 0, :]).then_inc(out_stored, 16)
            sp.wait_ge(out_stored, 16 * (NB + 1))

        @block.tensor
        def _(pe):
            def first(i, j, e, width=W):
                s = E * blocks(i, j) + e
                if e == 0:
                    pe.wait_ge(n_hi_done, blocks(i, j) + 1)
                    pe.wait_ge(n_lo_done, blocks(i, j) + 1)
                pe.wait_ge(w_split, 2 * e + 1)
                wait(pe, gelu_done, 2 * (s - 1))
                for f in range(KC):
                    n = 0
                    for k in range(KC):
                        for wt, x in ((w_lo, n_hi), (w_hi, n_lo), (w_hi, n_hi)):
                            mm = pe.matmul(pair[e % 2][:, f, 0:width], wt[:, e, 0, k, f * P:(f + 1) * P],
                                           x[:, j, k, 0:width], start=(n == 0), stop=(n == 3 * KC - 1))
                            n += 1
                    mm.then_inc(h_mm, 1)

            def half_bank(j, use, c):
                return pair[2 + (j + use) % 2][:, c // 2, (c % 2) * D:(c % 2) * D + D]

            def biases(i, j, tiles):
                pe.wait_ge(block_in[j], LOADS * (i + 1))
                pe.wait_ge(b2_steps, 4)
                wait(pe, y_added, USES * blocks(i, j) - 1)
                for c in range(tiles):
                    mm = pe.matmul(half_bank(j, 0, c), c_in[:, j, c * P:(c + 1) * P], b2_3[:, :],
                                   start=True, stop=True)
                mm.then_inc(y_mm, 1)

            def second(i, j, e, tiles):
                s = E * blocks(i, j) + e
                pe.wait_ge(g_lo_done, s + 1)
                pe.wait_ge(w_split, 2 * e + 2)
                wait(pe, y_added, USES * blocks(i, j) + e)
                for c in range(tiles):
                    n = 0
                    for k in range(KC):
                        for x, wt in ((g_hi, w_lo), (g_lo, w_hi), (g_hi, w_hi)):
                            mm = pe.matmul(half_bank(j, e + 1, c), x[:, e % 2, k, c * P:(c + 1) * P],
                                           wt[:, e, 1, k, :], start=(n == 0), stop=(n == 3 * KC - 1))
                            n += 1
                mm.then_inc(y_mm, 1)

            first(0, 0, 0)

            def turn(i, j):
                width, tiles = (P, 1) if is_cls(i) else (W, TILES)
                for e in range(E):
                    if e + 1 < E:
                        first(i, j, e + 1, width)
                    elif not is_cls(i):
                        first(i + (j + 1) // NJ, (j + 1) % NJ, 0)
                    if e == 0:
                        biases(i, j, tiles)
                    second(i, j, e, tiles)

            schedule(pe, turn)

        @block.scalar
        def _(act):
            def high_n(i, j):
                act.wait_ge(block_in[j], LOADS * (i + 1))
                act.activation(n_hi[:, j, :, :], n_in[:, j, :, :], ACT.Copy).then_inc(n_hi_done, 1)

            def gelu(i, j, e, width=W):
                s = E * blocks(i, j) + e
                wait(act, g_lo_done, s - 1)
                for f in range(KC):
                    act.wait_ge(h_mm, 2 * s + f + 1)
                    act.activation(g[:, e % 2, f, 0:width], pair[e % 2][:, f, 0:width], ACT.Gelu,
                                   bias=b1_sb[:, e, f:f + 1]).then_inc(gelu_done, 1)
                if e >= 2:
                    act.wait_ge(y_mm, USES * blocks(i, j) + e)
                else:
                    wait(act, y_mm, USES * blocks(i, j) - 1 + e)
                act.wait_ge(gelu_done, 2 * s + 2)
                act.activation(g_hi[:, e % 2, :, 0:width], g[:, e % 2, :, 0:width], ACT.Copy).then_inc(g_hi_done, 1)

            act.wait_ge(small_in, 16 * 5)
            high_n(0, 0)
            gelu(0, 0, 0)

            def turn(i, j):
                for e in range(1, E):
                    gelu(i, j, e, P if is_cls(i) else W)
                    if e == 4 and not is_cls(i):
                        high_n(i + (j + 1) // NJ, (j + 1) % NJ)
                if not is_cls(i):
                    gelu(i + (j + 1) // NJ, (j + 1) % NJ, 0)

            schedule(act, turn)

        @block.vector
        def _(dve):
            def low_n(i, j):
                dve.wait_ge(n_hi_done, blocks(i, j) + 1)
                dve.tensor_tensor(n_lo[:, j, :, :], n_in[:, j, :, :], n_hi[:, j, :, :].bitcast(F32), ALU.subtract)\
                    .then_inc(n_lo_done, 1)

            def low_g(i, j, e, width=W):
                s = E * blocks(i, j) + e
                dve.wait_ge(g_hi_done, s + 1)
                dve.tensor_tensor(g_lo[:, e % 2, :, 0:width], g[:, e % 2, :, 0:width],
                                  g_hi[:, e % 2, :, 0:width].bitcast(F32), ALU.subtract).then_inc(g_lo_done, 1)

            def whole_bank(buf, m):
                return buf[:, 2 * m:2 * m + 2, :].rearrange("p c n -> p (c n)")

            def start_sum(i, j, tiles):
                at = CLS if is_cls(i) else NJ * i + j
                dve.wait_ge(y_mm, USES * blocks(i, j) + 1)
                wait(dve, y_added, USES * blocks(i, j))
                if tiles == 1:
                    dve.tensor_tensor(acc[:, 0, :], pair[2 + j % 2][:, 0, 0:D], r_in[:, j, 0, :], ALU.add)\
                        .then_inc(y_added, 1)
                else:
                    ins = dve.tensor_tensor(acc[:, :, :].rearrange("p (m c) n -> p m (c n)", m=2),
                                            pair[2 + j % 2][:, :, :],
                                            r_in[:, j, :, :].rearrange("p (m c) n -> p m (c n)", m=2), ALU.add)
                    ins.then_inc(y_added, 1)
                dve.tensor_copy(share[:, 0:tiles, :],
                                combine[:, bass.ds(at, 1), 0:tiles, :].rearrange("p a c e -> p (a c) e"))\
                    .then_inc(share_done, 1)
                dve.wait_ge(share_done, blocks(i, j) + 1)

            def add_y(i, j, e, tiles):
                dve.wait_ge(y_mm, USES * blocks(i, j) + e + 2)
                dve.wait_ge(y_added, USES * blocks(i, j) + e + 1)
                dst = acc
                if e == E - 1:
                    wait(dve, out_stored, 16 * blocks(i, j))
                    dst = total
                for c in range(tiles):
                    ins = dve.scalar_tensor_tensor(
                        dst[:, c, :], pair[2 + (j + e + 1) % 2][:, c // 2, (c % 2) * D:(c % 2) * D + D],
                        share[:, c, e:e + 1], acc[:, c, :], ALU.mult, ALU.add)
                ins.then_inc(y_added, 1)

            dve.wait_ge(small_in, 16 * 5)
            dve.tensor_copy(b2_hi[:, :], b2_sb[:, :]).then_inc(b2_steps, 1)
            dve.wait_ge(b2_steps, 1)
            dve.tensor_tensor(b2_low[:, :], b2_sb[:, :], b2_hi[:, :].bitcast(F32), ALU.subtract).then_inc(b2_steps, 1)
            dve.tensor_scalar(b2_top[:, :], b2_hi[:, :].bitcast(F32), rows_sb[:, 0:1], None, ALU.mult)\
                .then_inc(b2_steps, 1)
            dve.wait_ge(b2_steps, 3)
            dve.scalar_tensor_tensor(b2_3[:, :], b2_low[:, :], rows_sb[:, 1:2], b2_top[:, :], ALU.mult, ALU.add)\
                .then_inc(b2_steps, 1)
            low_n(0, 0)
            low_g(0, 0, 0)

            def turn(i, j):
                width, tiles = (P, 1) if is_cls(i) else (W, TILES)
                for e in range(E):
                    if e + 1 < E:
                        low_g(i, j, e + 1, width)
                    elif not is_cls(i):
                        low_g(i + (j + 1) // NJ, (j + 1) % NJ, 0)
                    if e == 0:
                        start_sum(i, j, tiles)
                    add_y(i, j, e, tiles)
                    if e == 4 and not is_cls(i):
                        low_n(i + (j + 1) // NJ, (j + 1) % NJ)

            schedule(dve, turn)

        @block.gpsimd
        def _(pool):
            for e in range(E):
                for m in range(2):
                    n = 2 * e + m
                    pool.wait_ge(weights_in, 16 * 2 * E)
                    src = raw[:, e, m, :, :]
                    pool.tensor_scalar(w_hi[:, e, m, :, :], src, 1.0, 0.0, ALU.mult, ALU.add).then_inc(w_hi_done, 1)
                    pool.wait_ge(w_hi_done, n + 1)
                    pool.tensor_tensor(w_lo[:, e, m, :, :], src, w_hi[:, e, m, :, :].bitcast(F32), ALU.subtract)\
                        .then_inc(w_split, 1)


_INS = ("x_fm", "pos_fm", "dense_w", "dense_b", "cls_rows", "wq", "wk", "wv", "router_fm", "w1", "b1_fm", "w2",
        "b2", "rope", "mask", "ident", "iota", "lo_rows")


def _patches(img):
    n, g = img.shape[0], IMG // PATCH
    return img.reshape(n, g, PATCH, g, PATCH).transpose(0, 2, 4, 1, 3).reshape(n, D, S)


def _tables():
    inv_freq = (np.float32(1.0) / np.float32(10000.0) ** (np.arange(0, D, 2, dtype=np.float32) / np.float32(D)))
    angle = (inv_freq[:, None] * np.arange(1, S + 1, dtype=np.float32)[None, :]).astype(np.float64)
    at = np.arange(S) % P
    grow, fall = GAMMA ** (at + 1.0), GAMMA ** (P - 1.0 - at)
    rope = np.stack([np.cos(angle) * grow, np.sin(angle) * grow, np.cos(angle) * fall, np.sin(angle) * fall], axis=1)
    j, i = np.arange(P)[:, None], np.arange(P)[None, :]
    mask = np.where(j <= i, GAMMA ** -float(P), 0.0)
    lo = np.repeat([0.0, 1.0, 0.0], E)
    return {
        "rope": rope.reshape(P, 4, NJ, W).astype(np.float32),
        "mask": mask.astype(np.float32),
        "ident": np.eye(P, dtype=np.float32),
        "iota": np.broadcast_to(np.arange(E, dtype=np.float32), (P, E)),
        "lo_rows": np.stack([1.0 - lo, lo], axis=1).astype(np.float32),
    }


def kernel(**inputs):
    import numpy as _np
    import concourse.bacc as _bacc
    from concourse import mybir as _mybir
    from concourse.bass_utils import run_bass_kernel_spmd as _run

    a = {k: _np.asarray(v) for k, v in inputs.items()}
    halves = _np.concatenate([_np.arange(0, D, 2), _np.arange(1, D, 2)])
    x = _patches(a["x"].reshape(B, IMG, IMG)).reshape(B, KC, P, NJ, W).transpose(0, 3, 2, 1, 4).reshape(NB, P, KC, W)
    g = IMG // 8
    pos = a["L0_tok_pos_emb"].reshape(g, g, 8, 8).transpose(0, 2, 1, 3).reshape(1, IMG, IMG)
    given = {
        "x_fm": x,
        "pos_fm": _patches(pos)[0].reshape(KC, P, S).transpose(1, 0, 2),
        "dense_w": a["L0_tok_dense_w"],
        "dense_b": _np.broadcast_to(a["L0_tok_dense_b"], (P, D)),
        "cls_rows": _np.broadcast_to(a["cls_tok"].reshape(1, D), (P, D)),
        "wq": a["L0_attn_W_Q"][:, halves],
        "wk": a["L0_attn_W_K"][:, halves],
        "wv": a["L0_attn_W_V"],
        "router_fm": a["L0_ffn_router_w"].T.reshape(KC, P, E).transpose(1, 0, 2),
        "w1": a["L0_ffn_w1"],
        "b1_fm": a["L0_ffn_b1"].reshape(E, KC, P).transpose(2, 0, 1),
        "w2": a["L0_ffn_w2"],
        "b2": a["L0_ffn_b2"],
        **_tables(),
    }
    nc = _bacc.Bacc("TRN2", target_bir_lowering=False, num_devices=1)
    arrays, args = {}, {}
    for name in _INS:
        v = _np.ascontiguousarray(given[name])
        arrays[name] = v
        args[name] = nc.dram_tensor(name, v.shape, _mybir.dt.from_np(v.dtype), kind="ExternalInput").ap()
    out = nc.dram_tensor("out", (B, S + 1, D), _mybir.dt.float32, kind="ExternalOutput").ap()
    vit_kernel(nc, out=out, **args)
    r = _run(nc, [arrays], core_ids=[0])
    return r.results[0]["out"]
```

```python
from contextlib import ExitStack

import numpy as np

import concourse.bass as bass
from concourse import mybir

F32 = mybir.dt.float32
F32R = mybir.dt.float32r
U32 = mybir.dt.uint32
I32 = mybir.dt.int32
BF16 = mybir.dt.bfloat16
ALU = mybir.AluOpType
ACT = mybir.ActivationFunctionType
AX = mybir.AxisListType

P = 128
IMG, PATCH = 512, 16
B = 16
D = 256
KC = D // P
S = (IMG // PATCH) ** 2
TILES = 4
W = TILES * P
NJ = S // W
NB = B * NJ
E = 8
GAMMA = 0.96875
DECAY = GAMMA ** P
EPS = 1e-5
TOKENS = B * (S + 1)
REC = D + 16
AT_SHARE, AT_ROW = D, D + E
REGION = TOKENS + W
DUMMY = E
NX = (2 * TOKENS + E * (W - 1)) // W
STEPS = 4
NX = -(-NX // STEPS) * STEPS
MIN_X = -(-2 * TOKENS // W)
MOST = -(-TOKENS // W)


def vit_kernel(nc, x_fm, pos_fm, dense_w, dense_b, cls_rows, wq, wk, wv, router_fm, w1, b1_fm, w2, b2,
               rope, mask, ident, iota, before, rows, cls_row, pad_row, starts, steps, numbers, hi_lo, out):
    assert NX - MOST > 0
    records = nc.dram_tensor("records", [E * REGION + NX * W, REC], F32, kind="Internal").ap()

    top = ExitStack()
    with top:
        def sem(name):
            return top.enter_context(nc.semaphore(name))

        def wait(eng, s, value):
            if not isinstance(value, int) or value > 0:
                eng.wait_ge(s, value)

        def sb(name, shape, dt=F32):
            return top.enter_context(nc.sbuf_tensor(name, shape, dt))

        pair = [top.enter_context(nc.psum_tensor(f"pair{n}", [P, 2, 512], F32)) for n in range(4)]
        raw = sb("raw", [P, E, 2, KC, D])
        expert_of = sb("expert_of", [P, NX], I32)
        record_of = sb("record_of", [P, NX], I32)

        phase1(nc, sem, wait, pair, raw, expert_of, record_of, records, x_fm, pos_fm, dense_w, dense_b, cls_rows,
               wq, wk, wv, router_fm, w1, w2, rope, mask, ident, iota, before, rows, cls_row, pad_row, starts, steps,
               numbers, out)
        phase2(nc, sem, wait, pair, raw, expert_of, record_of, records, b1_fm, b2, ident, hi_lo, out)


def phase1(nc, sem, wait, pair, raw, expert_of, record_of, records, x_fm, pos_fm, dense_w, dense_b, cls_rows,
           wq, wk, wv, router_fm, w1, w2, rope, mask, ident, iota, before, rows, cls_row, pad_row, starts, steps,
           numbers, out):
    ctx = ExitStack()
    with ctx:
        def sb(name, shape, dt=F32):
            return ctx.enter_context(nc.sbuf_tensor(name, shape, dt))

        ident_sb = sb("ident_sb", [P, P])
        mask_sb = sb("mask_sb", [P, P])
        iota_sb = sb("iota_sb", [P, E])
        before_sb = sb("before_sb", [P, 2, P])
        before_bf = sb("before_bf", [P, 2, P], BF16)
        rows_sb = sb("rows_sb", [P, NJ, TILES])
        cls_row_sb = sb("cls_row_sb", [P, 1])
        pad_row_sb = sb("pad_row_sb", [P, TILES])
        steps_sb = sb("steps_sb", [P, MOST])
        numbers_sb = sb("numbers_sb", [P, NX])
        starts_sb = sb("starts_sb", [P, E])
        rope_sb = sb("rope_sb", [P, 4, NJ, W])
        dense_sb = sb("dense_sb", [P, KC, D])
        bias_sb = sb("bias_sb", [P, D])
        router_sb = sb("router_sb", [P, KC, E])
        qkv_hi = sb("qkv_hi", [P, 3, KC, D], F32R)
        qkv_lo = sb("qkv_lo", [P, 3, KC, D], F32R)
        posw = sb("posw", [P, S // P, D])
        half = sb("half", [P, TILES])
        x_sb = sb("x_sb", [P, NJ, KC, W])
        h0 = sb("h0", [P, NJ, TILES, D])
        h1 = sb("h1", [P, TILES, D])
        a_sb = sb("a_sb", [P, TILES, D])
        rec = sb("rec", [P, NJ, TILES, REC])
        pad = sb("pad", [P, TILES, REC])
        stats = [sb(f"stats{n}", [P, TILES, 6]) for n in range(2)]
        moments = [sb(f"moments{n}", [P, TILES, 2]) for n in range(2)]
        var_eps = [sb(f"var_eps{n}", [P, TILES]) for n in range(2)]
        rstd = [sb(f"rstd{n}", [P, TILES]) for n in range(2)]
        a_hi = sb("a_hi", [P, KC, W], F32R)
        a_lo = sb("a_lo", [P, KC, W], F32R)
        by_cos = sb("by_cos", [P, 2, 2, W])
        by_sin = sb("by_sin", [P, 2, 2, W])
        q_sb = sb("q_sb", [P, NJ, KC, W])
        k_sb = sb("k_sb", [P, KC, W])
        v_sb = sb("v_sb", [P, NJ, TILES, D])
        kt_sb = sb("kt_sb", [P, TILES, D])
        p_sb = sb("p_sb", [P, TILES, P])
        z_sb = sb("z_sb", [P, NJ * TILES, KC, D])
        before_states = z_sb[:, 1:, :, :].rearrange("p c k n -> p (c k n)")
        pos_sb = before_states[:, 0:KC * S].rearrange("p (k s) -> p k s", k=KC)
        qkv_sb = before_states[:, KC * S:KC * S + 3 * KC * D].rearrange("p (m k n) -> p m k n", m=3, k=KC)
        nt_sb = sb("nt_sb", [P, NJ, KC, W])
        r_sb = sb("r_sb", [P, NJ, TILES, D])
        lg = sb("lg", [P, TILES, E])
        top8 = sb("top8", [P, TILES, 8])
        idx8 = sb("idx8", [P, TILES, 8], U32)
        idxf = sb("idxf", [P, TILES, 2])
        below = sb("below", [P, TILES, E])
        expo = sb("expo", [P, TILES, E])
        zsum = sb("zsum", [P, TILES])
        zrec = sb("zrec", [P, TILES])
        hit0 = sb("hit0", [P, TILES, E])
        hit1 = sb("hit1", [P, TILES, E])
        prob = sb("prob", [P, TILES, E])
        picked = sb("picked", [P, TILES, E])
        psum2 = sb("psum2", [P, TILES])
        prec2 = sb("prec2", [P, TILES])
        chosen = sb("chosen", [P, TILES, E])
        hits = sb("hits", [P, TILES, E])
        taken = sb("taken", [P, TILES, E], BF16)
        free = sb("free", [P, E])
        place = sb("place", [P, TILES, E])
        mine = sb("mine", [P, 2, TILES, E])
        minef = sb("minef", [P, 2, TILES])
        place_of = sb("place_of", [P, NJ, 2, TILES], U32)
        count = sb("count", [P, E])
        fuller = sb("fuller", [P, E, MOST])
        blocks_of = sb("blocks_of", [P, E])
        blocks_to = sb("blocks_to", [P, E])
        ones = sb("ones", [P, E])
        past, past_blocks = (buf[:, 0, :, :].rearrange("p a n -> p (a n)")[:, 0:NX * E]
                             .rearrange("p (x e) -> p x e", e=E) for buf in (by_cos, by_sin))
        expert_f = sb("expert_f", [P, NX])
        skipped = sb("skipped", [P, NX])
        real_expert = sb("real_expert", [P, NX])
        record_f = sb("record_f", [P, NX])
        end_of = sb("end_of", [P, E], I32)
        q0, k0, v0, qk0 = (by_sin[:, 0, n // 2, n % 2 * D:(n % 2 + 1) * D] for n in range(4))
        s0 = sb("s0", [P, 1])

        loaded = sem("loaded")
        x_loaded = [sem(f"x_loaded{j}") for j in range(NJ)]
        half_set = sem("half_set")
        qkv_split = sem("qkv_split")
        posw_mm, posw_done = sem("posw_mm"), sem("posw_done")
        h0_mm, h0_done = sem("h0_mm"), sem("h0_done")
        stats_done = [sem(f"stats_done{n}") for n in range(2)]
        moments_done = [sem(f"moments_done{n}") for n in range(2)]
        var_done = [sem(f"var_done{n}") for n in range(2)]
        rstd_done = [sem(f"rstd_done{n}") for n in range(2)]
        normed = [sem(f"normed{n}") for n in range(2)]
        at_mm, a_hi_done, a_lo_done = sem("at_mm"), sem("a_hi_done"), sem("a_lo_done")
        q_mm, k_mm, v_mm = sem("q_mm"), sem("k_mm"), sem("v_mm")
        rope_mult, rope_done = sem("rope_mult"), sem("rope_done")
        v_done = sem("v_done")
        s_mm, p_done = sem("s_mm"), sem("p_done")
        kt_mm, kt_done = sem("kt_mm"), sem("kt_done")
        dz_mm, z_done = sem("dz_mm"), sem("z_done")
        o_mm, h1_done = sem("o_mm"), sem("h1_done")
        r_done = sem("r_done")
        nt_mm, nt_done = sem("nt_mm"), sem("nt_done")
        lg_mm, lg_done = sem("lg_mm"), sem("lg_done")
        top_done, idx_done = sem("top_done"), sem("idx_done")
        below_done, expo_done = sem("below_done"), sem("expo_done")
        route = sem("route")
        rank_mm, placed = sem("rank_mm"), sem("placed")
        place_steps = sem("place_steps")
        scattered = [sem(f"scattered{j}") for j in range(NJ)]
        cls_scattered, pads_stored = sem("cls_scattered"), sem("pads_stored")
        row_done, begun, pad_done = sem("row_done"), sem("begun"), sem("pad_done")
        table, tables_done = sem("table"), sem("tables_done")
        raw_loaded = sem("raw_loaded")
        cls_mm, cls_qkv, cls_state = sem("cls_mm"), sem("cls_qkv"), sem("cls_state")
        cls_score, split_hi = sem("cls_score"), sem("split_hi")
        r_stored = [sem(f"r_stored{j}") for j in range(NJ)]
        cls_stored = sem("cls_stored")

        apart = sem("apart")
        LOADS = 20 * 16
        ROUTE = 13
        PLACE = 5
        SCATTERS = 16 * 2 * TILES
        def parity(j, d):
            return (j + d) % NJ

        def image(i, j, d):
            return i + (j + d) // NJ

        def lives(i, j, d):
            return not isinstance(i, int) or 0 <= NJ * i + j + d < NB

        def own(i, j, d=0):
            return NJ * i + j + d + 1

        def both(i, j, d=0):
            return own(i, j, d) + 1

        def states_through(i, j, d=0):
            last = NJ * TILES - 1
            return last * image(i, j, d) + (last if parity(j, d) == NJ - 1 else TILES * (parity(j, d) + 1))

        def state_tiles(j):
            return range(TILES - 1 if j == NJ - 1 else TILES)

        def wait_apart(eng, s, count):
            eng.wait_ge(s, count)
            eng.sem_inc(apart, 1)

        def schedule(eng, turn):
            for i in range(2):
                for j in range(NJ):
                    turn(i, j)
            with eng.Fori(2, B - 1) as i:
                for j in range(NJ):
                    turn(i, j)
            for i in (B - 1, B):
                for j in range(NJ):
                    turn(i, j)

        block = ctx.enter_context(nc.Block())

        @block.sync
        def _(sp):
            for dst, src in ((ident_sb[:, :], ident), (mask_sb[:, :], mask), (iota_sb[:, :], iota),
                             (h0[:, 0, 0, :], cls_rows), (router_sb[:, :, :], router_fm),
                             (dense_sb[:, :, :], dense_w.rearrange("(k p) n -> p k n", p=P)),
                             (bias_sb[:, :], dense_b), (pos_sb[:, :, :], pos_fm),
                             (qkv_sb[:, 0, :, :], wq.rearrange("(k p) n -> p k n", p=P)),
                             (qkv_sb[:, 1, :, :], wk.rearrange("(k p) n -> p k n", p=P)),
                             (qkv_sb[:, 2, :, :], wv.rearrange("(k p) n -> p k n", p=P)),
                             (before_sb[:, :, :], before), (rows_sb[:, :, :], rows), (cls_row_sb[:, :], cls_row),
                             (pad_row_sb[:, :], pad_row), (steps_sb[:, :], steps), (numbers_sb[:, :], numbers),
                             (starts_sb[:, :], starts),
                             (rope_sb[:, 0:2, :, :], rope[:, 0:2]), (rope_sb[:, 2:4, :, :], rope[:, 2:4])):
                sp.dma_start(dst, src).then_inc(loaded, 16)

            def load_x(i, j):
                wait(sp, h0_mm, 2 * own(i, j, -2))
                sp.dma_start(x_sb[:, j, :, :], x_fm[bass.ds(NJ * i + j, 1)].rearrange("a p k t -> (a p) k t"))\
                    .then_inc(x_loaded[j], 16)

            def store_r(i, j):
                sp.wait_ge(r_done, both(i, j))
                sp.dma_start(out[bass.ds(i * (S + 1) + 1 + j * W, W)].rearrange("(c p) n -> p c n", p=P),
                             r_sb[:, j, :, :]).then_inc(r_stored[j], 16)

            load_x(0, 0)
            load_x(0, 1)
            sp.wait_ge(r_done, 1)
            sp.dma_start(out[0:TOKENS].rearrange("(b s) n -> b s n", b=B)[:, 0, :], r_sb[0:B, 1, 0, :])\
                .then_inc(cls_stored, 16)
            sp.wait_ge(pad_done, 2)
            for b in range(NX - MIN_X):
                sp.dma_start(records[E * REGION + b * W:E * REGION + (b + 1) * W].rearrange("(p c) n -> p c n", p=P),
                             pad[:, :, :]).then_inc(pads_stored, 16)
            sp.dma_start(out[TOKENS:TOKENS + W].rearrange("(p c) n -> p c n", p=P), pad[:, :, 0:D]).then_inc(pads_stored, 16)
            for e in range(E):
                for m, w in enumerate((w1, w2)):
                    sp.dma_start(raw[:, e, m, :, :], w[e].rearrange("(k p) n -> p k n", p=P)).then_inc(raw_loaded, 16)

            def turn(i, j):
                if lives(i, j, 2):
                    load_x(image(i, j, 2), j)
                if lives(i, j, -1):
                    store_r(image(i, j, -1), parity(j, -1))

            schedule(sp, turn)
            sp.wait_ge(tables_done, 1)
            for e in range(E):
                end = nc.values_load(end_of[0:1, e:e + 1], engines=[sp.engine], min_val=e * REGION,
                                     max_val=e * REGION + TOKENS)
                sp.dma_start(records[bass.ds(end, W)].rearrange("(p c) n -> p c n", p=P), pad[:, :, :])\
                    .then_inc(pads_stored, 16)
            sp.wait_ge(pads_stored, 16 * (NX - MIN_X + 1 + E))
            sp.wait_ge(cls_stored, 16)
            sp.wait_ge(raw_loaded, 16 * 2 * E)
            for j in range(NJ):
                sp.wait_ge(r_stored[j], 16 * B)

        @block.tensor
        def _(pe):
            def split_product(dst, x, w, x_stationary):
                passes = [(k, a, b) for k in range(KC) for a, b in ((0, 1), (1, 0), (0, 0))]
                for n, (k, a, b) in enumerate(passes):
                    lhs, rhs = (x[a](k), w[b](k)) if x_stationary else (w[b](k), x[a](k))
                    mm = pe.matmul(dst, lhs, rhs, start=(n == 0), stop=(n == len(passes) - 1))
                return mm

            def half_bank(buf, c, width=D):
                return buf[:, c // 2, (c % 2) * D:(c % 2) * D + width]

            def transpose_tiles(src, dst, ready, base, tiles, done):
                for k in range(KC):
                    for c in range(tiles):
                        if k == 0:
                            pe.wait_ge(ready, base + c + 1)
                        mm = pe.transpose(dst[:, k, c * P:(c + 1) * P], src[:, c, k * P:(k + 1) * P], ident_sb[:, :])
                    mm.then_inc(done, 1)

            def project(i, j):
                pe.wait_ge(x_loaded[j], 16 * (i + 1))
                wait(pe, rope_mult, 2 * own(i, j, -1))
                for c in range(TILES):
                    for k in range(KC):
                        mm = pe.matmul(half_bank(pair[0], c), x_sb[:, j, k, c * P:(c + 1) * P], dense_sb[:, k, :],
                                       start=(k == 0), stop=(k == KC - 1))
                    if c % 2:
                        mm.then_inc(h0_mm, 1)

            def transpose_a(i, j):
                wait(pe, h1_done, 2 * both(i, j, -2))
                transpose_tiles(a_sb, pair[3], normed[0], TILES * own(i, j, -1) + 1, TILES, at_mm)

            def qkv(i, j):
                pe.wait_ge(a_hi_done, 2 * both(i, j))
                pe.wait_ge(a_lo_done, 2 * both(i, j))
                x = (lambda k: a_hi[:, k, :]), (lambda k: a_lo[:, k, :])
                for m, dst, done in ((1, pair[1], k_mm), (0, pair[0], q_mm)):
                    if m == 1:
                        wait(pe, z_done, states_through(i, j, -2) + 2 if lives(i, j, -1) else 0)
                    else:
                        pe.wait_ge(lg_done, both(i, j, -2) if lives(i, j, -2) else 1)
                        pe.wait_ge(h0_done, 2 * own(i, j))
                    for f in range(KC):
                        w = [lambda k, half=half: half[:, m, k, f * P:(f + 1) * P] for half in (qkv_hi, qkv_lo)]
                        split_product(dst[:, f, :], x, w, False).then_inc(done, 1)
                wait(pe, z_done, states_through(i, j, -1))
                for c in range(TILES):
                    x = [lambda k, half=half: half[:, k, c * P:(c + 1) * P] for half in (a_hi, a_lo)]
                    w = [lambda k, half=half: half[:, 2, k, :] for half in (qkv_hi, qkv_lo)]
                    mm = split_product(half_bank(pair[2], c), x, w, True)
                    if c % 2:
                        mm.then_inc(v_mm, 1)

            def scores(i, j):
                pe.wait_ge(rope_done, 2 * own(i, j))
                for c in range(TILES):
                    for k in range(KC):
                        mm = pe.matmul(pair[1][:, 0, c * P:(c + 1) * P], k_sb[:, k, c * P:(c + 1) * P],
                                       q_sb[:, j, k, c * P:(c + 1) * P], start=(k == 0), stop=(k == KC - 1))
                mm.then_inc(s_mm, 1)
                pe.wait_ge(v_done, 2 * own(i, j))
                for c in range(TILES):
                    for k in range(KC):
                        mm = pe.transpose(pair[2][:, c // 2, (c % 2) * D + k * P:(c % 2) * D + (k + 1) * P],
                                          k_sb[:, k, c * P:(c + 1) * P], ident_sb[:, :])
                    if c % 2:
                        mm.then_inc(kt_mm, 1)

            def state_steps(i, j):
                pe.wait_ge(p_done, own(i, j))
                pe.wait_ge(placed, both(i, j, -2))
                for c in state_tiles(j):
                    if c % 2 == 0:
                        pe.wait_ge(kt_done, 2 * own(i, j, -1) + 1 + c // 2)
                    for k in range(KC):
                        mm = pe.matmul(pair[1 + c // 2][:, c % 2, k * D:(k + 1) * D],
                                       kt_sb[:, c, k * P:(k + 1) * P], v_sb[:, j, c, :], start=True, stop=True)
                    mm.then_inc(dz_mm, 1)

            def retention(i, j):
                pe.wait_ge(p_done, own(i, j))
                for c in range(TILES):
                    if c > 0 or j > 0:
                        pe.wait_ge(z_done, states_through(i, j, -1) + c)
                    for k in range(KC):
                        pe.matmul(half_bank(pair[3], c), q_sb[:, j, k, c * P:(c + 1) * P],
                                  z_sb[:, j * TILES + c, k, :], start=(k == 0), stop=False)
                    mm = pe.matmul(half_bank(pair[3], c), p_sb[:, c, :], v_sb[:, j, c, :], start=False, stop=True)
                    if c % 2:
                        mm.then_inc(o_mm, 1)

            def transpose_n(i, j):
                if lives(i, j, 2):
                    pe.wait_ge(h0_done, 2 * own(i, j, 2))
                else:
                    pe.wait_ge(rope_mult, 2 * NB)
                    pe.wait_ge(nt_done, 2 * both(i, j, -1))
                transpose_tiles(rec[:, j, :, :], pair[0], normed[1], TILES * own(i, j, -1) + 1, TILES, nt_mm)

            def logits(src, tiles):
                for c in range(tiles):
                    for k in range(KC):
                        mm = pe.matmul(pair[0][:, 0, c * E:(c + 1) * E], src[:, k, c * P:(c + 1) * P],
                                       router_sb[:, k, :], start=(k == 0), stop=(k == KC - 1))
                mm.then_inc(lg_mm, 1)

            def ranks(parts):
                dst = pair[1][:, 1, 0:(TILES + 1) * E]
                pe.matmul(dst[:, 0:TILES * E], before_bf[0:parts, 0, :],
                          taken[0:parts, :, :].rearrange("p c e -> p (c e)"), start=True, stop=False)
                for c in range(TILES - 1):
                    later = TILES - 1 - c
                    pe.matmul(dst[:, (c + 1) * E:TILES * E].rearrange("p (c e) -> p c e", e=E),
                              before_bf[0:parts, 1, :], taken[0:parts, c:c + 1, :].to_broadcast([parts, later, E]),
                              start=False, stop=(c == TILES - 2))
                for c in range(TILES):
                    mm = pe.matmul(dst[:, TILES * E:], before_bf[0:parts, 1, :], taken[0:parts, c, :],
                                   start=(c == 0), stop=(c == TILES - 1))
                mm.then_inc(rank_mm, 1)

            pe.wait_ge(loaded, LOADS)
            for c in range(S // P):
                for k in range(KC):
                    mm = pe.matmul(half_bank(pair[c // TILES], c % TILES), pos_sb[:, k, c * P:(c + 1) * P],
                                   dense_sb[:, k, :], start=(k == 0), stop=(k == KC - 1))
            mm.then_inc(posw_mm, 1)
            transpose_tiles(a_sb, pair[3], normed[0], 0, 1, at_mm)
            pe.wait_ge(qkv_split, 1)
            pe.wait_ge(a_hi_done, 2)
            pe.wait_ge(a_lo_done, 2)
            for m in range(3):
                x = [lambda k, half=half: half[:, k, 0:P] for half in (a_hi, a_lo)]
                w = [lambda k, half=half: half[:, m, k, :] for half in (qkv_hi, qkv_lo)]
                mm = split_product(half_bank(pair[2], m), x, w, True)
            mm.then_inc(cls_mm, 1)
            pe.wait_ge(cls_qkv, 3)
            for k in range(KC):
                mm = pe.matmul(pair[3][:, 0, k * D:(k + 1) * D], k0[0:1, k * P:(k + 1) * P], v0[0:1, :],
                               start=True, stop=True)
            mm.then_inc(cls_mm, 1)
            pe.wait_ge(posw_done, 1)
            transpose_tiles(rec[:, 1, :, :], pair[0], normed[1], 0, 1, nt_mm)
            pe.wait_ge(nt_done, 2)
            pe.wait_ge(cls_state, 1)
            logits(nt_sb[:, 1, :, :], 1)
            pe.wait_ge(lg_done, 1)
            project(0, 0)
            pe.wait_ge(route, ROUTE)
            ranks(B)
            transpose_a(0, 0)

            def turn(i, j):
                if lives(i, j, 0):
                    qkv(i, j)
                if lives(i, j, -1):
                    retention(image(i, j, -1), parity(j, -1))
                if lives(i, j, 1):
                    project(image(i, j, 1), parity(j, 1))
                if lives(i, j, -2):
                    pe.wait_ge(route, ROUTE * both(i, j, -2))
                    pe.wait_ge(placed, both(i, j, -3))
                    if lives(i, j, 0):
                        pe.wait_ge(rope_mult, 2 * own(i, j) - 1)
                    else:
                        pe.wait_ge(z_done, (NJ * TILES - 1) * B)
                    ranks(P)
                if lives(i, j, 0):
                    scores(i, j)
                if lives(i, j, 0):
                    state_steps(i, j)
                if lives(i, j, -1):
                    transpose_n(image(i, j, -1), parity(j, -1))
                if lives(i, j, 1):
                    transpose_a(image(i, j, 1), parity(j, 1))
                if lives(i, j, -1):
                    pe.wait_ge(nt_done, 2 * both(i, j, -1))
                    logits(nt_sb[:, parity(j, -1), :, :], TILES)

            schedule(pe, turn)

        @block.scalar
        def _(act):
            def copy_banks(dst, src, need, count, done):
                for m in range(2):
                    act.wait_ge(need, count + m + 1)
                    act.activation(dst(m), src[:, m, :], ACT.Copy).then_inc(done, 1)

            def split_a(i, j):
                wait(act, v_mm, 2 * own(i, j, -1))
                copy_banks(lambda m: a_hi[:, m, :], pair[3], at_mm, 2 * both(i, j, -1), a_hi_done)

            def copy_v(i, j):
                wait(act, o_mm, 2 * own(i, j, -2))
                copy_banks(lambda m: v_sb[:, j, 2 * m:2 * m + 2, :].rearrange("p c n -> p (c n)"), pair[2], v_mm,
                           2 * own(i, j, -1), v_done)

            def copy_kt(i, j):
                wait(act, dz_mm, states_through(i, j, -1))
                copy_banks(lambda m: kt_sb[:, 2 * m:2 * m + 2, :].rearrange("p c n -> p (c n)"), pair[2], kt_mm,
                           2 * own(i, j, -1), kt_done)

            def copy_n(i, j):
                wait(act, lg_mm, both(i, j, -2))
                copy_banks(lambda m: nt_sb[:, j, m, :], pair[0], nt_mm, 2 * both(i, j, -1), nt_done)

            def exps(tiles, turn_no):
                act.wait_ge(below_done, turn_no + 1)
                act.activation(expo[:, 0:tiles, :], below[:, 0:tiles, :], ACT.Exp).then_inc(expo_done, 1)

            for m in range(2):
                act.wait_ge(at_mm, m + 1)
                act.activation(a_hi[:, m, 0:P], pair[3][:, m, 0:P], ACT.Copy).then_inc(a_hi_done, 1)
            act.wait_ge(cls_mm, 1)
            act.activation(q0, pair[2][:, 0, 0:D], ACT.Copy).then_inc(cls_qkv, 1)
            act.activation(k0, pair[2][:, 0, D:2 * D], ACT.Copy).then_inc(cls_qkv, 1)
            act.activation(v0, pair[2][:, 1, 0:D], ACT.Copy).then_inc(cls_qkv, 1)
            act.wait_ge(cls_mm, 2)
            act.activation(z_sb[:, 0, :, :].rearrange("p k n -> p (k n)"), pair[3][:, 0, :], ACT.Copy)\
                .then_inc(cls_state, 1)
            for m in range(2):
                act.wait_ge(nt_mm, m + 1)
                act.activation(nt_sb[:, 1, m, 0:P], pair[0][:, m, 0:P], ACT.Copy).then_inc(nt_done, 1)
            exps(1, 0)
            split_a(0, 0)

            def turn(i, j):
                if lives(i, j, 0):
                    copy_v(i, j)
                if lives(i, j, -2):
                    exps(TILES, both(i, j, -3))
                if lives(i, j, 0):
                    copy_kt(i, j)
                if lives(i, j, -1):
                    copy_n(image(i, j, -1), parity(j, -1))
                if lives(i, j, 1):
                    split_a(image(i, j, 1), parity(j, 1))

            schedule(act, turn)

        @block.vector
        def _(dve):
            def take_moments(which, src, tiles, turn_no):
                for c in range(tiles):
                    ins = dve.bn_stats(stats[which][:, c, :], src[:, c, :])
                ins.then_inc(stats_done[which], 1)
                wait_apart(dve, stats_done[which], turn_no + 1)
                for c in range(tiles):
                    ins = dve.bn_aggr(moments[which][:, c, :], stats[which][:, c, :])
                ins.then_inc(moments_done[which], 1)

            def norm(which, src, dst, tiles, turn_no, free):
                free()
                dve.wait_ge(moments_done[which], turn_no + 1)
                dve.wait_ge(rstd_done[which], turn_no + 1)
                for c in range(tiles):
                    dve.tensor_scalar(dst[:, c, :], src[:, c, :], moments[which][:, c, 0:1], rstd[which][:, c:c + 1],
                                      ALU.subtract, ALU.mult).then_inc(normed[which], 1)

            def two_tiles(buf, m):
                return buf[:, 2 * m:2 * m + 2, :].rearrange("p c n -> p (c n)")

            def add_position(i, j):
                wait(dve, h1_done, 2 * both(i, j, -2))
                for m in range(2):
                    dve.wait_ge(h0_mm, 2 * own(i, j, -1) + m + 1)
                    dve.tensor_tensor(two_tiles(h0[:, j, :, :], m), pair[0][:, m, :],
                                      two_tiles(posw, 2 * j + m), ALU.add).then_inc(h0_done, 1)

            def first_moments(i, j):
                dve.wait_ge(h0_done, 2 * own(i, j))
                take_moments(0, h0[:, j, :, :], TILES, both(i, j, -1))

            def first_norm(i, j):
                norm(0, h0[:, j, :, :], a_sb, TILES, both(i, j, -1), lambda: dve.wait_ge(at_mm, 2 * both(i, j, -1)))

            def low_a(i, j):
                wait(dve, v_mm, 2 * own(i, j, -1))
                for m in range(2):
                    dve.wait_ge(a_hi_done, 2 * both(i, j, -1) + m + 1)
                    dve.tensor_tensor(a_lo[:, m, :], pair[3][:, m, :], a_hi[:, m, :].bitcast(F32), ALU.subtract)\
                        .then_inc(a_lo_done, 1)

            def rotate(i, j, m):
                src, mm, tables = ((pair[1], k_mm, 2), (pair[0], q_mm, 0))[m]
                wait(dve, rope_done, 2 * own(i, j, -1) - 1 + m)
                dve.wait_ge(mm, 2 * own(i, j))
                for dst, table in ((by_cos, tables), (by_sin, tables + 1)):
                    ins = dve.tensor_tensor(dst[:, m, :, :], src[:, :, :],
                                            rope_sb[:, table, j:j + 1, :].to_broadcast([P, 2, W]), ALU.mult)
                ins.then_inc(rope_mult, 1)

            def masked(i, j):
                dve.wait_ge(s_mm, own(i, j))
                wait(dve, o_mm, 2 * own(i, j, -1))
                dve.tensor_tensor(p_sb[:, :, :], pair[1][:, 0, :].rearrange("p (c n) -> p c n", c=TILES),
                                  mask_sb[:, :].unsqueeze(1).to_broadcast([P, TILES, P]), ALU.mult)\
                    .then_inc(p_done, 1)

            def states(i, j, tiles):
                for c in tiles:
                    dve.wait_ge(dz_mm, states_through(i, j, -1) + c + 1)
                    n = j * TILES + c
                    if n > 0:
                        dve.wait_ge(z_done, states_through(i, j, -1) + c)
                    dve.scalar_tensor_tensor(z_sb[:, n + 1, :, :].rearrange("p k n -> p (k n)"),
                                             z_sb[:, n, :, :].rearrange("p k n -> p (k n)"), DECAY,
                                             pair[1 + c // 2][:, c % 2, :], ALU.mult, ALU.add).then_inc(z_done, 1)

            def after_retention(i, j):
                dve.wait_ge(r_done, both(i, j, -1))
                for m in range(2):
                    dve.wait_ge(o_mm, 2 * own(i, j, -1) + m + 1)
                    dve.tensor_tensor(two_tiles(h1, m), pair[3][:, m, :], two_tiles(h0[:, j, :, :], m), ALU.add)\
                        .then_inc(h1_done, 1)
                dve.wait_ge(h1_done, 2 * both(i, j))
                take_moments(1, h1, TILES, both(i, j, -1))

            def second_norm(i, j):
                def free_records():
                    wait(dve, scattered[j], SCATTERS * i)
                    if isinstance(i, int) and i == j == 0:
                        dve.wait_ge(cls_scattered, 32)
                    wait(dve, nt_mm, 2 * both(i, j, -2))

                norm(1, h1, rec[:, j, :, 0:D], TILES, both(i, j, -1), free_records)

            def take_logits(tiles, turn_no):
                dve.wait_ge(lg_mm, turn_no + 1)
                dve.tensor_copy(lg[:, 0:tiles, :], pair[0][:, 0, 0:tiles * E].rearrange("p (c e) -> p c e", e=E))\
                    .then_inc(lg_done, 1)

            def router(tiles, turn_no, j):
                T = slice(0, tiles)
                shape = [P, tiles, E]
                landed = [ROUTE * turn_no]

                def step(ins):
                    ins.then_inc(route, 1)
                    landed[0] = landed[0] + 1

                def steps_landed():
                    dve.wait_ge(route, landed[0])

                wait_apart(dve, lg_done, turn_no + 1)
                for c in range(tiles):
                    ins = dve.max(top8[:, c, :], lg[:, c, :])
                ins.then_inc(top_done, 1)
                dve.wait_ge(top_done, turn_no + 1)
                dve.tensor_tensor(below[:, T, :], lg[:, T, :], top8[:, T, 0:1].to_broadcast(shape), ALU.subtract)\
                    .then_inc(below_done, 1)
                for c in range(tiles):
                    ins = dve.max_index(idx8[:, c, :], top8[:, c, :], lg[:, c, :])
                ins.then_inc(idx_done, 1)
                dve.wait_ge(idx_done, turn_no + 1)
                step(dve.tensor_copy(idxf[:, T, :], idx8[:, T, 0:2]))
                steps_landed()
                experts = iota_sb[:, :].unsqueeze(1).to_broadcast(shape)
                step(dve.tensor_tensor(hit0[:, T, :], experts, idxf[:, T, 0:1].to_broadcast(shape), ALU.is_equal))
                step(dve.tensor_tensor(hit1[:, T, :], experts, idxf[:, T, 1:2].to_broadcast(shape), ALU.is_equal))
                dve.wait_ge(expo_done, turn_no + 1)
                step(dve.tensor_reduce(zsum[:, T], expo[:, T, :], AX.X, ALU.add))
                steps_landed()
                step(dve.reciprocal(zrec[:, T], zsum[:, T]))
                step(dve.tensor_tensor(hits[:, T, :], hit0[:, T, :], hit1[:, T, :], ALU.add))
                steps_landed()
                wait(dve, rank_mm, turn_no)
                step(dve.tensor_copy(taken[:, T, :], hits[:, T, :]))
                step(dve.tensor_tensor(prob[:, T, :], expo[:, T, :], zrec[:, T].unsqueeze(2).to_broadcast(shape),
                                       ALU.mult))
                steps_landed()
                step(dve.tensor_tensor(picked[:, T, :], prob[:, T, :], hits[:, T, :], ALU.mult))
                steps_landed()
                step(dve.tensor_reduce(psum2[:, T], picked[:, T, :], AX.X, ALU.add))
                steps_landed()
                step(dve.tensor_scalar(psum2[:, T], psum2[:, T], 1e-12, None, ALU.max))
                steps_landed()
                step(dve.reciprocal(prec2[:, T], psum2[:, T]))
                steps_landed()
                step(dve.tensor_tensor(rec[:, j, T, AT_SHARE:AT_SHARE + E], picked[:, T, :],
                                       prec2[:, T].unsqueeze(2).to_broadcast(shape), ALU.mult))

            def places(turn_no, j, buffer_free):
                ranked = pair[1][:, 1, 0:(TILES + 1) * E].rearrange("p (c e) -> p c e", e=E)
                base = PLACE * turn_no
                dve.wait_ge(rank_mm, turn_no + 1)
                dve.tensor_tensor(place[:, :, :], ranked[:, 0:TILES, :],
                                  free[:, :].unsqueeze(1).to_broadcast([P, TILES, E]), ALU.add)\
                    .then_inc(place_steps, 1)
                dve.wait_ge(place_steps, base + 1)
                dve.tensor_tensor(free[:, :], ranked[:, TILES, :], free[:, :], ALU.add).then_inc(placed, 1)
                for n, hit in enumerate((hit0, hit1)):
                    dve.tensor_tensor(mine[:, n, :, :], place[:, :, :], hit[:, :, :], ALU.mult)\
                        .then_inc(place_steps, 1)
                dve.wait_ge(place_steps, base + 3)
                dve.tensor_reduce(minef[:, :, :], mine[:, :, :, :], AX.X, ALU.add).then_inc(place_steps, 1)
                buffer_free()
                dve.wait_ge(place_steps, base + 4)
                dve.tensor_copy(place_of[:, j, :, :], minef[:, :, :]).then_inc(place_steps, 1)

            def output_rows(i, j):
                dve.wait_ge(place_steps, PLACE * both(i, j, -1))
                dve.tensor_copy(rec[:, j, :, AT_ROW:AT_ROW + 1].bitcast(U32), rows_sb[:, j, :].unsqueeze(2))\
                    .then_inc(row_done, 1)
                dve.wait_ge(row_done, 2 * own(i, j, -1) + 1)
                dve.tensor_scalar(rows_sb[:, j, :], rows_sb[:, j, :], float(S + 1), None, ALU.add).then_inc(row_done, 1)

            dve.memset(half[:, :], -0.5).then_inc(half_set, 1)
            dve.wait_ge(loaded, LOADS)
            take_moments(0, h0[:, 0, :, :], 1, 0)
            norm(0, h0[:, 0, :, :], a_sb, 1, 0, lambda: None)
            dve.tensor_copy(before_bf[:, :, :], before_sb[:, :, :]).then_inc(begun, 1)
            dve.memset(taken[:, :, :], 0.0).then_inc(begun, 1)
            dve.memset(ones[:, :], 1.0).then_inc(begun, 1)
            dve.memset(hit0[:, :, :], 0.0).then_inc(begun, 1)
            dve.memset(hit1[:, :, :], 0.0).then_inc(begun, 1)
            dve.tensor_copy(free[:, :], starts_sb[:, :]).then_inc(begun, 1)
            dve.memset(rec[:, :, :, :], 0.0).then_inc(begun, 1)
            dve.memset(pad[:, :, :], 0.0).then_inc(pad_done, 1)
            dve.wait_ge(pad_done, 1)
            dve.tensor_copy(pad[:, :, AT_ROW:AT_ROW + 1].bitcast(U32),
                            pad_row_sb[:, :].unsqueeze(2)).then_inc(pad_done, 1)
            dve.wait_ge(begun, 7)
            dve.tensor_copy(rec[:, 1, 0, AT_ROW:AT_ROW + 1].bitcast(U32), cls_row_sb[:, :]).then_inc(begun, 1)
            dve.wait_ge(posw_mm, 1)
            for c in range(S // P):
                ins = dve.tensor_tensor(posw[:, c, :], pair[c // 4][:, (c // 2) % 2, (c % 2) * D:(c % 2) * D + D],
                                        bias_sb[:, :], ALU.add)
            ins.then_inc(posw_done, 1)
            for m in range(2):
                dve.wait_ge(a_hi_done, m + 1)
                dve.tensor_tensor(a_lo[:, m, 0:P], pair[3][:, m, 0:P], a_hi[:, m, 0:P].bitcast(F32), ALU.subtract)\
                    .then_inc(a_lo_done, 1)
            dve.wait_ge(cls_qkv, 3)
            dve.tensor_tensor(qk0, q0, k0, ALU.mult).then_inc(cls_score, 1)
            dve.wait_ge(cls_score, 1)
            dve.tensor_reduce(s0[:, :], qk0, AX.X, ALU.add).then_inc(cls_score, 1)
            dve.wait_ge(cls_score, 2)
            dve.scalar_tensor_tensor(h1[:, 0, :], v0, s0[:, 0:1], h0[:, 0, 0, :], ALU.mult, ALU.add)\
                .then_inc(h1_done, 2)
            dve.wait_ge(h1_done, 2)
            take_moments(1, h1, 1, 0)
            norm(1, h1, rec[:, 1, :, 0:D], 1, 0, lambda: None)
            take_logits(1, 0)
            router(1, 0, 1)
            places(0, 1, lambda: None)
            dve.wait_ge(posw_done, 1)
            add_position(0, 0)
            first_moments(0, 0)
            first_norm(0, 0)
            low_a(0, 0)

            def turn(i, j):
                if lives(i, j, -2):
                    take_logits(TILES, both(i, j, -3))
                if lives(i, j, 0):
                    rotate(i, j, 0)
                    rotate(i, j, 1)
                if lives(i, j, -2):
                    router(TILES, both(i, j, -3), j)
                if lives(i, j, -1):
                    after_retention(image(i, j, -1), parity(j, -1))
                if lives(i, j, -2):
                    def buffer_free():
                        wait(dve, scattered[j], SCATTERS * image(i, j, -2))

                    places(both(i, j, -3), j, buffer_free)
                    output_rows(image(i, j, -2), j)
                if lives(i, j, 1):
                    add_position(image(i, j, 1), parity(j, 1))
                if lives(i, j, 0):
                    masked(i, j)
                if lives(i, j, 1):
                    first_moments(image(i, j, 1), parity(j, 1))
                if lives(i, j, -1):
                    second_norm(image(i, j, -1), parity(j, -1))
                if lives(i, j, 1):
                    first_norm(image(i, j, 1), parity(j, 1))
                if lives(i, j, 0):
                    states(i, j, state_tiles(j)[:2])
                if lives(i, j, 1):
                    low_a(image(i, j, 1), parity(j, 1))
                if lives(i, j, 0):
                    states(i, j, state_tiles(j)[2:])

            schedule(dve, turn)

            made = [0]

            def step(ins):
                ins.then_inc(table, 1)
                made[0] += 1

            def steps_landed():
                dve.wait_ge(table, made[0])

            def by_expert(buf, n):
                return buf[:, :].unsqueeze(1).to_broadcast([P, n, E])

            dve.wait_ge(placed, NB + 1)
            dve.wait_ge(rope_done, 2 * NB)
            step(dve.tensor_tensor(count[:, :], free[:, :], starts_sb[:, :], ALU.subtract))
            step(dve.tensor_copy(end_of[:, :], free[:, :]))
            steps_landed()
            step(dve.tensor_tensor(fuller[:, :, :], count[:, :].unsqueeze(2).to_broadcast([P, E, MOST]),
                                   steps_sb[:, :].unsqueeze(1).to_broadcast([P, E, MOST]), ALU.is_gt))
            steps_landed()
            step(dve.tensor_reduce(blocks_of[:, :], fuller[:, :, :], AX.X, ALU.add))
            steps_landed()
            step(dve.tensor_tensor_scan(blocks_to[:, :], ones[:, :], blocks_of[:, :], 0.0, ALU.mult, ALU.add))
            steps_landed()
            step(dve.tensor_tensor(past[:, :, :], numbers_sb[:, :].unsqueeze(2).to_broadcast([P, NX, E]),
                                   by_expert(blocks_to, NX), ALU.is_ge))
            steps_landed()
            step(dve.tensor_reduce(expert_f[:, :], past[:, :, :], AX.X, ALU.add))
            step(dve.tensor_tensor(past_blocks[:, :, :], past[:, :, :], by_expert(blocks_of, NX), ALU.mult))
            steps_landed()
            step(dve.tensor_reduce(skipped[:, :], past_blocks[:, :, :], AX.X, ALU.add))
            steps_landed()
            step(dve.tensor_tensor(skipped[:, :], numbers_sb[:, :], skipped[:, :], ALU.subtract))
            steps_landed()
            step(dve.tensor_scalar(skipped[:, :], skipped[:, :], float(W), None, ALU.mult))
            steps_landed()
            step(dve.scalar_tensor_tensor(record_f[:, :], expert_f[:, :], float(REGION), skipped[:, :], ALU.mult,
                                          ALU.add))
            step(dve.tensor_scalar(real_expert[:, :], expert_f[:, :], float(E - 1), None, ALU.min))
            steps_landed()
            step(dve.tensor_copy(record_of[:, :], record_f[:, :]))
            step(dve.tensor_copy(expert_of[:, :], real_expert[:, :]))
            steps_landed()
            for j in range(NJ):
                dve.wait_ge(scattered[j], SCATTERS * B)
            dve.wait_ge(cls_scattered, 32)
            dve.sem_inc(tables_done, 1)

        @block.gpsimd
        def _(pool):
            def inverse_deviation(which, tiles, turn_no):
                wait_apart(pool, moments_done[which], turn_no + 1)
                pool.tensor_scalar(var_eps[which][:, 0:tiles], moments[which][:, 0:tiles, 1], EPS, None, ALU.add)\
                    .then_inc(var_done[which], 1)
                pool.wait_ge(var_done[which], turn_no + 1)
                pool.tensor_tensor(rstd[which][:, 0:tiles], var_eps[which][:, 0:tiles], half[:, 0:tiles], ALU.pow)\
                    .then_inc(rstd_done[which], 1)

            def rotate(i, j, m):
                if m == 1:
                    wait(pool, o_mm, 2 * own(i, j, -2))
                    dst = q_sb[:, j, :, :]
                else:
                    wait(pool, kt_mm, 2 * own(i, j, -1))
                    dst = k_sb[:, :, :]
                pool.wait_ge(rope_mult, 2 * own(i, j, -1) + m + 1)
                pool.tensor_tensor(dst[:, 0, :], by_cos[:, m, 0, :], by_sin[:, m, 1, :], ALU.subtract)
                pool.tensor_tensor(dst[:, 1, :], by_cos[:, m, 1, :], by_sin[:, m, 0, :], ALU.add)\
                    .then_inc(rope_done, 1)

            def residual(i, j):
                wait(pool, r_stored[j], 16 * i)
                if isinstance(i, int) and i == j == 0:
                    pool.wait_ge(cls_stored, 16)
                pool.wait_ge(normed[1], TILES * own(i, j) + 1)
                pool.tensor_tensor(r_sb[:, j, :, :], h1[:, :, :], rec[:, j, :, 0:D], ALU.add).then_inc(r_done, 1)

            def scatter(i, j, tiles):
                wait_apart(pool, row_done, 2 * own(i, j, -1) + 1)
                for c in tiles:
                    for n in range(2):
                        pool.indirect_dma_start(records, bass.IndirectOffsetOnAxis(ap=place_of[:, j, n, c:c + 1], axis=0),
                                                rec[:, j, c, :], None).then_inc(scattered[j], 16)

            pool.wait_ge(half_set, 1)
            inverse_deviation(0, 1, 0)
            pool.wait_ge(loaded, LOADS)
            whole = "p m k n -> p (m k n)"
            pool.tensor_scalar(qkv_hi[:, :, :, :].rearrange(whole), qkv_sb[:, :, :, :].rearrange(whole), 1.0, 0.0,
                               ALU.mult, ALU.add).then_inc(split_hi, 1)
            pool.wait_ge(split_hi, 1)
            pool.tensor_tensor(qkv_lo[:, :, :, :].rearrange(whole), qkv_sb[:, :, :, :].rearrange(whole),
                               qkv_hi[:, :, :, :].rearrange(whole).bitcast(F32), ALU.subtract).then_inc(qkv_split, 1)
            inverse_deviation(1, 1, 0)
            pool.wait_ge(normed[1], 1)
            pool.tensor_tensor(r_sb[:, 1, 0, :], h1[:, 0, :], rec[:, 1, 0, 0:D], ALU.add).then_inc(r_done, 1)
            pool.wait_ge(place_steps, PLACE)
            for n in range(2):
                pool.indirect_dma_start(records, bass.IndirectOffsetOnAxis(ap=place_of[0:B, 1, n, 0:1], axis=0),
                                        rec[0:B, 1, 0, :], None).then_inc(cls_scattered, 16)
            inverse_deviation(0, TILES, 1)

            def turn(i, j):
                if lives(i, j, 0):
                    rotate(i, j, 0)
                    rotate(i, j, 1)
                if lives(i, j, -3):
                    scatter(image(i, j, -3), parity(j, -3), range(TILES // 2, TILES))
                if lives(i, j, -1):
                    inverse_deviation(1, TILES, both(i, j, -2))
                if lives(i, j, 1):
                    inverse_deviation(0, TILES, both(i, j, 0))
                if lives(i, j, -1):
                    residual(image(i, j, -1), parity(j, -1))
                if lives(i, j, -2):
                    scatter(image(i, j, -2), j, range(TILES // 2))

            schedule(pool, turn)
            scatter(B - 1, NJ - 1, range(TILES // 2, TILES))


def phase2(nc, sem, wait, pair, raw, expert_of, record_of, records, b1_fm, b2, ident, hi_lo, out):
    ctx = ExitStack()
    with ctx:
        def sb(name, shape, dt=F32):
            return ctx.enter_context(nc.sbuf_tensor(name, shape, dt))

        SIDE = 2 * KC * D
        every = sb("every", [P, E, 2 * SIDE + D], F32R)
        b1_sb = sb("b1_sb", [P, E, KC])
        b2_sb = sb("b2_sb", [2, E, D])
        b2_hi = sb("b2_hi", [2, E, D], F32R)
        b2_lo = sb("b2_lo", [2, E, D])
        b2_top = sb("b2_top", [2, E, D])
        hi_lo_sb = sb("hi_lo_sb", [2, 2])
        ident_sb = sb("ident_p2", [P, P])
        ones_row = sb("ones_row", [2, P], F32R)
        w1_sb = sb("w1_sb", [P, 2, SIDE], F32R)
        bias = sb("bias", [P, 2, KC])
        share = sb("share", [P, 2, TILES])
        row_of = sb("row_of", [P, STEPS, TILES], U32)
        x_in = sb("x_in", [P, STEPS, TILES, REC])
        x_hi = sb("x_hi", [P, KC, W], F32R)
        x_lo = sb("x_lo", [P, KC, W], F32R)
        g = raw[:, 0:2, :, :, :].rearrange("p o k a n -> p o k (a n)")
        y_sb = raw[:, 2:4, :, :, :].rearrange("p o m k n -> p o (m k) n")
        g_hi = sb("g_hi", [P, 2, KC, W], F32R)
        g_lo = sb("g_lo", [P, 2, KC, W], F32R)

        apart = sem("apart_p2")
        small_in, w_hi_done, w_lo_done, b2_steps = sem("small_in"), sem("w_hi_done"), sem("w_lo_done"), sem("b2_steps")
        x_loaded = [sem(f"records_in{n}") for n in range(STEPS)]
        t_mm, x_hi_done, x_lo_done = sem("t_mm"), sem("x_hi_done"), sem("x_lo_done")
        w1_here, share_here = sem("w1_here"), sem("share_here")
        h_mm, gelu_done, g_hi_done, g_lo_done = sem("h_mm"), sem("gelu_done"), sem("g_hi_done"), sem("g_lo_done")
        y_mm, y_done = sem("y_mm"), sem("y_done")
        added = [sem(f"added{n}") for n in range(STEPS)]

        ADDS = 16 * TILES

        def own(i, j, d=0):
            return STEPS * i + j + d + 1

        def lives(i, j, d):
            return not isinstance(i, int) or 0 <= STEPS * i + j + d < NX

        def at(i, j, d):
            return i + (j + d) // STEPS, (j + d) % STEPS

        def schedule(eng, turn):
            for j in range(STEPS):
                turn(0, j)
            with eng.Fori(1, NX // STEPS - 1) as i:
                for j in range(STEPS):
                    turn(i, j)
            for j in range(STEPS):
                turn(NX // STEPS - 1, j)

        block = ctx.enter_context(nc.Block())

        @block.sync
        def _(sp):
            def load(i, j):
                wait(sp, t_mm, 2 * own(i, j, -STEPS))
                wait(sp, share_here, own(i, j, -STEPS))
                first = nc.values_load(record_of[0:1, bass.ds(STEPS * i + j, 1)], engines=[sp.engine], min_val=0,
                                       max_val=E * REGION + (NX - 1) * W)
                sp.dma_start(x_in[:, j, :, :], records[bass.ds(first, W)].rearrange("(p c) n -> p c n", p=P))\
                    .then_inc(x_loaded[j], 16)

            for j in range(STEPS):
                load(0, j)
                if j == 0:
                    for m in range(2):
                        sp.dma_start(b2_sb[m:m + 1, :, :], b2.unsqueeze(0)).then_inc(small_in, 16)
                    for dst, src in ((hi_lo_sb[:, :], hi_lo), (b1_sb[:, :, :], b1_fm), (ident_sb[:, :], ident)):
                        sp.dma_start(dst, src).then_inc(small_in, 16)

            def turn(i, j):
                if lives(i, j, STEPS):
                    load(*at(i, j, STEPS))

            schedule(sp, turn)
            for j in range(STEPS):
                sp.wait_ge(added[j], ADDS * (NX // STEPS))

        @block.tensor
        def _(pe):
            def transposes(i, j):
                pe.wait_ge(x_loaded[j], 16 * (i + 1))
                wait(pe, x_hi_done, 2 * own(i, j, -1))
                wait(pe, x_lo_done, 2 * own(i, j, -1))
                for k in range(KC):
                    for c in range(TILES):
                        mm = pe.transpose(pair[0][:, k, c * P:(c + 1) * P], x_in[:, j, c, k * P:(k + 1) * P],
                                          ident_sb[:, :])
                    mm.then_inc(t_mm, 1)

            def first(i, j):
                o = j % 2
                pe.wait_ge(x_hi_done, 2 * own(i, j))
                pe.wait_ge(x_lo_done, 2 * own(i, j))
                pe.wait_ge(w1_here, own(i, j))
                wait(pe, gelu_done, 2 * own(i, j, -2))
                w = w1_sb[:, o, :].rearrange("p (h k n) -> p h k n", h=2, k=KC)
                for f in range(KC):
                    n = 0
                    for k in range(KC):
                        for h, x in ((1, x_hi), (0, x_lo), (0, x_hi)):
                            mm = pe.matmul(pair[1 + 2 * o][:, f, :], w[:, h, k, f * P:(f + 1) * P], x[:, k, :],
                                           start=(n == 0), stop=(n == 3 * KC - 1))
                            n += 1
                    mm.then_inc(h_mm, 1)

            def second(i, j):
                o = j % 2
                e = nc.values_load(expert_of[0:1, bass.ds(STEPS * i + j, 1)], engines=[pe.engine], min_val=0,
                                   max_val=E - 1)
                pe.wait_ge(g_lo_done, own(i, j))
                wait(pe, y_done, own(i, j, -1))
                for c in range(TILES):
                    dst = pair[2][:, c // 2, (c % 2) * D:(c % 2) * D + D]
                    pe.matmul(dst, ones_row[:, :], every[0:2, bass.ds(e, 1), 2 * SIDE:].rearrange("p a n -> p (a n)"),
                              start=True, stop=False)
                    n = 0
                    for k in range(KC):
                        for x, h in ((g_hi, 1), (g_lo, 0), (g_hi, 0)):
                            part = SIDE + (h * KC + k) * D
                            w = every[:, bass.ds(e, 1), part:part + D].rearrange("p a n -> p (a n)")
                            mm = pe.matmul(dst, x[:, o, k, c * P:(c + 1) * P], w, start=False, stop=(n == 3 * KC - 1))
                            n += 1
                mm.then_inc(y_mm, 1)

            pe.wait_ge(small_in, 16 * 5)
            transposes(0, 0)
            pe.wait_ge(b2_steps, 6)
            pe.wait_ge(w_lo_done, 2 * E)
            first(0, 0)
            transposes(0, 1)

            def turn(i, j):
                if lives(i, j, 1):
                    first(*at(i, j, 1))
                if lives(i, j, 2):
                    transposes(*at(i, j, 2))
                second(i, j)

            schedule(pe, turn)

        @block.scalar
        def _(act):
            def high_x(i, j):
                for k in range(KC):
                    wait(act, h_mm, 2 * own(i, j, -1))
                    act.wait_ge(t_mm, 2 * own(i, j, -1) + k + 1)
                    act.activation(x_hi[:, k, :], pair[0][:, k, :], ACT.Copy).then_inc(x_hi_done, 1)

            def gelu(i, j):
                o = j % 2
                wait(act, g_lo_done, own(i, j, -2))
                act.wait_ge(w1_here, own(i, j))
                for f in range(KC):
                    act.wait_ge(h_mm, 2 * own(i, j, -1) + f + 1)
                    act.activation(g[:, o, f, :], pair[1 + 2 * o][:, f, :], ACT.Gelu, bias=bias[:, o, f:f + 1])\
                        .then_inc(gelu_done, 1)

            def high_g(i, j):
                o = j % 2
                wait(act, y_mm, own(i, j, -2))
                act.wait_ge(gelu_done, 2 * own(i, j))
                act.activation(g_hi[:, o, :, :], g[:, o, :, :], ACT.Copy).then_inc(g_hi_done, 1)

            for e in range(E):
                for m in range(2):
                    act.activation(every[:, e, m * SIDE:m * SIDE + KC * D],
                                   raw[:, e, m, :, :].rearrange("p k n -> p (k n)"), ACT.Copy).then_inc(w_hi_done, 1)
            high_x(0, 0)
            gelu(0, 0)
            high_x(0, 1)
            high_g(0, 0)

            def turn(i, j):
                if lives(i, j, 1):
                    gelu(*at(i, j, 1))
                if lives(i, j, 2):
                    high_x(*at(i, j, 2))
                if lives(i, j, 1):
                    high_g(*at(i, j, 1))

            schedule(act, turn)

        @block.vector
        def _(dve):
            def expert(i, j):
                return nc.values_load(expert_of[0:1, bass.ds(STEPS * i + j, 1)], engines=[dve.engine], min_val=0,
                                      max_val=E - 1)

            def low_x(i, j):
                for k in range(KC):
                    dve.wait_ge(x_hi_done, 2 * own(i, j, -1) + k + 1)
                    dve.tensor_tensor(x_lo[:, k, :], pair[0][:, k, :], x_hi[:, k, :].bitcast(F32), ALU.subtract)\
                        .then_inc(x_lo_done, 1)

            def take_w1(i, j):
                e = expert(i, j)
                wait(dve, gelu_done, 2 * own(i, j, -2))
                dve.sem_inc(apart, 1)
                dve.tensor_copy(w1_sb[:, j % 2, :], every[:, bass.ds(e, 1), 0:SIDE].rearrange("p a n -> p (a n)"))
                dve.tensor_copy(bias[:, j % 2, :], b1_sb[:, bass.ds(e, 1), :].rearrange("p a n -> p (a n)"))\
                    .then_inc(w1_here, 1)

            def take_share(i, j):
                e = expert(i, j)
                wait(dve, y_done, own(i, j, -2))
                dve.sem_inc(apart, 1)
                dve.tensor_copy(share[:, j % 2, :].unsqueeze(2), x_in[:, j, :, bass.ds(AT_SHARE + e, 1)])
                dve.tensor_copy(row_of[:, j, :].unsqueeze(2), x_in[:, j, :, AT_ROW:AT_ROW + 1].bitcast(U32))\
                    .then_inc(share_here, 1)

            def low_g(i, j):
                o = j % 2
                dve.wait_ge(g_hi_done, own(i, j))
                dve.tensor_tensor(g_lo[:, o, :, :], g[:, o, :, :], g_hi[:, o, :, :].bitcast(F32), ALU.subtract)\
                    .then_inc(g_lo_done, 1)

            def weigh(i, j):
                dve.wait_ge(share_here, own(i, j))
                dve.wait_ge(y_mm, own(i, j))
                ii, jj = at(i, j, -2)
                wait(dve, added[jj], ADDS * (ii + 1))
                for c in range(TILES):
                    ins = dve.tensor_scalar(y_sb[:, j % 2, c, :], pair[2][:, c // 2, (c % 2) * D:(c % 2) * D + D],
                                            share[:, j % 2, c:c + 1], None, ALU.mult)
                ins.then_inc(y_done, 1)

            dve.wait_ge(small_in, 16 * 5)
            dve.tensor_copy(b2_hi[:, :, :], b2_sb[:, :, :]).then_inc(b2_steps, 1)
            dve.memset(every[:, :, 2 * SIDE:].bitcast(F32), 0.0).then_inc(b2_steps, 1)
            dve.memset(ones_row[:, :].bitcast(F32), 1.0).then_inc(b2_steps, 1)
            dve.wait_ge(b2_steps, 3)
            dve.tensor_tensor(b2_lo[:, :, :], b2_sb[:, :, :], b2_hi[:, :, :].bitcast(F32), ALU.subtract)\
                .then_inc(b2_steps, 1)
            dve.tensor_scalar(b2_top[:, :, :], b2_hi[:, :, :].bitcast(F32), hi_lo_sb[:, 0:1], None, ALU.mult)\
                .then_inc(b2_steps, 1)
            dve.wait_ge(b2_steps, 5)
            dve.scalar_tensor_tensor(every[0:2, :, 2 * SIDE:], b2_lo[:, :, :], hi_lo_sb[:, 1:2], b2_top[:, :, :],
                                     ALU.mult, ALU.add).then_inc(b2_steps, 1)
            low_x(0, 0)
            for e in range(E):
                for m in range(2):
                    dve.wait_ge(w_hi_done, 2 * e + m + 1)
                    half = m * SIDE + KC * D
                    dve.tensor_tensor(every[:, e, half:half + KC * D], raw[:, e, m, :, :].rearrange("p k n -> p (k n)"),
                                      every[:, e, m * SIDE:half].bitcast(F32), ALU.subtract).then_inc(w_lo_done, 1)
            dve.wait_ge(w_lo_done, 2 * E)
            dve.wait_ge(b2_steps, 6)
            take_w1(0, 0)
            take_share(0, 0)
            take_w1(0, 1)
            low_x(0, 1)
            low_g(0, 0)

            def turn(i, j):
                if lives(i, j, 2):
                    take_w1(*at(i, j, 2))
                    low_x(*at(i, j, 2))
                if lives(i, j, 1):
                    take_share(*at(i, j, 1))
                    low_g(*at(i, j, 1))
                weigh(i, j)

            schedule(dve, turn)

        @block.gpsimd
        def _(pool):
            def turn(i, j):
                pool.wait_ge(y_done, own(i, j))
                ii, jj = at(i, j, -1)
                wait(pool, added[jj], ADDS * (ii + 1))
                pool.sem_inc(apart, 1)
                for c in range(TILES):
                    pool.indirect_dma_start(
                        out, bass.IndirectOffsetOnAxis(ap=row_of[:, j, c:c + 1], axis=0),
                        y_sb[:, j % 2, c, :], None, compute_op=ALU.add).then_inc(added[j], 16)

            schedule(pool, turn)


_INS = ("x_fm", "pos_fm", "dense_w", "dense_b", "cls_rows", "wq", "wk", "wv", "router_fm", "w1", "b1_fm", "w2",
        "b2", "rope", "mask", "ident", "iota", "before", "rows", "cls_row", "pad_row", "starts", "steps", "numbers",
        "hi_lo")


def _patches(img):
    n, g = img.shape[0], IMG // PATCH
    return img.reshape(n, g, PATCH, g, PATCH).transpose(0, 2, 4, 1, 3).reshape(n, D, S)


def _tables():
    inv_freq = (np.float32(1.0) / np.float32(10000.0) ** (np.arange(0, D, 2, dtype=np.float32) / np.float32(D)))
    angle = (inv_freq[:, None] * np.arange(1, S + 1, dtype=np.float32)[None, :]).astype(np.float64)
    at = np.arange(S) % P
    grow, fall = GAMMA ** (at + 1.0), GAMMA ** (P - 1.0 - at)
    rope = np.stack([np.cos(angle) * grow, np.sin(angle) * grow, np.cos(angle) * fall, np.sin(angle) * fall], axis=1)
    j, i = np.arange(P)[:, None], np.arange(P)[None, :]
    mask = np.where(j <= i, GAMMA ** -float(P), 0.0)
    t = np.arange(P)
    f32 = np.float32
    return {
        "rope": rope.reshape(P, 4, NJ, W).astype(np.float32),
        "mask": mask.astype(np.float32),
        "ident": np.eye(P, dtype=np.float32),
        "iota": np.broadcast_to(np.arange(E, dtype=np.float32), (P, E)),
        "before": np.stack([t[:, None] < t[None, :], np.ones((P, P))], axis=1).astype(f32),
        "rows": (1 + np.arange(NJ)[:, None] * W + np.arange(TILES)[None, :] * P + t[:, None, None]).astype(f32),
        "cls_row": ((t % B) * (S + 1)).astype(f32)[:, None],
        "pad_row": (TOKENS + np.arange(W).reshape(P, TILES)).astype(f32),
        "starts": np.broadcast_to(np.arange(E, dtype=f32) * REGION, (P, E)),
        "steps": np.broadcast_to(np.arange(MOST, dtype=f32) * W, (P, MOST)),
        "numbers": np.broadcast_to(np.arange(NX, dtype=f32), (P, NX)),
        "hi_lo": np.eye(2, dtype=f32),
    }


def kernel(**inputs):
    import numpy as _np
    import concourse.bacc as _bacc
    from concourse import mybir as _mybir
    from concourse.bass_utils import run_bass_kernel_spmd as _run

    a = {k: _np.asarray(v) for k, v in inputs.items()}
    halves = _np.concatenate([_np.arange(0, D, 2), _np.arange(1, D, 2)])
    x = _patches(a["x"].reshape(B, IMG, IMG)).reshape(B, KC, P, NJ, W).transpose(0, 3, 2, 1, 4).reshape(NB, P, KC, W)
    g = IMG // 8
    pos = a["L0_tok_pos_emb"].reshape(g, g, 8, 8).transpose(0, 2, 1, 3).reshape(1, IMG, IMG)
    given = {
        "x_fm": x,
        "pos_fm": _patches(pos)[0].reshape(KC, P, S).transpose(1, 0, 2),
        "dense_w": a["L0_tok_dense_w"],
        "dense_b": _np.broadcast_to(a["L0_tok_dense_b"], (P, D)),
        "cls_rows": _np.broadcast_to(a["cls_tok"].reshape(1, D), (P, D)),
        "wq": a["L0_attn_W_Q"][:, halves],
        "wk": a["L0_attn_W_K"][:, halves],
        "wv": a["L0_attn_W_V"],
        "router_fm": a["L0_ffn_router_w"].T.reshape(KC, P, E).transpose(1, 0, 2),
        "w1": a["L0_ffn_w1"],
        "b1_fm": a["L0_ffn_b1"].reshape(E, KC, P).transpose(2, 0, 1),
        "w2": a["L0_ffn_w2"],
        "b2": a["L0_ffn_b2"],
        **_tables(),
    }
    nc = _bacc.Bacc("TRN2", target_bir_lowering=False, num_devices=1)
    arrays, args = {}, {}
    for name in _INS:
        v = _np.ascontiguousarray(given[name])
        arrays[name] = v
        args[name] = nc.dram_tensor(name, v.shape, _mybir.dt.from_np(v.dtype), kind="ExternalInput").ap()
    out = nc.dram_tensor("out", (TOKENS + W, D), _mybir.dt.float32, kind="ExternalOutput").ap()
    vit_kernel(nc, out=out, **args)
    r = _run(nc, [arrays], core_ids=[0])
    return r.results[0]["out"][:TOKENS].reshape(B, S + 1, D)
```

```python
from contextlib import ExitStack

import numpy as np

import concourse.bass as bass
from concourse import mybir

F32 = mybir.dt.float32
F32R = mybir.dt.float32r
U32 = mybir.dt.uint32
I32 = mybir.dt.int32
BF16 = mybir.dt.bfloat16
ALU = mybir.AluOpType
ACT = mybir.ActivationFunctionType
AX = mybir.AxisListType

P = 128
IMG, PATCH = 512, 16
B = 16
D = 256
KC = D // P
S = (IMG // PATCH) ** 2
TILES = 4
W = TILES * P
NJ = S // W
NB = B * NJ
E = 8
GAMMA = 0.96875
DECAY = GAMMA ** P
EPS = 1e-5
TOKENS = B * (S + 1)
REC = D + 16
AT_SHARE, AT_ROW = D, D + E
REGION = TOKENS + W
DUMMY = E
NX = (2 * TOKENS + E * (W - 1)) // W
STEPS = 4
NX = -(-NX // STEPS) * STEPS
MIN_X = -(-2 * TOKENS // W)
MOST = -(-TOKENS // W)
SCATTERS = 16 * 2 * TILES
ADDS = 16 * TILES
PADS = 16 * (NX - MIN_X + 1 + E)


def vit_kernel(nc, x_fm, pos_fm, dense_w, dense_b, cls_rows, wq, wk, wv, router_fm, w1, b1_fm, w2, b2,
               rope, mask, ident, iota, before, rows, cls_row, pad_row, starts, steps, numbers, adds_before, out):
    assert NX - MOST > 0
    records = nc.dram_tensor("records", [E * REGION + NX * W, REC], F32, kind="Internal").ap()

    top = ExitStack()
    with top:
        def sem(name):
            return top.enter_context(nc.semaphore(name))

        def wait(eng, s, value):
            if not isinstance(value, int) or value > 0:
                eng.wait_ge(s, value)

        def sb(name, shape, dt=F32):
            return top.enter_context(nc.sbuf_tensor(name, shape, dt))

        pair = [top.enter_context(nc.psum_tensor(f"pair{n}", [P, 2, 512], F32)) for n in range(4)]
        raw = sb("raw", [P, E, 2, KC, D])
        expert_of = sb("expert_of", [P, NX], I32)
        record_of = sb("record_of", [P, NX], I32)
        adds_due = sb("adds_due", [P, NX], I32)
        pad = sb("pad", [P, TILES, REC])
        ident_sb = sb("ident_sb", [P, P])
        scattered = [sem(f"scattered{j}") for j in range(NJ)]
        cls_scattered, pads_stored = sem("cls_scattered"), sem("pads_stored")
        arrivals = [(s, SCATTERS * B) for s in scattered] + [(cls_scattered, 32), (pads_stored, PADS)]

        phase1(nc, sem, wait, pair, raw, expert_of, record_of, pad, ident_sb, scattered, cls_scattered, pads_stored,
               records, x_fm, pos_fm, dense_w, dense_b, cls_rows,
               wq, wk, wv, router_fm, w1, w2, rope, mask, ident, iota, before, rows, cls_row, pad_row, starts, steps,
               numbers, adds_before, adds_due, out)
        phase2(nc, sem, wait, pair, raw, expert_of, record_of, adds_due, ident_sb, arrivals, records, b1_fm, b2, out)


def phase1(nc, sem, wait, pair, raw, expert_of, record_of, pad, ident_sb, scattered, cls_scattered, pads_stored,
           records, x_fm, pos_fm, dense_w, dense_b, cls_rows,
           wq, wk, wv, router_fm, w1, w2, rope, mask, ident, iota, before, rows, cls_row, pad_row, starts, steps,
           numbers, adds_before, adds_due, out):
    ctx = ExitStack()
    with ctx:
        def sb(name, shape, dt=F32):
            return ctx.enter_context(nc.sbuf_tensor(name, shape, dt))

        mask_sb = sb("mask_sb", [P, P])
        iota_sb = sb("iota_sb", [P, E])
        before_sb = sb("before_sb", [P, 2, P])
        before_bf = sb("before_bf", [P, 2, P], BF16)
        rows_sb = sb("rows_sb", [P, NJ, TILES])
        cls_row_sb = sb("cls_row_sb", [P, 1])
        pad_row_sb = sb("pad_row_sb", [P, TILES])
        steps_sb = sb("steps_sb", [P, MOST])
        numbers_sb = sb("numbers_sb", [P, NX])
        starts_sb = sb("starts_sb", [P, E])
        rope_sb = sb("rope_sb", [P, 4, NJ, W])
        dense_hi = sb("dense_hi", [P, KC, D], F32R)
        dense_lo = sb("dense_lo", [P, KC, D], F32R)
        bias_sb = sb("bias_sb", [P, D])
        router_sb = sb("router_sb", [P, KC, E])
        qkv_hi = sb("qkv_hi", [P, 3, KC, D], F32R)
        qkv_lo = sb("qkv_lo", [P, 3, KC, D], F32R)
        posw = sb("posw", [P, S // P, D])
        half = sb("half", [P, TILES])
        x_sb = sb("x_sb", [P, KC, W])
        x_hi = sb("pixels_hi", [P, KC, W], F32R)
        x_lo = sb("pixels_lo", [P, KC, W], F32R)
        h0 = sb("h0", [P, NJ, TILES, D])
        h1 = sb("h1", [P, TILES, D])
        a_sb = sb("a_sb", [P, TILES, D])
        rec = sb("rec", [P, NJ, TILES, REC])
        stats = [sb(f"stats{n}", [P, TILES, 6]) for n in range(2)]
        moments = [sb(f"moments{n}", [P, TILES, 2]) for n in range(2)]
        var_eps = [sb(f"var_eps{n}", [P, TILES]) for n in range(2)]
        shift = sb("shift", [P, TILES])
        rstd = [sb(f"rstd{n}", [P, TILES]) for n in range(2)]
        a_hi = sb("a_hi", [P, KC, W], F32R)
        a_lo = sb("a_lo", [P, KC, W], F32R)
        by_cos = sb("by_cos", [P, 2, 2, W])
        by_sin = sb("by_sin", [P, 2, 2, W])
        q_sb = sb("q_sb", [P, NJ, KC, W])
        k_sb = sb("k_sb", [P, KC, W])
        v_sb = sb("v_sb", [P, NJ, TILES, D])
        kt_sb = sb("kt_sb", [P, TILES, D])
        p_sb = sb("p_sb", [P, TILES, P])
        z_sb = sb("z_sb", [P, NJ * TILES, KC, D])
        before_states = z_sb[:, 1:, :, :].rearrange("p c k n -> p (c k n)")
        pos_sb = before_states[:, 0:KC * S].rearrange("p (k s) -> p k s", k=KC)
        qkv_sb = before_states[:, KC * S:KC * S + 3 * KC * D].rearrange("p (m k n) -> p m k n", m=3, k=KC)
        nt_sb = sb("nt_sb", [P, NJ, KC, W])
        r_sb = sb("r_sb", [P, NJ, TILES, D])
        dense_sb = r_sb[:, 0, 0:KC, :]
        lg = sb("lg", [P, TILES, E])
        top8 = sb("top8", [P, TILES, 8])
        idx8 = sb("idx8", [P, TILES, 8], U32)
        idxf = sb("idxf", [P, TILES, 2])
        below = sb("below", [P, TILES, E])
        expo = sb("expo", [P, TILES, E])
        zsum = sb("zsum", [P, TILES])
        zrec = sb("zrec", [P, TILES])
        hit0 = sb("hit0", [P, TILES, E])
        hit1 = sb("hit1", [P, TILES, E])
        prob = sb("prob", [P, TILES, E])
        picked = sb("picked", [P, TILES, E])
        psum2 = sb("psum2", [P, TILES])
        prec2 = sb("prec2", [P, TILES])
        hits = sb("hits", [P, TILES, E])
        taken = sb("taken", [P, TILES, E], BF16)
        free = sb("free", [P, E])
        place = sb("place", [P, TILES, E])
        mine = sb("mine", [P, 2, TILES, E])
        minef = sb("minef", [P, 2, TILES])
        place_of = sb("place_of", [P, NJ, 2, TILES], U32)
        count = sb("count", [P, E])
        fuller = sb("fuller", [P, E, MOST])
        blocks_of = sb("blocks_of", [P, E])
        blocks_to = sb("blocks_to", [P, E])
        ones = sb("ones", [P, E])
        past, past_blocks = (buf[:, 0, :, :].rearrange("p a n -> p (a n)")[:, 0:NX * E]
                             .rearrange("p (x e) -> p x e", e=E) for buf in (by_cos, by_sin))
        expert_f = sb("expert_f", [P, NX])
        skipped = sb("skipped", [P, NX])
        real_expert = sb("real_expert", [P, NX])
        stays = sb("stays", [P, NX])
        has_round = sb("has_round", [P, NX])
        adds_before_sb = sb("adds_before_sb", [P, NX])
        record_f = sb("record_f", [P, NX])
        end_of = sb("end_of", [P, E], I32)
        q0, k0, v0, qk0 = (by_sin[:, 0, n // 2, n % 2 * D:(n % 2 + 1) * D] for n in range(4))
        s0 = sb("s0", [P, 1])

        early_loaded, loaded = sem("early_loaded"), sem("loaded")
        x_loaded, x_hi_done, x_lo_done = sem("x_loaded"), sem("pixels_hi_done"), sem("pixels_lo_done")
        dense_split = sem("dense_split")
        half_set = sem("half_set")
        qkv_split = sem("qkv_split")
        posw_mm, posw_done = sem("posw_mm"), sem("posw_done")
        h0_mm, h0_done = sem("h0_mm"), sem("h0_done")
        stats_done = [sem(f"stats_done{n}") for n in range(2)]
        moments_done = [sem(f"moments_done{n}") for n in range(2)]
        var_done = [sem(f"var_done{n}") for n in range(2)]
        rstd_done = [sem(f"rstd_done{n}") for n in range(2)]
        shift_done = sem("shift_done")
        normed = [sem(f"normed{n}") for n in range(2)]
        at_mm, a_hi_done, a_lo_done = sem("at_mm"), sem("a_hi_done"), sem("a_lo_done")
        q_mm, k_mm, v_mm = sem("q_mm"), sem("k_mm"), sem("v_mm")
        rope_mult, rope_done = sem("rope_mult"), sem("rope_done")
        v_done = sem("v_done")
        s_mm, p_done = sem("s_mm"), sem("p_done")
        kt_mm, kt_done = sem("kt_mm"), sem("kt_done")
        dz_mm, z_done = sem("dz_mm"), sem("z_done")
        o_mm, h1_done = sem("o_mm"), sem("h1_done")
        r_done = sem("r_done")
        nt_mm, nt_done = sem("nt_mm"), sem("nt_done")
        lg_mm, lg_done = sem("lg_mm"), sem("lg_done")
        top_done, idx_done = sem("top_done"), sem("idx_done")
        below_done, expo_done = sem("below_done"), sem("expo_done")
        route = sem("route")
        rank_mm, placed = sem("rank_mm"), sem("placed")
        place_steps = sem("place_steps")
        row_done, begun, pad_done = sem("row_done"), sem("begun"), sem("pad_done")
        table = sem("table")
        raw_loaded = sem("raw_loaded")
        cls_mm, cls_qkv, cls_state = sem("cls_mm"), sem("cls_qkv"), sem("cls_state")
        cls_score, split_hi = sem("cls_score"), sem("split_hi")
        r_stored = [sem(f"r_stored{j}") for j in range(NJ)]
        cls_stored = sem("cls_stored")

        apart = sem("apart")
        EARLY, LATE = 8 * 16, 12 * 16
        ROUTE = 13
        PLACE = 5
        def parity(j, d):
            return (j + d) % NJ

        def image(i, j, d):
            return i + (j + d) // NJ

        def lives(i, j, d):
            return not isinstance(i, int) or 0 <= NJ * i + j + d < NB

        def own(i, j, d=0):
            return NJ * i + j + d + 1

        def both(i, j, d=0):
            return own(i, j, d) + 1

        def states_through(i, j, d=0):
            last = NJ * TILES - 1
            return last * image(i, j, d) + (last if parity(j, d) == NJ - 1 else TILES * (parity(j, d) + 1))

        def state_tiles(j):
            return range(TILES - 1 if j == NJ - 1 else TILES)

        def wait_apart(eng, s, count):
            eng.wait_ge(s, count)
            eng.sem_inc(apart, 1)

        def first_turn(i, j):
            return isinstance(i, int) and i == j == 0

        def schedule(eng, turn):
            for i in range(2):
                for j in range(NJ):
                    turn(i, j)
            with eng.Fori(2, B - 1) as i:
                for j in range(NJ):
                    turn(i, j)
            for i in (B - 1, B):
                for j in range(NJ):
                    turn(i, j)

        block = ctx.enter_context(nc.Block())

        @block.sync
        def _(sp):
            early = ((h0[:, 1, 0, :], cls_rows), (dense_sb, dense_w.rearrange("(k p) n -> p k n", p=P)),
                     (pos_sb, pos_fm), (ident_sb[:, :], ident),
                     (qkv_sb[:, 0, :, :], wq.rearrange("(k p) n -> p k n", p=P)),
                     (qkv_sb[:, 1, :, :], wk.rearrange("(k p) n -> p k n", p=P)),
                     (qkv_sb[:, 2, :, :], wv.rearrange("(k p) n -> p k n", p=P)), (bias_sb[:, :], dense_b))
            late = ((router_sb[:, :, :], router_fm), (rows_sb[:, :, :], rows), (cls_row_sb[:, :], cls_row),
                    (pad_row_sb[:, :], pad_row), (starts_sb[:, :], starts), (iota_sb[:, :], iota),
                    (before_sb[:, :, :], before), (rope_sb[:, :, :, :], rope), (mask_sb[:, :], mask),
                    (steps_sb[:, :], steps), (numbers_sb[:, :], numbers), (adds_before_sb[:, :], adds_before))

            def load_x(i, j):
                wait(sp, x_hi_done, own(i, j, -1))
                wait(sp, x_lo_done, own(i, j, -1))
                sp.dma_start(x_sb[:, :, :], x_fm[bass.ds(NJ * i + j, 1)].rearrange("a p k t -> (a p) k t"))\
                    .then_inc(x_loaded, 16)

            def store_r(i, j):
                sp.wait_ge(r_done, both(i, j))
                sp.dma_start(out[bass.ds(i * (S + 1) + 1 + j * W, W)].rearrange("(c p) n -> p c n", p=P),
                             r_sb[:, j, :, :]).then_inc(r_stored[j], 16)

            for dst, src in early:
                sp.dma_start(dst, src).then_inc(early_loaded, 16)
            load_x(0, 0)
            for dst, src in late:
                sp.dma_start(dst, src).then_inc(loaded, 16)
            load_x(0, 1)
            sp.wait_ge(pad_done, 2)
            for b in range(NX - MIN_X):
                sp.dma_start(records[E * REGION + b * W:E * REGION + (b + 1) * W].rearrange("(p c) n -> p c n", p=P),
                             pad[:, :, :]).then_inc(pads_stored, 16)
            sp.dma_start(out[TOKENS:TOKENS + W].rearrange("(p c) n -> p c n", p=P), pad[:, :, 0:D])\
                .then_inc(pads_stored, 16)
            for e in range(E):
                for m, w in enumerate((w1, w2)):
                    sp.dma_start(raw[:, e, m, :, :], w[e].rearrange("(k p) n -> p k n", p=P)).then_inc(raw_loaded, 16)
            sp.wait_ge(r_done, 1)
            sp.dma_start(out[0:TOKENS].rearrange("(b s) n -> b s n", b=B)[:, 0, :], r_sb[0:B, 1, 0, :])\
                .then_inc(cls_stored, 16)

            def turn(i, j):
                if lives(i, j, 2):
                    load_x(image(i, j, 2), j)
                if lives(i, j, -1):
                    store_r(image(i, j, -1), parity(j, -1))

            schedule(sp, turn)
            sp.wait_ge(table, 2)
            for e in range(E):
                end = nc.values_load(end_of[0:1, e:e + 1], engines=[sp.engine], min_val=e * REGION,
                                     max_val=e * REGION + TOKENS)
                sp.dma_start(records[bass.ds(end, W)].rearrange("(p c) n -> p c n", p=P), pad[:, :, :])\
                    .then_inc(pads_stored, 16)
            sp.wait_ge(cls_stored, 16)
            sp.wait_ge(raw_loaded, 16 * 2 * E)
            for j in range(NJ):
                sp.wait_ge(r_stored[j], 16 * B)

        @block.tensor
        def _(pe):
            def split_product(dst, x, w, x_stationary, low_ready=None):
                passes = [(k, 0, b) for k in range(KC) for b in (1, 0)] + [(k, 1, 0) for k in range(KC)]
                for n, (k, a, b) in enumerate(passes):
                    if a == 1 and k == 0 and low_ready:
                        low_ready()
                    lhs, rhs = (x[a](k), w[b](k)) if x_stationary else (w[b](k), x[a](k))
                    mm = pe.matmul(dst, lhs, rhs, start=(n == 0), stop=(n == len(passes) - 1))
                return mm

            def half_bank(buf, c, width=D):
                return buf[:, c // 2, (c % 2) * D:(c % 2) * D + width]

            def transpose_tiles(src, dst, ready, base, tiles, done):
                for k in range(KC):
                    for c in range(tiles):
                        if k == 0:
                            pe.wait_ge(ready, base + c + 1)
                        mm = pe.transpose(dst[:, k, c * P:(c + 1) * P], src[:, c, k * P:(k + 1) * P], ident_sb[:, :])
                    mm.then_inc(done, 1)

            def project(i, j):
                pe.wait_ge(x_hi_done, own(i, j))
                pe.wait_ge(x_lo_done, own(i, j))
                wait(pe, rope_mult, 2 * own(i, j, -1))
                for c in range(TILES):
                    x = [lambda k, half=half: half[:, k, c * P:(c + 1) * P] for half in (x_hi, x_lo)]
                    w = [lambda k, half=half: half[:, k, :] for half in (dense_hi, dense_lo)]
                    mm = split_product(half_bank(pair[0], c), x, w, True)
                    if c % 2:
                        mm.then_inc(h0_mm, 1)

            def transpose_a(i, j):
                wait(pe, h1_done, 2 * both(i, j, -2))
                transpose_tiles(a_sb, pair[3], normed[0], TILES * own(i, j, -1) + 1, TILES, at_mm)

            def qkv(i, j):
                pe.wait_ge(a_hi_done, 2 * both(i, j))
                x = (lambda k: a_hi[:, k, :]), (lambda k: a_lo[:, k, :])
                for m, dst, done in ((1, pair[1], k_mm), (0, pair[0], q_mm)):
                    if m == 1:
                        wait(pe, z_done, states_through(i, j, -2) + 2 if lives(i, j, -1) else 0)
                    else:
                        pe.wait_ge(lg_done, both(i, j, -2) if lives(i, j, -2) else 1)
                        pe.wait_ge(h0_done, 2 * own(i, j))
                    for f in range(KC):
                        w = [lambda k, half=half: half[:, m, k, f * P:(f + 1) * P] for half in (qkv_hi, qkv_lo)]
                        low_ready = (lambda: pe.wait_ge(a_lo_done, 2 * both(i, j))) if m == 1 and f == 0 else None
                        split_product(dst[:, f, :], x, w, False, low_ready).then_inc(done, 1)
                wait(pe, z_done, states_through(i, j, -1))
                for c in range(TILES):
                    x = [lambda k, half=half: half[:, k, c * P:(c + 1) * P] for half in (a_hi, a_lo)]
                    w = [lambda k, half=half: half[:, 2, k, :] for half in (qkv_hi, qkv_lo)]
                    mm = split_product(half_bank(pair[2], c), x, w, True)
                    if c % 2:
                        mm.then_inc(v_mm, 1)

            def scores(i, j):
                pe.wait_ge(rope_done, 2 * own(i, j))
                for c in range(TILES):
                    for k in range(KC):
                        mm = pe.matmul(pair[1][:, 0, c * P:(c + 1) * P], k_sb[:, k, c * P:(c + 1) * P],
                                       q_sb[:, j, k, c * P:(c + 1) * P], start=(k == 0), stop=(k == KC - 1))
                mm.then_inc(s_mm, 1)
                pe.wait_ge(v_done, 2 * own(i, j))
                for c in range(TILES):
                    for k in range(KC):
                        mm = pe.transpose(pair[2][:, c // 2, (c % 2) * D + k * P:(c % 2) * D + (k + 1) * P],
                                          k_sb[:, k, c * P:(c + 1) * P], ident_sb[:, :])
                    if c % 2:
                        mm.then_inc(kt_mm, 1)

            def state_steps(i, j):
                for c in state_tiles(j):
                    if c == 0:
                        pe.wait_ge(p_done, own(i, j))
                    elif c == 1:
                        pe.wait_ge(placed, 1 if first_turn(i, j) else both(i, j, -2))
                    if c % 2 == 0:
                        pe.wait_ge(kt_done, 2 * own(i, j, -1) + 1 + c // 2)
                    for k in range(KC):
                        mm = pe.matmul(pair[1 + c // 2][:, c % 2, k * D:(k + 1) * D],
                                       kt_sb[:, c, k * P:(k + 1) * P], v_sb[:, j, c, :], start=True, stop=True)
                    mm.then_inc(dz_mm, 1)

            def retention(i, j):
                pe.wait_ge(p_done, own(i, j))
                for c in range(TILES):
                    if c > 0 or j > 0:
                        pe.wait_ge(z_done, states_through(i, j, -1) + c)
                    for k in range(KC):
                        pe.matmul(half_bank(pair[3], c), q_sb[:, j, k, c * P:(c + 1) * P],
                                  z_sb[:, j * TILES + c, k, :], start=(k == 0), stop=False)
                    mm = pe.matmul(half_bank(pair[3], c), p_sb[:, c, :], v_sb[:, j, c, :], start=False, stop=True)
                    if c % 2:
                        mm.then_inc(o_mm, 1)

            def transpose_n(i, j):
                if lives(i, j, 2):
                    pe.wait_ge(h0_done, 2 * own(i, j, 2))
                else:
                    pe.wait_ge(rope_mult, 2 * NB)
                    pe.wait_ge(nt_done, 2 * both(i, j, -1))
                transpose_tiles(rec[:, j, :, :], pair[0], normed[1], TILES * own(i, j, -1) + 1, TILES, nt_mm)

            def logits(src, tiles):
                for c in range(tiles):
                    for k in range(KC):
                        mm = pe.matmul(pair[0][:, 0, c * E:(c + 1) * E], src[:, k, c * P:(c + 1) * P],
                                       router_sb[:, k, :], start=(k == 0), stop=(k == KC - 1))
                mm.then_inc(lg_mm, 1)

            def ranks(parts):
                dst = pair[1][:, 1, 0:(TILES + 1) * E]
                pe.matmul(dst[:, 0:TILES * E], before_bf[0:parts, 0, :],
                          taken[0:parts, :, :].rearrange("p c e -> p (c e)"), start=True, stop=False)
                for c in range(TILES - 1):
                    later = TILES - 1 - c
                    pe.matmul(dst[:, (c + 1) * E:TILES * E].rearrange("p (c e) -> p c e", e=E),
                              before_bf[0:parts, 1, :], taken[0:parts, c:c + 1, :].to_broadcast([parts, later, E]),
                              start=False, stop=(c == TILES - 2))
                for c in range(TILES):
                    mm = pe.matmul(dst[:, TILES * E:], before_bf[0:parts, 1, :], taken[0:parts, c, :],
                                   start=(c == 0), stop=(c == TILES - 1))
                mm.then_inc(rank_mm, 1)

            pe.wait_ge(early_loaded, EARLY)
            for part in range(2):
                for c in range(TILES):
                    at = (part * TILES + c) * P
                    for k in range(KC):
                        mm = pe.matmul(half_bank(pair[1 + part], c), pos_sb[:, k, at:at + P], dense_sb[:, k, :],
                                       start=(k == 0), stop=(k == KC - 1))
                mm.then_inc(posw_mm, 1)
                if part == 0:
                    transpose_tiles(a_sb, pair[3], normed[0], 0, 1, at_mm)
            pe.wait_ge(dense_split, 2)
            project(0, 0)
            pe.wait_ge(qkv_split, 1)
            pe.wait_ge(a_hi_done, 2)
            pe.wait_ge(a_lo_done, 2)
            pe.wait_ge(posw_done, 1)
            for m in range(3):
                x = [lambda k, half=half: half[:, k, 0:P] for half in (a_hi, a_lo)]
                w = [lambda k, half=half: half[:, m, k, :] for half in (qkv_hi, qkv_lo)]
                mm = split_product(half_bank(pair[2], m), x, w, True)
            mm.then_inc(cls_mm, 1)
            pe.wait_ge(cls_qkv, 3)
            for k in range(KC):
                mm = pe.matmul(pair[1][:, 0, k * D:(k + 1) * D], k0[0:1, k * P:(k + 1) * P], v0[0:1, :],
                               start=True, stop=True)
            mm.then_inc(cls_mm, 1)
            transpose_a(0, 0)
            pe.wait_ge(h0_done, 2)
            transpose_tiles(rec[:, 1, :, :], pair[0], normed[1], 0, 1, nt_mm)
            pe.wait_ge(loaded, LATE)
            pe.wait_ge(nt_done, 2)
            logits(nt_sb[:, 1, :, :], 1)
            pe.wait_ge(cls_state, 1)

            def turn(i, j):
                if lives(i, j, 0):
                    qkv(i, j)
                if lives(i, j, -1):
                    retention(image(i, j, -1), parity(j, -1))
                if lives(i, j, 1):
                    project(image(i, j, 1), parity(j, 1))
                if first_turn(i, j):
                    pe.wait_ge(route, ROUTE)
                    pe.wait_ge(rope_mult, 1)
                    ranks(B)
                if lives(i, j, -2):
                    pe.wait_ge(route, ROUTE * both(i, j, -2))
                    pe.wait_ge(placed, both(i, j, -3))
                    if lives(i, j, 0):
                        pe.wait_ge(rope_mult, 2 * own(i, j) - 1)
                    else:
                        pe.wait_ge(z_done, (NJ * TILES - 1) * B)
                    ranks(P)
                if lives(i, j, 0):
                    scores(i, j)
                if lives(i, j, 0):
                    state_steps(i, j)
                if lives(i, j, -1):
                    transpose_n(image(i, j, -1), parity(j, -1))
                if lives(i, j, 1):
                    transpose_a(image(i, j, 1), parity(j, 1))
                if lives(i, j, -1):
                    pe.wait_ge(nt_done, 2 * both(i, j, -1))
                    logits(nt_sb[:, parity(j, -1), :, :], TILES)

            schedule(pe, turn)

        @block.scalar
        def _(act):
            def copy_banks(dst, src, need, count, done):
                for m in range(2):
                    act.wait_ge(need, count + m + 1)
                    act.activation(dst(m), src[:, m, :], ACT.Copy).then_inc(done, 1)

            def high_x(i, j):
                act.wait_ge(x_loaded, 16 * own(i, j))
                wait(act, h0_mm, 2 * own(i, j, -1))
                wait(act, x_lo_done, own(i, j, -1))
                act.activation(x_hi[:, :, :], x_sb[:, :, :], ACT.Copy).then_inc(x_hi_done, 1)

            def split_a(i, j):
                wait(act, v_mm, 2 * own(i, j, -1))
                copy_banks(lambda m: a_hi[:, m, :], pair[3], at_mm, 2 * both(i, j, -1), a_hi_done)

            def copy_v(i, j):
                wait(act, o_mm, 2 * own(i, j, -2))
                copy_banks(lambda m: v_sb[:, j, 2 * m:2 * m + 2, :].rearrange("p c n -> p (c n)"), pair[2], v_mm,
                           2 * own(i, j, -1), v_done)

            def copy_kt(i, j):
                wait(act, dz_mm, states_through(i, j, -1))
                copy_banks(lambda m: kt_sb[:, 2 * m:2 * m + 2, :].rearrange("p c n -> p (c n)"), pair[2], kt_mm,
                           2 * own(i, j, -1), kt_done)

            def copy_n(i, j):
                wait(act, lg_mm, both(i, j, -2))
                copy_banks(lambda m: nt_sb[:, j, m, :], pair[0], nt_mm, 2 * both(i, j, -1), nt_done)

            def second_norm(i, j):
                wait(act, scattered[j], SCATTERS * i)
                if isinstance(i, int) and i == j == 0:
                    act.wait_ge(cls_scattered, 32)
                wait(act, nt_mm, 2 * both(i, j, -2))
                act.wait_ge(shift_done, own(i, j))
                for c in range(TILES):
                    act.activation(rec[:, j, c, 0:D], h1[:, c, :], ACT.Identity, bias=shift[:, c:c + 1],
                                   scale=rstd[1][:, c:c + 1]).then_inc(normed[1], 1)

            def exps(tiles, turn_no):
                act.wait_ge(below_done, turn_no + 1)
                act.activation(expo[:, 0:tiles, :], below[:, 0:tiles, :], ACT.Exp).then_inc(expo_done, 1)

            act.wait_ge(early_loaded, EARLY)
            act.activation(dense_hi[:, :, :], dense_sb, ACT.Copy).then_inc(dense_split, 1)
            high_x(0, 0)
            for m in range(2):
                act.wait_ge(at_mm, m + 1)
                act.activation(a_hi[:, m, 0:P], pair[3][:, m, 0:P], ACT.Copy).then_inc(a_hi_done, 1)
            act.wait_ge(cls_mm, 1)
            act.activation(q0, pair[2][:, 0, 0:D], ACT.Copy).then_inc(cls_qkv, 1)
            act.activation(k0, pair[2][:, 0, D:2 * D], ACT.Copy).then_inc(cls_qkv, 1)
            act.activation(v0, pair[2][:, 1, 0:D], ACT.Copy).then_inc(cls_qkv, 1)
            act.wait_ge(cls_mm, 2)
            act.activation(z_sb[:, 0, :, :].rearrange("p k n -> p (k n)"), pair[1][:, 0, :], ACT.Copy)\
                .then_inc(cls_state, 1)
            split_a(0, 0)
            for m in range(2):
                act.wait_ge(nt_mm, m + 1)
                act.activation(nt_sb[:, 1, m, 0:P], pair[0][:, m, 0:P], ACT.Copy).then_inc(nt_done, 1)
            high_x(0, 1)

            def turn(i, j):
                if lives(i, j, 0):
                    copy_v(i, j)
                if first_turn(i, j):
                    exps(1, 0)
                if lives(i, j, -2):
                    exps(TILES, both(i, j, -3))
                if lives(i, j, 0):
                    copy_kt(i, j)
                if lives(i, j, -1):
                    second_norm(image(i, j, -1), parity(j, -1))
                    copy_n(image(i, j, -1), parity(j, -1))
                if lives(i, j, 1):
                    split_a(image(i, j, 1), parity(j, 1))
                if lives(i, j, 2):
                    high_x(image(i, j, 2), j)

            schedule(act, turn)

        @block.vector
        def _(dve):
            def take_moments(which, src, tiles, turn_no):
                for c in range(tiles):
                    ins = dve.bn_stats(stats[which][:, c, :], src[:, c, :])
                ins.then_inc(stats_done[which], 1)
                wait_apart(dve, stats_done[which], turn_no + 1)
                for c in range(tiles):
                    ins = dve.bn_aggr(moments[which][:, c, :], stats[which][:, c, :])
                ins.then_inc(moments_done[which], 1)

            def norm(which, src, dst, tiles, turn_no, free):
                free()
                dve.wait_ge(moments_done[which], turn_no + 1)
                dve.wait_ge(rstd_done[which], turn_no + 1)
                for c in range(tiles):
                    dve.tensor_scalar(dst[:, c, :], src[:, c, :], moments[which][:, c, 0:1], rstd[which][:, c:c + 1],
                                      ALU.subtract, ALU.mult).then_inc(normed[which], 1)

            def two_tiles(buf, m):
                return buf[:, 2 * m:2 * m + 2, :].rearrange("p c n -> p (c n)")

            def add_position(i, j):
                wait(dve, h1_done, 2 * both(i, j, -2))
                for m in range(2):
                    dve.wait_ge(h0_mm, 2 * own(i, j, -1) + m + 1)
                    dve.tensor_tensor(two_tiles(h0[:, j, :, :], m), pair[0][:, m, :],
                                      two_tiles(posw, 2 * j + m), ALU.add).then_inc(h0_done, 1)

            def first_moments(i, j):
                dve.wait_ge(h0_done, 2 * own(i, j))
                take_moments(0, h0[:, j, :, :], TILES, both(i, j, -1))

            def first_norm(i, j):
                norm(0, h0[:, j, :, :], a_sb, TILES, both(i, j, -1), lambda: dve.wait_ge(at_mm, 2 * both(i, j, -1)))

            def low_a(i, j):
                wait(dve, v_mm, 2 * own(i, j, -1))
                for m in range(2):
                    dve.wait_ge(a_hi_done, 2 * both(i, j, -1) + m + 1)
                    dve.tensor_tensor(a_lo[:, m, :], pair[3][:, m, :], a_hi[:, m, :].bitcast(F32), ALU.subtract)\
                        .then_inc(a_lo_done, 1)

            def rotate(i, j, m):
                src, mm, tables = ((pair[1], k_mm, 2), (pair[0], q_mm, 0))[m]
                wait(dve, rope_done, 2 * own(i, j, -1) - 1 + m)
                dve.wait_ge(mm, 2 * own(i, j))
                for dst, table in ((by_cos, tables), (by_sin, tables + 1)):
                    ins = dve.tensor_tensor(dst[:, m, :, :], src[:, :, :],
                                            rope_sb[:, table, j:j + 1, :].to_broadcast([P, 2, W]), ALU.mult)
                ins.then_inc(rope_mult, 1)

            def masked(i, j):
                dve.wait_ge(s_mm, own(i, j))
                wait(dve, o_mm, 2 * own(i, j, -1))
                dve.tensor_tensor(p_sb[:, :, :], pair[1][:, 0, :].rearrange("p (c n) -> p c n", c=TILES),
                                  mask_sb[:, :].unsqueeze(1).to_broadcast([P, TILES, P]), ALU.mult)\
                    .then_inc(p_done, 1)

            def states(i, j, tiles):
                for c in tiles:
                    dve.wait_ge(dz_mm, states_through(i, j, -1) + c + 1)
                    n = j * TILES + c
                    if n > 0:
                        dve.wait_ge(z_done, states_through(i, j, -1) + c)
                    dve.scalar_tensor_tensor(z_sb[:, n + 1, :, :].rearrange("p k n -> p (k n)"),
                                             z_sb[:, n, :, :].rearrange("p k n -> p (k n)"), DECAY,
                                             pair[1 + c // 2][:, c % 2, :], ALU.mult, ALU.add).then_inc(z_done, 1)

            def after_retention(i, j):
                dve.wait_ge(r_done, both(i, j, -1))
                for m in range(2):
                    dve.wait_ge(o_mm, 2 * own(i, j, -1) + m + 1)
                    dve.tensor_tensor(two_tiles(h1, m), pair[3][:, m, :], two_tiles(h0[:, j, :, :], m), ALU.add)\
                        .then_inc(h1_done, 1)
                dve.wait_ge(h1_done, 2 * both(i, j))
                take_moments(1, h1, TILES, both(i, j, -1))

            def take_shift(i, j):
                dve.wait_ge(rstd_done[1], both(i, j))
                dve.scalar_tensor_tensor(shift[:, :], moments[1][:, :, 0], -1.0, rstd[1][:, :], ALU.mult, ALU.mult)\
                    .then_inc(shift_done, 1)

            def take_logits(tiles, turn_no):
                dve.wait_ge(lg_mm, turn_no + 1)
                dve.tensor_copy(lg[:, 0:tiles, :], pair[0][:, 0, 0:tiles * E].rearrange("p (c e) -> p c e", e=E))\
                    .then_inc(lg_done, 1)

            def router(tiles, turn_no, j):
                T = slice(0, tiles)
                shape = [P, tiles, E]
                landed = [ROUTE * turn_no]

                def step(ins):
                    ins.then_inc(route, 1)
                    landed[0] = landed[0] + 1

                def steps_landed():
                    dve.wait_ge(route, landed[0])

                wait_apart(dve, lg_done, turn_no + 1)
                for c in range(tiles):
                    ins = dve.max(top8[:, c, :], lg[:, c, :])
                ins.then_inc(top_done, 1)
                dve.wait_ge(top_done, turn_no + 1)
                dve.tensor_tensor(below[:, T, :], lg[:, T, :], top8[:, T, 0:1].to_broadcast(shape), ALU.subtract)\
                    .then_inc(below_done, 1)
                for c in range(tiles):
                    ins = dve.max_index(idx8[:, c, :], top8[:, c, :], lg[:, c, :])
                ins.then_inc(idx_done, 1)
                dve.wait_ge(idx_done, turn_no + 1)
                step(dve.tensor_copy(idxf[:, T, :], idx8[:, T, 0:2]))
                steps_landed()
                experts = iota_sb[:, :].unsqueeze(1).to_broadcast(shape)
                step(dve.tensor_tensor(hit0[:, T, :], experts, idxf[:, T, 0:1].to_broadcast(shape), ALU.is_equal))
                step(dve.tensor_tensor(hit1[:, T, :], experts, idxf[:, T, 1:2].to_broadcast(shape), ALU.is_equal))
                dve.wait_ge(expo_done, turn_no + 1)
                step(dve.tensor_reduce(zsum[:, T], expo[:, T, :], AX.X, ALU.add))
                steps_landed()
                step(dve.reciprocal(zrec[:, T], zsum[:, T]))
                step(dve.tensor_tensor(hits[:, T, :], hit0[:, T, :], hit1[:, T, :], ALU.add))
                steps_landed()
                wait(dve, rank_mm, turn_no)
                step(dve.tensor_copy(taken[:, T, :], hits[:, T, :]))
                step(dve.tensor_tensor(prob[:, T, :], expo[:, T, :], zrec[:, T].unsqueeze(2).to_broadcast(shape),
                                       ALU.mult))
                steps_landed()
                step(dve.tensor_tensor(picked[:, T, :], prob[:, T, :], hits[:, T, :], ALU.mult))
                steps_landed()
                step(dve.tensor_reduce(psum2[:, T], picked[:, T, :], AX.X, ALU.add))
                steps_landed()
                step(dve.tensor_scalar(psum2[:, T], psum2[:, T], 1e-12, None, ALU.max))
                steps_landed()
                step(dve.reciprocal(prec2[:, T], psum2[:, T]))
                steps_landed()
                step(dve.tensor_tensor(rec[:, j, T, AT_SHARE:AT_SHARE + E], picked[:, T, :],
                                       prec2[:, T].unsqueeze(2).to_broadcast(shape), ALU.mult))

            def take_ranks(turn_no):
                ranked = pair[1][:, 1, 0:(TILES + 1) * E].rearrange("p (c e) -> p c e", e=E)
                base = PLACE * turn_no
                dve.wait_ge(rank_mm, turn_no + 1)
                dve.tensor_tensor(place[:, :, :], ranked[:, 0:TILES, :],
                                  free[:, :].unsqueeze(1).to_broadcast([P, TILES, E]), ALU.add)\
                    .then_inc(place_steps, 1)
                dve.wait_ge(place_steps, base + 1)
                dve.tensor_tensor(free[:, :], ranked[:, TILES, :], free[:, :], ALU.add).then_inc(placed, 1)

            def places(turn_no, j):
                base = PLACE * turn_no
                for n, hit in enumerate((hit0, hit1)):
                    dve.tensor_tensor(mine[:, n, :, :], place[:, :, :], hit[:, :, :], ALU.mult)\
                        .then_inc(place_steps, 1)
                dve.wait_ge(place_steps, base + 3)
                dve.tensor_reduce(minef[:, :, :], mine[:, :, :, :], AX.X, ALU.add).then_inc(place_steps, 1)
                dve.wait_ge(place_steps, base + 4)
                dve.tensor_copy(place_of[:, j, :, :], minef[:, :, :]).then_inc(place_steps, 1)

            def output_rows(i, j):
                dve.wait_ge(place_steps, PLACE * both(i, j, -1))
                dve.tensor_copy(rec[:, j, :, AT_ROW:AT_ROW + 1].bitcast(U32), rows_sb[:, j, :].unsqueeze(2))\
                    .then_inc(row_done, 1)
                dve.wait_ge(row_done, 2 * own(i, j, -1) + 1)
                dve.tensor_scalar(rows_sb[:, j, :], rows_sb[:, j, :], float(S + 1), None, ALU.add).then_inc(row_done, 1)

            dve.memset(half[:, :], -0.5).then_inc(half_set, 1)
            dve.memset(taken[:, :, :], 0.0).then_inc(begun, 1)
            dve.memset(ones[:, :], 1.0).then_inc(begun, 1)
            dve.memset(hit0[:, :, :], 0.0).then_inc(begun, 1)
            dve.memset(hit1[:, :, :], 0.0).then_inc(begun, 1)
            dve.memset(rec[:, :, :, :], 0.0).then_inc(begun, 1)
            dve.memset(pad[:, :, :], 0.0).then_inc(pad_done, 1)
            dve.wait_ge(early_loaded, EARLY)
            take_moments(0, h0[:, 1, :, :], 1, 0)
            norm(0, h0[:, 1, :, :], a_sb, 1, 0, lambda: None)
            dve.wait_ge(dense_split, 1)
            dve.tensor_tensor(dense_lo[:, :, :], dense_sb, dense_hi[:, :, :].bitcast(F32), ALU.subtract)\
                .then_inc(dense_split, 1)

            def add_bias(part):
                dve.wait_ge(posw_mm, part + 1)
                for c in range(TILES):
                    ins = dve.tensor_tensor(posw[:, part * TILES + c, :],
                                            pair[1 + part][:, c // 2, (c % 2) * D:(c % 2) * D + D], bias_sb[:, :],
                                            ALU.add)
                return ins

            add_bias(0)
            for m in range(2):
                dve.wait_ge(a_hi_done, m + 1)
                dve.tensor_tensor(a_lo[:, m, 0:P], pair[3][:, m, 0:P], a_hi[:, m, 0:P].bitcast(F32), ALU.subtract)\
                    .then_inc(a_lo_done, 1)
            add_bias(1).then_inc(posw_done, 1)
            dve.wait_ge(posw_done, 1)
            add_position(0, 0)
            first_moments(0, 0)
            dve.wait_ge(loaded, LATE)
            dve.tensor_copy(before_bf[:, :, :], before_sb[:, :, :]).then_inc(begun, 1)
            dve.tensor_copy(free[:, :], starts_sb[:, :]).then_inc(begun, 1)
            dve.wait_ge(pad_done, 1)
            dve.tensor_copy(pad[:, :, AT_ROW:AT_ROW + 1].bitcast(U32),
                            pad_row_sb[:, :].unsqueeze(2)).then_inc(pad_done, 1)
            dve.wait_ge(begun, 7)
            dve.tensor_copy(rec[:, 1, 0, AT_ROW:AT_ROW + 1].bitcast(U32), cls_row_sb[:, :]).then_inc(begun, 1)
            first_norm(0, 0)
            dve.wait_ge(cls_qkv, 3)
            dve.tensor_tensor(qk0, q0, k0, ALU.mult).then_inc(cls_score, 1)
            dve.wait_ge(cls_score, 1)
            dve.tensor_reduce(s0[:, :], qk0, AX.X, ALU.add).then_inc(cls_score, 1)
            dve.wait_ge(cls_score, 2)
            dve.scalar_tensor_tensor(h1[:, 0, :], v0, s0[:, 0:1], h0[:, 1, 0, :], ALU.mult, ALU.add)\
                .then_inc(h1_done, 2)
            dve.wait_ge(h1_done, 2)
            take_moments(1, h1, 1, 0)
            norm(1, h1, rec[:, 1, :, 0:D], 1, 0, lambda: None)
            low_a(0, 0)
            take_logits(1, 0)

            def turn(i, j):
                if lives(i, j, -2):
                    take_logits(TILES, both(i, j, -3))
                if lives(i, j, 0):
                    rotate(i, j, 0)
                    rotate(i, j, 1)
                if first_turn(i, j):
                    router(1, 0, 1)
                    take_ranks(0)
                    places(0, 1)
                if lives(i, j, -2):
                    wait(dve, scattered[j], SCATTERS * image(i, j, -2))
                    if isinstance(i, int) and i == 1 and j == 0:
                        dve.wait_ge(cls_scattered, 32)
                    router(TILES, both(i, j, -3), j)
                if lives(i, j, -1):
                    after_retention(image(i, j, -1), parity(j, -1))
                if lives(i, j, 1):
                    add_position(image(i, j, 1), parity(j, 1))
                if lives(i, j, -1):
                    take_shift(image(i, j, -1), parity(j, -1))
                if lives(i, j, -2):
                    take_ranks(both(i, j, -3))
                if lives(i, j, 0):
                    masked(i, j)
                if lives(i, j, 1):
                    first_moments(image(i, j, 1), parity(j, 1))
                if lives(i, j, -2):
                    places(both(i, j, -3), j)
                    output_rows(image(i, j, -2), j)
                if lives(i, j, 1):
                    first_norm(image(i, j, 1), parity(j, 1))
                if lives(i, j, 0):
                    states(i, j, state_tiles(j)[:2])
                if lives(i, j, 1):
                    low_a(image(i, j, 1), parity(j, 1))
                if lives(i, j, 0):
                    states(i, j, state_tiles(j)[2:])

            schedule(dve, turn)

            made = [0]

            def step(ins):
                ins.then_inc(table, 1)
                made[0] += 1

            def steps_landed():
                dve.wait_ge(table, made[0])

            def by_expert(buf, n):
                return buf[:, :].unsqueeze(1).to_broadcast([P, n, E])

            dve.wait_ge(placed, NB + 1)
            dve.wait_ge(rope_done, 2 * NB)
            step(dve.tensor_tensor(count[:, :], free[:, :], starts_sb[:, :], ALU.subtract))
            step(dve.tensor_copy(end_of[:, :], free[:, :]))
            steps_landed()
            step(dve.tensor_tensor(fuller[:, :, :], count[:, :].unsqueeze(2).to_broadcast([P, E, MOST]),
                                   steps_sb[:, :].unsqueeze(1).to_broadcast([P, E, MOST]), ALU.is_gt))
            steps_landed()
            step(dve.tensor_reduce(blocks_of[:, :], fuller[:, :, :], AX.X, ALU.add))
            steps_landed()
            step(dve.tensor_tensor_scan(blocks_to[:, :], ones[:, :], blocks_of[:, :], 0.0, ALU.mult, ALU.add))
            steps_landed()
            step(dve.tensor_tensor(past[:, :, :], numbers_sb[:, :].unsqueeze(2).to_broadcast([P, NX, E]),
                                   by_expert(blocks_to, NX), ALU.is_ge))
            steps_landed()
            step(dve.tensor_reduce(expert_f[:, :], past[:, :, :], AX.X, ALU.add))
            step(dve.tensor_tensor(past_blocks[:, :, :], past[:, :, :], by_expert(blocks_of, NX), ALU.mult))
            steps_landed()
            step(dve.tensor_reduce(skipped[:, :], past_blocks[:, :, :], AX.X, ALU.add))
            steps_landed()
            step(dve.tensor_tensor(skipped[:, :], numbers_sb[:, :], skipped[:, :], ALU.subtract))
            steps_landed()
            step(dve.tensor_scalar(skipped[:, :], skipped[:, :], float(W), None, ALU.mult))
            steps_landed()
            step(dve.scalar_tensor_tensor(record_f[:, :], expert_f[:, :], float(REGION), skipped[:, :], ALU.mult,
                                          ALU.add))
            step(dve.tensor_scalar(real_expert[:, :], expert_f[:, :], float(E - 1), None, ALU.min))
            step(dve.tensor_tensor(stays[:, 1:], expert_f[:, 1:], expert_f[:, :NX - 1], ALU.is_equal))
            step(dve.tensor_scalar(has_round[:, :], adds_before_sb[:, :], float(ADDS), None, ALU.is_gt))
            steps_landed()
            step(dve.tensor_tensor(past[:, :, 0], real_expert[:, :], expert_f[:, :], ALU.is_equal))
            step(dve.tensor_tensor(stays[:, 1:], stays[:, 1:], has_round[:, 1:], ALU.mult))
            steps_landed()
            step(dve.tensor_tensor(stays[:, 1:], stays[:, 1:], past[:, 1:, 0], ALU.mult))
            steps_landed()
            step(dve.scalar_tensor_tensor(stays[:, 1:], stays[:, 1:], -float(ADDS), adds_before_sb[:, 1:], ALU.mult,
                                          ALU.add))
            steps_landed()
            step(dve.tensor_copy(adds_due[:, 1:], stays[:, 1:]))
            step(dve.tensor_copy(record_of[:, :], record_f[:, :]))
            step(dve.tensor_copy(expert_of[:, :], real_expert[:, :]))
            steps_landed()

        @block.gpsimd
        def _(pool):
            def inverse_deviation(which, tiles, turn_no):
                wait_apart(pool, moments_done[which], turn_no + 1)
                pool.tensor_scalar(var_eps[which][:, 0:tiles], moments[which][:, 0:tiles, 1], EPS, None, ALU.add)\
                    .then_inc(var_done[which], 1)
                pool.wait_ge(var_done[which], turn_no + 1)
                pool.tensor_tensor(rstd[which][:, 0:tiles], var_eps[which][:, 0:tiles], half[:, 0:tiles], ALU.pow)\
                    .then_inc(rstd_done[which], 1)

            def low_x(i, j):
                pool.wait_ge(x_hi_done, own(i, j))
                wait(pool, h0_mm, 2 * own(i, j, -1))
                pool.tensor_tensor(x_lo[:, :, :], x_sb[:, :, :], x_hi[:, :, :].bitcast(F32), ALU.subtract)\
                    .then_inc(x_lo_done, 1)

            def rotate(i, j, m):
                if m == 1:
                    wait(pool, o_mm, 2 * own(i, j, -2))
                    dst = q_sb[:, j, :, :]
                else:
                    wait(pool, kt_mm, 2 * own(i, j, -1))
                    dst = k_sb[:, :, :]
                pool.wait_ge(rope_mult, 2 * own(i, j, -1) + m + 1)
                pool.tensor_tensor(dst[:, 0, :], by_cos[:, m, 0, :], by_sin[:, m, 1, :], ALU.subtract)
                pool.tensor_tensor(dst[:, 1, :], by_cos[:, m, 1, :], by_sin[:, m, 0, :], ALU.add)\
                    .then_inc(rope_done, 1)

            def residual(i, j):
                wait(pool, r_stored[j], 16 * i)
                if isinstance(i, int) and i == j == 0:
                    pool.wait_ge(cls_stored, 16)
                pool.wait_ge(normed[1], TILES * own(i, j) + 1)
                pool.tensor_tensor(r_sb[:, j, :, :], h1[:, :, :], rec[:, j, :, 0:D], ALU.add).then_inc(r_done, 1)

            def scatter(i, j, tiles):
                wait_apart(pool, row_done, 2 * own(i, j, -1) + 1)
                for c in tiles:
                    for n in range(2):
                        pool.indirect_dma_start(
                            records, bass.IndirectOffsetOnAxis(ap=place_of[:, j, n, c:c + 1], axis=0),
                            rec[:, j, c, :], None).then_inc(scattered[j], 16)

            pool.wait_ge(half_set, 1)
            inverse_deviation(0, 1, 0)
            low_x(0, 0)
            pool.wait_ge(early_loaded, EARLY)
            whole = "p m k n -> p (m k n)"
            pool.tensor_scalar(qkv_hi[:, :, :, :].rearrange(whole), qkv_sb[:, :, :, :].rearrange(whole), 1.0, 0.0,
                               ALU.mult, ALU.add).then_inc(split_hi, 1)
            pool.wait_ge(split_hi, 1)
            pool.tensor_tensor(qkv_lo[:, :, :, :].rearrange(whole), qkv_sb[:, :, :, :].rearrange(whole),
                               qkv_hi[:, :, :, :].rearrange(whole).bitcast(F32), ALU.subtract).then_inc(qkv_split, 1)
            inverse_deviation(0, TILES, 1)
            inverse_deviation(1, 1, 0)
            pool.wait_ge(normed[1], 1)
            pool.tensor_tensor(r_sb[:, 1, 0, :], h1[:, 0, :], rec[:, 1, 0, 0:D], ALU.add).then_inc(r_done, 1)
            low_x(0, 1)

            def turn(i, j):
                if lives(i, j, 0):
                    rotate(i, j, 0)
                    rotate(i, j, 1)
                if first_turn(i, j):
                    pool.wait_ge(place_steps, PLACE)
                    for n in range(2):
                        pool.indirect_dma_start(records, bass.IndirectOffsetOnAxis(ap=place_of[0:B, 1, n, 0:1], axis=0),
                                                rec[0:B, 1, 0, :], None).then_inc(cls_scattered, 16)
                if lives(i, j, -3):
                    scatter(image(i, j, -3), parity(j, -3), range(TILES // 2, TILES))
                if lives(i, j, -1):
                    inverse_deviation(1, TILES, both(i, j, -2))
                if lives(i, j, 1):
                    inverse_deviation(0, TILES, both(i, j, 0))
                if lives(i, j, -1):
                    residual(image(i, j, -1), parity(j, -1))
                if lives(i, j, -2):
                    scatter(image(i, j, -2), j, range(TILES // 2))
                if lives(i, j, 2):
                    low_x(image(i, j, 2), j)

            schedule(pool, turn)
            scatter(B - 1, NJ - 1, range(TILES // 2, TILES))


def phase2(nc, sem, wait, pair, raw, expert_of, record_of, adds_due, ident_sb, arrivals, records, b1_fm,
           b2, out):
    ctx = ExitStack()
    with ctx:
        def sb(name, shape, dt=F32):
            return ctx.enter_context(nc.sbuf_tensor(name, shape, dt))

        SIDE = 2 * KC * D
        every = sb("every", [P, E, 2 * SIDE], F32R)
        b1_sb = sb("b1_sb", [P, E, KC])
        b2_sb = sb("b2_sb", [P, E, D])
        w1_sb = sb("w1_sb", [P, 2, SIDE], F32R)
        bias = sb("bias", [P, 2, KC])
        out_bias = sb("out_bias", [P, STEPS, D])
        share = sb("share", [P, STEPS, TILES])
        row_of = sb("row_of", [P, STEPS, TILES], U32)
        x_in = sb("x_in", [P, STEPS, TILES, REC])
        x_hi = sb("x_hi", [P, KC, W], F32R)
        x_lo = sb("x_lo", [P, KC, W], F32R)
        g = raw[:, 0:2, :, :, :].rearrange("p o k a n -> p o k (a n)")
        y_sb = raw[:, 2:4, :, :, :].rearrange("p o m k n -> p o (m k) n")
        y_full = sb("y_full", [P, TILES, D])
        g_hi = sb("g_hi", [P, 2, KC, W], F32R)
        g_lo = sb("g_lo", [P, 2, KC, W], F32R)

        apart = sem("apart_p2")
        small_in, w_hi_done = sem("small_in"), sem("w_hi_done")
        w_lo_done, w_lo_pool = sem("w_lo_done"), sem("w_lo_pool")
        x_loaded = [sem(f"records_in{n}") for n in range(STEPS)]
        t_mm, x_hi_done, x_lo_done = sem("t_mm"), sem("x_hi_done"), sem("x_lo_done")
        w1_here, share_here = sem("w1_here"), sem("share_here")
        h_mm, gelu_done, g_hi_done, g_lo_done = sem("h_mm"), sem("gelu_done"), sem("g_hi_done"), sem("g_lo_done")
        y_mm, y_full_done, y_done = sem("y_mm"), sem("y_full_done"), sem("y_done")
        added = [sem(f"added{n}") for n in range(STEPS)]

        POOLS = 5

        def w_lo(eng, n):
            e, m = n // 2, n % 2
            half = m * SIDE + KC * D
            eng.wait_ge(w_hi_done, n + 1)
            return eng.tensor_tensor(every[:, e, half:half + KC * D], raw[:, e, m, :, :].rearrange("p k n -> p (k n)"),
                                     every[:, e, m * SIDE:half].bitcast(F32), ALU.subtract)

        def own(i, j, d=0):
            return STEPS * i + j + d + 1

        def lives(i, j, d):
            return not isinstance(i, int) or 0 <= STEPS * i + j + d < NX

        def at(i, j, d):
            return i + (j + d) // STEPS, (j + d) % STEPS

        def schedule(eng, turn):
            for j in range(STEPS):
                turn(0, j)
            with eng.Fori(1, NX // STEPS - 1) as i:
                for j in range(STEPS):
                    turn(i, j)
            for j in range(STEPS):
                turn(NX // STEPS - 1, j)

        block = ctx.enter_context(nc.Block())

        @block.sync
        def _(sp):
            def load(i, j):
                wait(sp, t_mm, 2 * own(i, j, -STEPS))
                wait(sp, share_here, own(i, j, -STEPS))
                first = nc.values_load(record_of[0:1, bass.ds(STEPS * i + j, 1)], engines=[sp.engine], min_val=0,
                                       max_val=E * REGION + (NX - 1) * W)
                sp.dma_start(x_in[:, j, :, :], records[bass.ds(first, W)].rearrange("(p c) n -> p c n", p=P))\
                    .then_inc(x_loaded[j], 16)

            for dst, src in ((b2_sb[:, :, :], b2), (b1_sb[:, :, :], b1_fm)):
                sp.dma_start(dst, src).then_inc(small_in, 16)
            for s, count in arrivals:
                sp.wait_ge(s, count)
            for j in range(STEPS):
                load(0, j)

            def turn(i, j):
                if lives(i, j, STEPS):
                    load(*at(i, j, STEPS))

            schedule(sp, turn)
            for j in range(STEPS):
                sp.wait_ge(added[j], ADDS * (NX // STEPS))

        @block.tensor
        def _(pe):
            def transposes(i, j):
                pe.wait_ge(x_loaded[j], 16 * (i + 1))
                wait(pe, x_hi_done, 2 * own(i, j, -1))
                wait(pe, x_lo_done, 2 * own(i, j, -1))
                for k in range(KC):
                    for c in range(TILES):
                        mm = pe.transpose(pair[0][:, k, c * P:(c + 1) * P], x_in[:, j, c, k * P:(k + 1) * P],
                                          ident_sb[:, :])
                    mm.then_inc(t_mm, 1)

            def first(i, j):
                o = j % 2
                pe.wait_ge(x_hi_done, 2 * own(i, j))
                pe.wait_ge(x_lo_done, 2 * own(i, j))
                pe.wait_ge(w1_here, own(i, j))
                wait(pe, gelu_done, 2 * own(i, j, -2))
                w = w1_sb[:, o, :].rearrange("p (h k n) -> p h k n", h=2, k=KC)
                for f in range(KC):
                    n = 0
                    for k in range(KC):
                        for h, x in ((1, x_hi), (0, x_lo), (0, x_hi)):
                            mm = pe.matmul(pair[1 + 2 * o][:, f, :], w[:, h, k, f * P:(f + 1) * P], x[:, k, :],
                                           start=(n == 0), stop=(n == 3 * KC - 1))
                            n += 1
                    mm.then_inc(h_mm, 1)

            def second(i, j):
                o = j % 2
                e = nc.values_load(expert_of[0:1, bass.ds(STEPS * i + j, 1)], engines=[pe.engine], min_val=0,
                                   max_val=E - 1)
                pe.wait_ge(g_lo_done, own(i, j))
                wait(pe, y_full_done, own(i, j, -1))
                for c in range(TILES):
                    dst = pair[2][:, c // 2, (c % 2) * D:(c % 2) * D + D]
                    n = 0
                    for k in range(KC):
                        for x, h in ((g_hi, 1), (g_lo, 0), (g_hi, 0)):
                            part = SIDE + (h * KC + k) * D
                            w = every[:, bass.ds(e, 1), part:part + D].rearrange("p a n -> p (a n)")
                            mm = pe.matmul(dst, x[:, o, k, c * P:(c + 1) * P], w, start=(n == 0),
                                           stop=(n == 3 * KC - 1))
                            n += 1
                mm.then_inc(y_mm, 1)

            transposes(0, 0)
            pe.wait_ge(w_lo_done, 2 * E - POOLS)
            pe.wait_ge(w_lo_pool, POOLS)
            first(0, 0)
            transposes(0, 1)

            def turn(i, j):
                if lives(i, j, 1):
                    first(*at(i, j, 1))
                if lives(i, j, 2):
                    transposes(*at(i, j, 2))
                second(i, j)

            schedule(pe, turn)

        @block.scalar
        def _(act):
            def high_x(i, j):
                for k in range(KC):
                    wait(act, h_mm, 2 * own(i, j, -1))
                    act.wait_ge(t_mm, 2 * own(i, j, -1) + k + 1)
                    act.activation(x_hi[:, k, :], pair[0][:, k, :], ACT.Copy).then_inc(x_hi_done, 1)

            def gelu(i, j):
                o = j % 2
                wait(act, g_lo_done, own(i, j, -2))
                act.wait_ge(w1_here, own(i, j))
                for f in range(KC):
                    act.wait_ge(h_mm, 2 * own(i, j, -1) + f + 1)
                    act.activation(g[:, o, f, :], pair[1 + 2 * o][:, f, :], ACT.Gelu, bias=bias[:, o, f:f + 1])\
                        .then_inc(gelu_done, 1)

            def high_g(i, j):
                o = j % 2
                wait(act, y_mm, own(i, j, -2))
                act.wait_ge(gelu_done, 2 * own(i, j))
                act.activation(g_hi[:, o, :, :], g[:, o, :, :], ACT.Copy).then_inc(g_hi_done, 1)

            def weigh(i, j):
                act.wait_ge(share_here, own(i, j))
                act.wait_ge(y_full_done, own(i, j))
                ii, jj = at(i, j, -2)
                wait(act, added[jj], ADDS * (ii + 1))
                for c in range(TILES):
                    ins = act.activation(y_sb[:, j % 2, c, :], y_full[:, c, :], ACT.Copy, scale=share[:, j, c:c + 1])
                ins.then_inc(y_done, 1)

            for e in range(E):
                for m in range(2):
                    act.activation(every[:, e, m * SIDE:m * SIDE + KC * D],
                                   raw[:, e, m, :, :].rearrange("p k n -> p (k n)"), ACT.Copy).then_inc(w_hi_done, 1)
            high_x(0, 0)
            gelu(0, 0)
            high_x(0, 1)
            high_g(0, 0)

            def turn(i, j):
                if lives(i, j, 1):
                    gelu(*at(i, j, 1))
                if lives(i, j, 2):
                    high_x(*at(i, j, 2))
                if lives(i, j, -1):
                    weigh(*at(i, j, -1))
                if lives(i, j, 1):
                    high_g(*at(i, j, 1))

            schedule(act, turn)
            weigh(NX // STEPS - 1, STEPS - 1)

        @block.vector
        def _(dve):
            def expert(i, j):
                return nc.values_load(expert_of[0:1, bass.ds(STEPS * i + j, 1)], engines=[dve.engine], min_val=0,
                                      max_val=E - 1)

            def low_x(i, j):
                for k in range(KC):
                    dve.wait_ge(x_hi_done, 2 * own(i, j, -1) + k + 1)
                    dve.tensor_tensor(x_lo[:, k, :], pair[0][:, k, :], x_hi[:, k, :].bitcast(F32), ALU.subtract)\
                        .then_inc(x_lo_done, 1)

            def take_w1(i, j):
                e = expert(i, j)
                wait(dve, gelu_done, 2 * own(i, j, -2))
                dve.sem_inc(apart, 1)
                dve.tensor_copy(w1_sb[:, j % 2, :], every[:, bass.ds(e, 1), 0:SIDE].rearrange("p a n -> p (a n)"))
                dve.tensor_copy(bias[:, j % 2, :], b1_sb[:, bass.ds(e, 1), :].rearrange("p a n -> p (a n)"))\
                    .then_inc(w1_here, 1)

            def take_share(i, j):
                e = expert(i, j)
                wait(dve, y_done, own(i, j, -STEPS))
                wait(dve, added[j], ADDS * i)
                dve.sem_inc(apart, 1)
                dve.tensor_copy(out_bias[:, j, :], b2_sb[:, bass.ds(e, 1), :].rearrange("p a n -> p (a n)"))
                dve.tensor_copy(share[:, j, :].unsqueeze(2), x_in[:, j, :, bass.ds(AT_SHARE + e, 1)])
                dve.tensor_copy(row_of[:, j, :].unsqueeze(2), x_in[:, j, :, AT_ROW:AT_ROW + 1].bitcast(U32))\
                    .then_inc(share_here, 1)

            def low_g(i, j):
                o = j % 2
                dve.wait_ge(g_hi_done, own(i, j))
                dve.tensor_tensor(g_lo[:, o, :, :], g[:, o, :, :], g_hi[:, o, :, :].bitcast(F32), ALU.subtract)\
                    .then_inc(g_lo_done, 1)

            def add_b2(i, j):
                dve.wait_ge(share_here, own(i, j))
                dve.wait_ge(y_mm, own(i, j))
                wait(dve, y_done, own(i, j, -1))
                dve.tensor_tensor(y_full[:, :, :], pair[2][:, :, :].rearrange("p b (c n) -> p (b c) n", n=D),
                                  out_bias[:, j:j + 1, :].to_broadcast([P, TILES, D]), ALU.add)\
                    .then_inc(y_full_done, 1)

            for n in range(POOLS, 2 * E):
                w_lo(dve, n).then_inc(w_lo_done, 1)
            low_x(0, 0)
            dve.wait_ge(small_in, 16 * 2)
            dve.wait_ge(w_lo_done, 2 * E - POOLS)
            dve.wait_ge(w_lo_pool, POOLS)
            take_w1(0, 0)
            take_share(0, 0)
            take_w1(0, 1)
            low_x(0, 1)

            def turn(i, j):
                if lives(i, j, -1):
                    add_b2(*at(i, j, -1))
                low_g(i, j)
                if lives(i, j, 2):
                    take_w1(*at(i, j, 2))
                    low_x(*at(i, j, 2))
                if lives(i, j, 1):
                    take_share(*at(i, j, 1))

            schedule(dve, turn)
            add_b2(NX // STEPS - 1, STEPS - 1)

        @block.gpsimd
        def _(pool):
            for n in range(POOLS):
                w_lo(pool, n).then_inc(w_lo_pool, 1)

            def turn(i, j):
                pool.wait_ge(y_done, own(i, j))
                if lives(i, j, -1):
                    due = nc.values_load(adds_due[0:1, bass.ds(STEPS * i + j, 1)], engines=[pool.engine], min_val=1,
                                         max_val=ADDS * (NX // STEPS))
                    pool.wait_ge(added[(j - 1) % STEPS], due)
                pool.sem_inc(apart, 1)
                for c in range(TILES):
                    pool.indirect_dma_start(
                        out, bass.IndirectOffsetOnAxis(ap=row_of[:, j, c:c + 1], axis=0),
                        y_sb[:, j % 2, c, :], None, compute_op=ALU.add).then_inc(added[j], 16)

            schedule(pool, turn)


_INS = ("x_fm", "pos_fm", "dense_w", "dense_b", "cls_rows", "wq", "wk", "wv", "router_fm", "w1", "b1_fm", "w2",
        "b2", "rope", "mask", "ident", "iota", "before", "rows", "cls_row", "pad_row", "starts", "steps", "numbers",
        "adds_before")


def _patches(img):
    n, g = img.shape[0], IMG // PATCH
    return img.reshape(n, g, PATCH, g, PATCH).transpose(0, 2, 4, 1, 3).reshape(n, D, S)


def _tables():
    inv_freq = (np.float32(1.0) / np.float32(10000.0) ** (np.arange(0, D, 2, dtype=np.float32) / np.float32(D)))
    angle = (inv_freq[:, None] * np.arange(1, S + 1, dtype=np.float32)[None, :]).astype(np.float64)
    at = np.arange(S) % P
    grow, fall = GAMMA ** (at + 1.0), GAMMA ** (P - 1.0 - at)
    rope = np.stack([np.cos(angle) * grow, np.sin(angle) * grow, np.cos(angle) * fall, np.sin(angle) * fall], axis=1)
    j, i = np.arange(P)[:, None], np.arange(P)[None, :]
    mask = np.where(j <= i, GAMMA ** -float(P), 0.0)
    t = np.arange(P)
    f32 = np.float32
    return {
        "rope": rope.reshape(P, 4, NJ, W).astype(np.float32),
        "mask": mask.astype(np.float32),
        "ident": np.eye(P, dtype=np.float32),
        "iota": np.broadcast_to(np.arange(E, dtype=np.float32), (P, E)),
        "before": np.stack([t[:, None] < t[None, :], np.ones((P, P))], axis=1).astype(f32),
        "rows": (1 + np.arange(NJ)[:, None] * W + np.arange(TILES)[None, :] * P + t[:, None, None]).astype(f32),
        "cls_row": ((t % B) * (S + 1)).astype(f32)[:, None],
        "pad_row": (TOKENS + np.arange(W).reshape(P, TILES)).astype(f32),
        "starts": np.broadcast_to(np.arange(E, dtype=f32) * REGION, (P, E)),
        "steps": np.broadcast_to(np.arange(MOST, dtype=f32) * W, (P, MOST)),
        "numbers": np.broadcast_to(np.arange(NX, dtype=f32), (P, NX)),
        "adds_before": np.broadcast_to(((np.arange(NX) - 1) // STEPS + 1).astype(f32) * ADDS, (P, NX)),
    }


def kernel(**inputs):
    import numpy as _np
    import concourse.bacc as _bacc
    from concourse import mybir as _mybir
    from concourse.bass_utils import run_bass_kernel_spmd as _run

    a = {k: _np.asarray(v) for k, v in inputs.items()}
    halves = _np.concatenate([_np.arange(0, D, 2), _np.arange(1, D, 2)])
    x = _patches(a["x"].reshape(B, IMG, IMG)).reshape(B, KC, P, NJ, W).transpose(0, 3, 2, 1, 4).reshape(NB, P, KC, W)
    g = IMG // 8
    pos = a["L0_tok_pos_emb"].reshape(g, g, 8, 8).transpose(0, 2, 1, 3).reshape(1, IMG, IMG)
    given = {
        "x_fm": x,
        "pos_fm": _patches(pos)[0].reshape(KC, P, S).transpose(1, 0, 2),
        "dense_w": a["L0_tok_dense_w"],
        "dense_b": _np.broadcast_to(a["L0_tok_dense_b"], (P, D)),
        "cls_rows": _np.broadcast_to(a["cls_tok"].reshape(1, D), (P, D)),
        "wq": a["L0_attn_W_Q"][:, halves],
        "wk": a["L0_attn_W_K"][:, halves],
        "wv": a["L0_attn_W_V"],
        "router_fm": a["L0_ffn_router_w"].T.reshape(KC, P, E).transpose(1, 0, 2),
        "w1": a["L0_ffn_w1"],
        "b1_fm": a["L0_ffn_b1"].reshape(E, KC, P).transpose(2, 0, 1),
        "w2": a["L0_ffn_w2"],
        "b2": _np.broadcast_to(a["L0_ffn_b2"], (P, E, D)),
        **_tables(),
    }
    nc = _bacc.Bacc("TRN2", target_bir_lowering=False, num_devices=1)
    arrays, args = {}, {}
    for name in _INS:
        v = _np.ascontiguousarray(given[name])
        arrays[name] = v
        args[name] = nc.dram_tensor(name, v.shape, _mybir.dt.from_np(v.dtype), kind="ExternalInput").ap()
    out = nc.dram_tensor("out", (TOKENS + W, D), _mybir.dt.float32, kind="ExternalOutput").ap()
    vit_kernel(nc, out=out, **args)
    r = _run(nc, [arrays], core_ids=[0])
    return r.results[0]["out"][:TOKENS].reshape(B, S + 1, D)
```
